# Optimizing a Trainium2 kernel written in Bass

```python
import numpy as np
import jax
import jax.numpy as jnp

def _softmax(x, axis=-1):
    return jax.nn.softmax(x, axis=axis)

def _gelu(x):
    return jax.nn.gelu(x, approximate=True)

def _silu(x):
    return jax.nn.silu(x)

def _sigmoid(x):
    return jax.nn.sigmoid(x)

def _layernorm(x, axis=-1, eps=1e-05):
    m = jnp.mean(x, axis=axis, keepdims=True)
    v = jnp.var(x, axis=axis, keepdims=True)
    return (x - m) / jnp.sqrt(v + eps)

def _scatter_add(tgt, idx, src, axis=0):
    return tgt.at[idx].add(src)

def _segment_sum(src, seg, n):
    return jax.ops.segment_sum(src, seg, n)
kernel_name = 'mk_adaln_d1_jaxref_r4_fd6cbe'

def setup_inputs(seed: int=0):
    np.random.seed(seed)
    _w = jnp.asarray

    def _L0_attn_setup():
        import jax, jax.numpy as jnp
        import numpy as np
        D_MODEL = 256
        NUM_HEADS = 16
        HEAD_DIM = D_MODEL // NUM_HEADS

        def _rope(x):
            B, H, T, d = x.shape
            pos = jnp.arange(T, dtype=x.dtype)[:, None]
            freq_seq = jnp.arange(d // 2, dtype=x.dtype)
            inv_freq = 1.0 / 10000.0 ** (freq_seq / (d // 2))
            ang = pos * inv_freq[None, :]
            sin = jnp.sin(ang)[None, None]
            cos = jnp.cos(ang)[None, None]
            x1, x2 = (x[..., :d // 2], x[..., d // 2:])
            return jnp.concatenate((x1 * cos - x2 * sin, x1 * sin + x2 * cos), axis=-1)
        key = jax.random.key(seed)
        ks = jax.random.split(key, 9)
        B, T = (2, 512)
        s = 1.0 / np.sqrt(D_MODEL)
        inp = {'x': jax.random.normal(ks[0], (B, T, D_MODEL), dtype=jnp.float32), 'Wq': jax.random.normal(ks[1], (D_MODEL, D_MODEL), dtype=jnp.float32) * s, 'bq': jnp.zeros((D_MODEL,), dtype=jnp.float32), 'Wk': jax.random.normal(ks[2], (D_MODEL, D_MODEL), dtype=jnp.float32) * s, 'bk': jnp.zeros((D_MODEL,), dtype=jnp.float32), 'Wv': jax.random.normal(ks[3], (D_MODEL, D_MODEL), dtype=jnp.float32) * s, 'bv': jnp.zeros((D_MODEL,), dtype=jnp.float32), 'Wo': jax.random.normal(ks[4], (D_MODEL, D_MODEL), dtype=jnp.float32) * s, 'bo': jnp.zeros((D_MODEL,), dtype=jnp.float32)}
        return inp
    _L0_attn_in = _L0_attn_setup()

    def _L0_ffn_setup():
        import jax, jax.numpy as jnp
        import numpy as np
        N_EXP = 8
        TOP_K = 2
        CAP_FACTOR = 1.25
        NEG_INF = -1000000000.0

        def _moe_forward(x, w_g, c_fc, c_proj):
            B, T, D = x.shape
            N = B * T
            xf = x.reshape(N, D)
            logits = xf @ w_g
            topv, topi = jax.lax.top_k(logits, TOP_K)
            full = jnp.full_like(logits, NEG_INF)
            full = full.at[jnp.arange(N)[:, None], topi].set(topv)
            probs = jax.nn.softmax(full, axis=-1)
            capacity = int(TOP_K * CAP_FACTOR * N / N_EXP)
            capacity += capacity % 2
            mask = jax.nn.one_hot(jnp.swapaxes(topi, 0, 1), N_EXP, dtype=jnp.int32)
            rank = jnp.cumsum(mask.reshape(TOP_K * N, N_EXP), axis=0).reshape(TOP_K, N, N_EXP) - 1
            mask = mask * (rank < capacity)
            rank_sel = jnp.sum(mask * rank, axis=-1)
            wts = jnp.sum(mask * probs[None], axis=-1)
            cb = jnp.zeros((N, N_EXP, capacity), x.dtype)
            tok = jnp.arange(N)
            for k in range(TOP_K):
                cb = cb.at[tok, topi[:, k], rank_sel[k]].add(wts[k])
            sec_mask = (cb != 0).astype(x.dtype)
            exp_batches = jnp.einsum('nec,nd->ecd', sec_mask, xf)
            h = jax.nn.gelu(jnp.einsum('ecd,edh->ech', exp_batches, c_fc), approximate=False)
            exp_out = jnp.einsum('ech,ehd->ecd', h, c_proj)
            out = jnp.einsum('nec,ecd->nd', cb, exp_out)
            return out.reshape(B, T, D)
        key = jax.random.key(seed)
        k1, k2, k3, k4 = jax.random.split(key, 4)
        B, T, D = (4, 128, 256)
        H = 4 * D
        x = jax.random.normal(k1, (B, T, D), jnp.float32)
        w_g = jax.random.normal(k2, (D, N_EXP), jnp.float32) * 0.02
        c_fc = jax.random.normal(k3, (N_EXP, D, H), jnp.float32) * 0.02
        c_proj = jax.random.normal(k4, (N_EXP, H, D), jnp.float32) * 0.02
        return {'x': x, 'w_g': w_g, 'c_fc': c_fc, 'c_proj': c_proj}
    _L0_ffn_in = _L0_ffn_setup()
    _L0_c = _w((lambda *s: np.random.randn(*s).astype(np.float32) * 0.05)(2, 256))
    _L0_wmod = _w((lambda *s: np.random.randn(*s).astype(np.float32) * 0.05)(256, 6 * 256) * 256 ** (-0.5))
    _d = {'L0_attn_x': _L0_attn_in['x'], 'L0_attn_Wq': _L0_attn_in['Wq'], 'L0_attn_bq': _L0_attn_in['bq'], 'L0_attn_Wk': _L0_attn_in['Wk'], 'L0_attn_bk': _L0_attn_in['bk'], 'L0_attn_Wv': _L0_attn_in['Wv'], 'L0_attn_bv': _L0_attn_in['bv'], 'L0_attn_Wo': _L0_attn_in['Wo'], 'L0_attn_bo': _L0_attn_in['bo'], 'L0_ffn_w_g': _L0_ffn_in['w_g'], 'L0_ffn_c_fc': _L0_ffn_in['c_fc'], 'L0_ffn_c_proj': _L0_ffn_in['c_proj'], 'L0_c': _L0_c, 'L0_wmod': _L0_wmod}
    _x0 = _d['L0_attn_x']
    _d['L0_attn_x'] = jax.random.normal(jax.random.fold_in(jax.random.key(seed), 1), (2, 2048, 256), dtype=_x0.dtype)
    del _x0
    return _d

def reference(L0_attn_x, L0_attn_Wq, L0_attn_bq, L0_attn_Wk, L0_attn_bk, L0_attn_Wv, L0_attn_bv, L0_attn_Wo, L0_attn_bo, L0_ffn_w_g, L0_ffn_c_fc, L0_ffn_c_proj, L0_c, L0_wmod):

    def _L0_attn_ref(x, Wq, bq, Wk, bk, Wv, bv, Wo, bo):
        import jax, jax.numpy as jnp
        import numpy as np
        D_MODEL = 256
        NUM_HEADS = 16
        HEAD_DIM = D_MODEL // NUM_HEADS

        def _rope(x):
            B, H, T, d = x.shape
            pos = jnp.arange(T, dtype=x.dtype)[:, None]
            freq_seq = jnp.arange(d // 2, dtype=x.dtype)
            inv_freq = 1.0 / 10000.0 ** (freq_seq / (d // 2))
            ang = pos * inv_freq[None, :]
            sin = jnp.sin(ang)[None, None]
            cos = jnp.cos(ang)[None, None]
            x1, x2 = (x[..., :d // 2], x[..., d // 2:])
            return jnp.concatenate((x1 * cos - x2 * sin, x1 * sin + x2 * cos), axis=-1)
        B, T, _ = x.shape

        def proj(W, b):
            return (x @ W + b).reshape(B, T, NUM_HEADS, HEAD_DIM).transpose(0, 2, 1, 3)
        q = _rope(proj(Wq, bq))
        k = _rope(proj(Wk, bk))
        v = proj(Wv, bv)
        scores = jnp.einsum('bhqd,bhkd->bhqk', q, k) / jnp.sqrt(jnp.asarray(HEAD_DIM, dtype=x.dtype))
        attn = jax.nn.softmax(scores, axis=-1)
        ctx = jnp.einsum('bhqk,bhkd->bhqd', attn, v)
        ctx = ctx.transpose(0, 2, 1, 3).reshape(B, T, D_MODEL)
        return ctx @ Wo + bo

    def _L0_ffn_ref(x, w_g, c_fc, c_proj):
        import jax, jax.numpy as jnp
        import numpy as np
        N_EXP = 8
        TOP_K = 2
        CAP_FACTOR = 1.25
        NEG_INF = -1000000000.0

        def _moe_forward(x, w_g, c_fc, c_proj):
            B, T, D = x.shape
            N = B * T
            xf = x.reshape(N, D)
            logits = xf @ w_g
            topv, topi = jax.lax.top_k(logits, TOP_K)
            full = jnp.full_like(logits, NEG_INF)
            full = full.at[jnp.arange(N)[:, None], topi].set(topv)
            probs = jax.nn.softmax(full, axis=-1)
            capacity = int(TOP_K * CAP_FACTOR * N / N_EXP)
            capacity += capacity % 2
            mask = jax.nn.one_hot(jnp.swapaxes(topi, 0, 1), N_EXP, dtype=jnp.int32)
            rank = jnp.cumsum(mask.reshape(TOP_K * N, N_EXP), axis=0).reshape(TOP_K, N, N_EXP) - 1
            mask = mask * (rank < capacity)
            rank_sel = jnp.sum(mask * rank, axis=-1)
            wts = jnp.sum(mask * probs[None], axis=-1)
            cb = jnp.zeros((N, N_EXP, capacity), x.dtype)
            tok = jnp.arange(N)
            for k in range(TOP_K):
                cb = cb.at[tok, topi[:, k], rank_sel[k]].add(wts[k])
            sec_mask = (cb != 0).astype(x.dtype)
            exp_batches = jnp.einsum('nec,nd->ecd', sec_mask, xf)
            h = jax.nn.gelu(jnp.einsum('ecd,edh->ech', exp_batches, c_fc), approximate=False)
            exp_out = jnp.einsum('ech,ehd->ecd', h, c_proj)
            out = jnp.einsum('nec,ecd->nd', cb, exp_out)
            return out.reshape(B, T, D)
        return _moe_forward(x, w_g, c_fc, c_proj)
    x = L0_attn_x
    mod = (_silu(L0_c) @ L0_wmod).reshape(L0_c.shape[0], 6, 1, -1)
    sa, ca, ga, sb, cb, gb = (mod[:, 0], mod[:, 1], mod[:, 2], mod[:, 3], mod[:, 4], mod[:, 5])
    ga = (2 * (ga >= 0) - 1) * jnp.maximum(jnp.abs(ga), 0.25)
    gb = (2 * (gb >= 0) - 1) * jnp.maximum(jnp.abs(gb), 0.25)
    h = _layernorm(x, axis=-1) * (1 + ca) + sa
    x = x + ga * _L0_attn_ref(h, L0_attn_Wq, L0_attn_bq, L0_attn_Wk, L0_attn_bk, L0_attn_Wv, L0_attn_bv, L0_attn_Wo, L0_attn_bo)
    h = _layernorm(x, axis=-1) * (1 + cb) + sb
    x = x + gb * _L0_ffn_ref(h, L0_ffn_w_g, L0_ffn_c_fc, L0_ffn_c_proj)
    return x

_drawn_inputs = setup_inputs


def setup_inputs(seed=0):
    import zlib

    import numpy as np

    out = dict(_drawn_inputs(seed))
    spreads = {'L0_attn_bq': (0.0, 0.8),
     'L0_attn_bk': (0.0, 0.8),
     'L0_attn_bv': (0.0, 0.311),
     'L0_attn_bo': (0.0, 0.328)}
    factors = {'L0_attn_Wq': 5.555,
     'L0_attn_Wk': 5.292,
     'L0_attn_Wv': 4.759,
     'L0_ffn_w_g': 3.338,
     'L0_ffn_c_fc': 2.947,
     'L0_ffn_c_proj': 2.876}
    for name, (base, spread) in spreads.items():
        noise = np.random.default_rng([zlib.crc32(name.encode()), seed]).standard_normal(out[name].shape)
        drawn = base * np.exp(spread * noise) if base else spread * noise
        out[name] = jnp.asarray(drawn.astype(out[name].dtype))
    for name, factor in factors.items():
        out[name] = (out[name] * factor).astype(out[name].dtype)
    return out
```

```python
from contextlib import ExitStack

import numpy as np

import concourse.bass as bass
from concourse import mybir

B, T, D = 2, 2048, 256
N = B * T
H, DH = 16, 16
BH = B * H
NE, HID = 8, 1024
P = 128
TT = N // P
KC = D // P
CAP = int(2 * 1.25 * N / NE)
CAP += CAP % 2
SLOTS = NE * CAP
BLK = 256
NB = CAP // BLK
assert NB * BLK == CAP
TRASH = SLOTS + BLK
XROWS = TRASH + 2 * N
EPS = 1e-5

QT = 8
UQ = QT * P
NKT = T // P
VW = 32
KS = 6 * DH
PRO = 65
PU = 33


def adaln_block(nc, x, wqk, bqk, wv, bv, wo, bo, wg, cfc, cproj, c, wmod, trig, consts, out):
    f32, bf16, i32 = mybir.dt.float32, mybir.dt.bfloat16, mybir.dt.int32
    ALU, ACT, AX = mybir.AluOpType, mybir.ActivationFunctionType, mybir.AxisListType

    qs = nc.dram_tensor("q_parts", [BH, 3 * DH, T], bf16, kind="Internal").ap()
    ks = nc.dram_tensor("k_parts", [BH, 3 * DH, T], bf16, kind="Internal").ap()
    os_ = nc.dram_tensor("o_heads", [BH, DH + 1, T], f32, kind="Internal").ap()
    linv = nc.dram_tensor("inv_sums", [BH, T], f32, kind="Internal").ap()
    xe = nc.dram_tensor("x_slots", [XROWS, D], f32, kind="Internal").ap()
    ye = nc.dram_tensor("y_slots", [SLOTS, D], f32, kind="Internal").ap()

    ctx = ExitStack()
    with ctx:
        def sb(name, shape, dt=f32, stack=ctx):
            return stack.enter_context(nc.sbuf_tensor(name, shape, dt))

        def sem(name):
            return ctx.enter_context(nc.semaphore(name))

        xs = sb("xs", [P, TT, D])
        cst = sb("cst", [P, 336])
        ident, tri = cst[:, 0:128], cst[:, 128:256]
        iota_m8, iota8 = cst[:, 256:264], cst[:, 264:272]
        trash_id = cst[:, 272:336]
        identb = sb("identb", [P, P], bf16)
        bc = sb("bc", [P, 4, B, D])
        GA, GB, CB, SB = range(4)
        bob = sb("bob", [P, D])
        wo_s = sb("wo_s", [P, KC, D])
        wg_s = sb("wg_s", [P, KC, NE])
        bv_s = sb("bv_s", [P, KC])
        stats = sb("stats", [P, TT, 6])
        mv = sb("mv", [P, TT, 2])
        std = sb("std", [P, TT])
        rstd = sb("rstd", [P, TT])

        att = ExitStack()
        vall = sb("vall", [P, BH, NKT, DH + 1], stack=att)
        stk = sb("stk", [P, 4, T], bf16, att)
        qmx, kmx = stk[0:KS, 0:2, :], stk[0:KS, 2:4, :]
        qex = sb("qex", [KS + 3, 2, T], bf16, att)
        kex = sb("kex", [KS + 3, 2, T], bf16, att)
        vst = sb("vst", [P, 2, NKT, VW], stack=att)
        pr = sb("pr", [P, 4, UQ], stack=att)
        osb = sb("osb", [P, 2, 256], stack=att)
        mxp = sb("mxp", [P, 2, QT, 4], stack=att)
        nm = sb("nm", [P, 2, QT], stack=att)
        nmr = sb("nmr", [P, 2, 2, QT], stack=att)
        nil = sb("nil", [P, QT], stack=att)
        nmp = sb("nmp", [P, 2, 3, QT], bf16, att)
        nms = sb("nms", [3 * QT, 2, P], bf16, att)

        pre = ExitStack()
        wqk_s = sb("wqk_s", [P, KC, 4, P], stack=pre)
        bqk_s = sb("bqk_s", [P, 4], stack=pre)
        wv_s = sb("wv_s", [P, KC, D], stack=pre)
        trg = sb("trg", [P, 2, T], stack=pre)
        zero = sb("zero", [P, 328], stack=pre)
        cT = sb("cT", [P, KC, B], stack=pre)
        sl = sb("sl", [P, 3, KC, B], stack=pre)
        modc = sb("modc", [P, 2, KC, B], stack=pre)
        hT = sb("hT", [P, 2, KC, 512], stack=pre)
        rq = sb("rq", [P, 2, 4, 512], stack=pre)
        attpre = ExitStack()
        gts = pr[:, 0, 0:2 * D].rearrange("p (a d) -> p a d", a=2)
        tq = pr[:, 0:2, :].rearrange("p a n -> p (a n)").rearrange("p (a n) -> p a n", a=4)
        xn = pr[:, 2:4, :].rearrange("p r (t d) -> p r t d", t=4)
        parts = sb("parts", [P, 2, 3, 4, 512], bf16, pre)
        rep = parts[:, 0, 0, :, :].rearrange("p s n -> p (s n)").bitcast(f32) \
            .rearrange("p (k b n) -> p k b n", k=KC, b=B)[:, :, :, 0:P]
        wm = stk[:].rearrange("p a n -> p (a n)").bitcast(f32)[:, 0:KC * 6 * D].rearrange("p (k n) -> p k n", k=KC)
        pre.close()

        att.close()

        post = ExitStack()
        cxT = sb("cxT", [P, KC, N], stack=post)
        lT = sb("lT", [P, N], stack=post)
        ls = sb("ls", [P, 2, 512], stack=post)
        h2 = sb("h2", [P, TT, D], stack=post)
        h2T = sb("h2T", [P, 2, KC, P], stack=post)
        t2 = sb("t2", [P, 2, D], stack=post)
        post.close()
        moe = ExitStack()
        w1 = sb("w1", [P, 2, KC, HID], stack=moe)
        w2 = sb("w2", [P, 2, HID // P, D], stack=moe)
        xr = sb("xr", [P, 2, 2, D], stack=moe)
        xT = sb("xT", [P, 2, KC, BLK], stack=moe)
        hd = sb("hd", [P, 2, HID // P, BLK], stack=moe)
        yb = sb("yb", [P, 2, 2, D], stack=moe)
        ga_ = sb("gath", [P, 4, 2, D], stack=moe)
        assert True
        moe.close()
        rt = ExitStack()
        hold = sb("hold", [P, 26000], stack=rt)
        lg = sb("lg", [P, TT, NE], stack=rt)
        oh = sb("oh", [P, 2, TT, NE], stack=rt)
        lw = sb("lw", [P, TT, NE], stack=rt)
        lw2 = sb("lw2", [P, TT, NE], stack=rt)
        sel = sb("sel", [P, TT, NE], stack=rt)
        m12 = sb("m12", [P, 4, TT], stack=rt)
        pw = sb("pw", [P, 2, TT], stack=rt)
        pf = sb("pf", [P, 2, 64, NE], stack=rt)
        rk = sb("rk", [P, 4, 2, TT], stack=rt)
        idx = sb("idx", [P, 2, 2, TT], i32, rt)
        onesm = sb("onesm", [P, P], stack=rt)
        rt.close()

        ps = ctx.enter_context(nc.psum_tensor("ps", [P, 8, 512], f32))
        bank = [ps[:, b, :] for b in range(8)]

        names = """c_in w_in x_in0 x_in1 x_in2 x_in3 zero_set zero_out v_one
            sil_exp sil_rep modc_mm bc_mm mod_done dch pch ach std_in std_out xn_done xT_mm hT_done
            qk_mm qk_used v_mm v_used r_done hi_done mid_in mid_done lo_in lo_done parts_out0 parts_out1 idb
            mxld0 mxld1 exld0 exld1 item mxfree nm_done nmp_done shift0 shift1
            vst_done st_mm p_done pv_mm o_done oout0 oout1
            l_in l_rec l_out lb_in ctx_in ctx_done wo_mm x1_done h2_done h2T_mm h2T_done lg_mm lg_done
            ex_in ex_done oh_done cum_mm idx_done slots_in w1_in0 w1_in1 w2_in0 w2_in1 xr_in0 xr_in1 tx_mm xT_sb
            fc_mm hd_done pj_mm y_done y_out0 y_out1 g_in0 g_in1 g_in2 g_in3 comb out_done""".split()
        S = {n: sem(n) for n in names}

        block = ctx.enter_context(nc.Block())

        def turned(i, u):
            if isinstance(i, int) and 4 * i + u == 0:
                return 33
            quiet = isinstance(i, int) and 4 * i + u == 2 * BH - 1
            return v1(i, 4 * PU, PRO + PU * (u - 1) + (1 if quiet else 11))

        def v1(i, a, c_):
            return i * a + c_

        NBODY = BH // 2

        @block.sync
        def _(sp):
            sp.dma_start(cT[:], c).then_inc(S["c_in"], 16)
            sp.dma_start(wm, wmod.rearrange("(k p) n -> p k n", p=P)).then_inc(S["c_in"], 16)
            sp.dma_start(cst[:], consts).then_inc(S["c_in"], 16)
            xv = x.rearrange("b (t p) d -> p (b t) d", p=P)
            for q in range(4):
                sp.dma_start(xs[:, 8 * q:8 * q + 8, :], xv[:, 8 * q:8 * q + 8, :]).then_inc(S[f"x_in{q}"], 16)
            sp.dma_start(wqk_s[:], wqk.rearrange("(k p) s n -> p k s n", p=P)).then_inc(S["w_in"], 16)
            sp.dma_start(bqk_s[:], bqk).then_inc(S["w_in"], 16)
            sp.dma_start(wv_s[:], wv.rearrange("(k p) n -> p k n", p=P)).then_inc(S["w_in"], 16)
            sp.dma_start(trg[:], trig).then_inc(S["w_in"], 16)
            sp.dma_start(wo_s[:], wo.rearrange("(k p) n -> p k n", p=P)).then_inc(S["w_in"], 16)
            sp.dma_start(wg_s[:], wg.rearrange("(k p) n -> p k n", p=P)).then_inc(S["w_in"], 16)
            sp.dma_start(bv_s[:], bv).then_inc(S["w_in"], 16)
            sp.dma_start(bob[:], bo.rearrange("(a n) -> a n", a=1).broadcast_to([P, D])).then_inc(S["w_in"], 16)

            sp.wait_ge(S["zero_set"], 1)
            zv = xe[0:TRASH, :].rearrange("(p r) d -> p (r d)", p=P)
            ZN = TRASH // P * D // 328
            for z in range(ZN):
                sp.dma_start(zv[:, 328 * z:328 * z + 328], zero[:]).then_inc(S["zero_out"], 16)

            for g in range(8):
                b, t0 = g // 4, g % 4 * 512
                sp.wait_ge(S["lo_done"], g + 1)
                for s, scr in ((0, qs), (1, ks)):
                    for part in range(3):
                        row = (part if s == 0 else 2 - part) * DH
                        for ab in range(2):
                            dst = scr[b * H:(b + 1) * H, row + 8 * ab:row + 8 * ab + 8, t0:t0 + 512]
                            sp.dma_start(dst, parts[:, g % 2, part, 2 * s + ab, :]) \
                                .then_inc(S[f"parts_out{g % 2}"], 16)
            for par in range(2):
                sp.wait_ge(S[f"parts_out{par}"], 4 * 12 * 16)

            def load_stacks(qd, kd, par, head, sm):
                for dst, scr, q in ((qd, qs, True), (kd, ks, False)):
                    sp.dma_start(dst[0:48, par, :], scr[head, :, :]).then_inc(sm, 16)
                    src = scr[head, 0:32, :] if q else scr[head, 16:48, :]
                    sp.dma_start(dst[48:80, par, :], src).then_inc(sm, 16)
                    src = scr[head, 0:16, :] if q else scr[head, 32:48, :]
                    sp.dma_start(dst[80:96, par, :], src).then_inc(sm, 16)

            def shift(par, half, count):
                sp.wait_ge(S["mxfree"], count)
                dst = qex[KS:KS + 3, par, UQ * half:UQ * half + UQ].rearrange("r (t q) -> r t q", t=QT)
                sp.dma_start(dst, nms[:, half, :]).then_inc(S[f"shift{half}"], 16)

            load_stacks(qmx, kmx, 0, 0, S["mxld0"])
            load_stacks(qmx, kmx, 1, 1, S["mxld1"])
            load_stacks(qex, kex, 0, 0, S["exld0"])
            shift(0, 0, turned(0, 0))

            def body(i, last):
                for n in range(2):
                    head = i * 2 + n
                    final = last and n == 1
                    if not last:
                        sp.wait_ge(S["item"], v1(i, 4 * PU, PRO + 2 * PU * n))
                        load_stacks(qmx, kmx, n, i * 2 + (n + 2), S[f"mxld{n}"])
                    if not final:
                        if n or not isinstance(i, int):
                            sp.wait_ge(S["st_mm"], v1(i, 64, 32 * n))
                        load_stacks(qex, kex, 1 - n, i * 2 + (n + 1), S[f"exld{1 - n}"])
                    shift(n, 1, turned(i, 2 * n + 1))
                    for half in range(2):
                        if half == 1 and not final:
                            pass
                        sp.wait_ge(S["o_done"], v1(i, 4, 2 * n + half + 1))
                        for g in range(4):
                            q0 = UQ * half + 256 * g
                            sp.dma_start(os_[head, :, q0:q0 + 256],
                                         osb[32 * g:32 * g + DH + 1, half, :]).then_inc(S[f"oout{half}"], 16)
                        if half == 0 and not final:
                            shift(1 - n, 0, turned(i, 2 * n + 2))

            with sp.Fori(0, NBODY - 1) as i:
                body(i, False)
            body(NBODY - 1, True)

            for half in range(2):
                sp.wait_ge(S[f"oout{half}"], BH * 4 * 16)
            lv = os_[:, DH, :].rearrange("h (s n) -> h s n", n=512)
            for h in range(BH):
                sp.dma_start(ls[4 * h:4 * h + 4, 0, :], lv[h]).then_inc(S["l_in"], 16)
            for b in range(B):
                for k in range(KC):
                    h0 = b * H + k * 8
                    for h in range(8):
                        sp.dma_start(cxT[16 * h:16 * h + 16, k, b * T:(b + 1) * T], os_[h0 + h, 0:DH, :]) \
                            .then_inc(S["ctx_in"], 16)
            sp.wait_ge(S["l_rec"], 1)
            sp.dma_start(linv.rearrange("h (s n) -> (h s) n", n=512), ls[:, 1, :]).then_inc(S["l_out"], 16)
            sp.wait_ge(S["l_out"], 16)
            for k in range(KC):
                if k:
                    sp.wait_ge(S["ctx_done"], B * k)
                for b in range(B):
                    for h in range(8):
                        hh = b * H + k * 8 + h
                        sp.dma_start(lT[16 * h:16 * h + 16, b * T:(b + 1) * T],
                                     linv[hh:hh + 1, :].broadcast_to([16, T])).then_inc(S["lb_in"], 16)

            w1v = cfc.rearrange("e (k p) n -> e p k n", p=P)
            w2v = cproj.rearrange("e (k p) n -> e p k n", p=P)
            sp.wait_ge(S["wo_mm"], TT)
            for e in range(2):
                sp.dma_start(w1[:, e], w1v[e]).then_inc(S[f"w1_in{e}"], 16)
                sp.dma_start(w2[:, e], w2v[e]).then_inc(S[f"w2_in{e}"], 16)
            sp.wait_ge(S["slots_in"], 2 * TT * 16)

            def load_rows(par, row):
                sp.dma_start(xr[:, par], xe[row:row + BLK, :].rearrange("(t p) d -> p t d", p=P)) \
                    .then_inc(S[f"xr_in{par}"], 16)

            def load_rows_at(par, blk):
                sp.dma_start(xr[:, par], xe.rearrange("(g t p) d -> g p t d", p=P, t=2)[blk]) \
                    .then_inc(S[f"xr_in{par}"], 16)

            load_rows_at(0, 0)
            load_rows_at(1, 1)

            def moe_body(i, last):
                for e in range(2):
                    for b in range(NB):
                        n = e * NB + b
                        if not (last and n >= 2 * NB - 1):
                            sp.wait_ge(S["tx_mm"], v1(i, 2 * NB, n + 1))
                            load_rows_at(n % 2, i * (2 * NB) + (n + 2))
                        sp.wait_ge(S["y_done"], v1(i, 4 * NB, 2 * n + 2))
                        sp.dma_start(ye.rearrange("(g t p) d -> g p t d", p=P, t=2)[i * (2 * NB) + n],
                                     yb[:, n % 2]).then_inc(S[f"y_out{n % 2}"], 16)
                        if b == NB - 1 and not last:
                            sp.wait_ge(S["pj_mm"], v1(i, 4 * NB, 2 * n + 2))
                            sp.dma_start(w1[:, e], w1v[i * 2 + (e + 2)]).then_inc(S[f"w1_in{e}"], 16)
                            sp.dma_start(w2[:, e], w2v[i * 2 + (e + 2)]).then_inc(S[f"w2_in{e}"], 16)

            with sp.Fori(0, NE // 2 - 1) as i:
                moe_body(i, False)
            moe_body(NE // 2 - 1, True)

            ov = out.rearrange("b (t p) d -> p (b t) d", p=P)
            for q in range(4):
                sp.wait_ge(S["comb"], 8 * q + 8)
                sp.dma_start(ov[:, 8 * q:8 * q + 8, :], xs[:, 8 * q:8 * q + 8, :]).then_inc(S["out_done"], 16)
            sp.wait_ge(S["out_done"], 64)
            sp.wait_ge(S["zero_out"], 16 * ZN)

        @block.vector
        def _(dve):
            V = nc.vector
            chain = [0]

            def link(ins):
                chain[0] += 1
                ins.then_inc(S["dch"], 1)
                dve.wait_ge(S["dch"], chain[0])

            V.memset(zero[:], 0.0).then_inc(S["zero_set"], 1)
            V.memset(nil[:], 0.0).then_inc(S["v_one"], 1)
            V.memset(vst[:], 0.0).then_inc(S["v_one"], 1)
            V.memset(vall[:, :, :, DH:DH + 1], 1.0).then_inc(S["v_one"], 1)
            V.memset(onesb := kex[KS:KS + 3, :, :], 1.0).then_inc(S["v_one"], 1)
            dve.wait_ge(S["sil_exp"], 1)
            link(V.tensor_scalar(sl[:, 1], sl[:, 0], 1.0, None, ALU.add))
            link(V.reciprocal(sl[:, 2], sl[:, 1]))
            link(V.tensor_tensor(sl[:, 0], cT[:], sl[:, 2], ALU.mult))
            V.tensor_copy(rep, sl[:, 0].unsqueeze(3).broadcast_to([P, KC, B, P])).then_inc(S["sil_rep"], 1)
            dve.wait_ge(S["c_in"], 48)
            V.tensor_copy(identb[:], ident).then_inc(S["idb"], 1)
            dve.wait_ge(S["modc_mm"], 1)
            mc = bank[0][:, 0:8].rearrange("p (j k b) -> p j k b", j=2, k=KC)
            link(V.tensor_copy(modc[:, 0], mc[:, 0]))
            link(V.tensor_scalar(modc[:, 1], mc[:, 1], 1.0, None, ALU.add))
            for j in (GA, GB):
                dve.wait_ge(S["bc_mm"], j + 1)
                for b in range(B):
                    g = bank[1 + j][:, D * b:D * b + D]
                    link(V.tensor_scalar(gts[:, 0], g, 0.0, 2.0, ALU.is_ge, ALU.mult))
                    link(V.tensor_scalar(gts[:, 1], g, -1.0, 0.25, ALU.mult, ALU.max))
                    link(V.tensor_tensor(gts[:, 1], g, gts[:, 1], ALU.max))
                    link(V.scalar_tensor_tensor(bc[:, j, b], gts[:, 0], -1.0, gts[:, 1], ALU.add, ALU.mult))
            dve.wait_ge(S["bc_mm"], CB + 1)
            link(V.tensor_scalar(bc[:, CB], bank[1 + CB].rearrange("p (b n) -> p b n", b=B), 1.0, None, ALU.add))
            dve.wait_ge(S["bc_mm"], SB + 1)
            V.tensor_copy(bc[:, SB], bank[1 + SB].rearrange("p (b n) -> p b n", b=B)).then_inc(S["mod_done"], 1)

            def norm_stats(t):
                link(V.bn_stats(stats[:, t, :], xs[:, t, :]))
                V.bn_aggr(mv[:, t, :], stats[:, t, :])

            def norm_std(k):
                chain[0] += 1
                V.tensor_scalar(std[:], mv[:, :, 1], EPS, None, ALU.add).then_inc(S["std_in"], 1)
                chain[0] -= 1
                dve.wait_ge(S["std_out"], k)
                link(V.reciprocal(rstd[:], std[:]))

            for t in range(TT):
                if t % 8 == 0:
                    dve.wait_ge(S[f"x_in{t // 8}"], 16)
                link(V.bn_stats(stats[:, t, :], xs[:, t, :]))
                link(V.bn_aggr(mv[:, t, :], stats[:, t, :]))
            norm_std(1)

            def normed(g):
                if g >= 2:
                    dve.wait_ge(S["xT_mm"], 2 * (g - 1))
                for t in range(4):
                    n = 4 * g + t
                    V.tensor_scalar(xn[:, g % 2, t, :], xs[:, n, :], mv[:, n, 0:1], rstd[:, n:n + 1],
                                    ALU.subtract, ALU.mult).then_inc(S["xn_done"], 1)

            normed(0)
            dve.wait_ge(S["w_in"], 128)
            for g in range(8):
                if g < 7:
                    normed(g + 1)
                pos = slice(g % 4 * 512, g % 4 * 512 + 512)
                cos, sin = trg[:, 0, pos], trg[:, 1, pos]
                if g >= 2:
                    dve.wait_ge(S["lo_in"], g - 1)
                    dve.wait_ge(S["lo_done"], g - 1)
                for s in range(2):
                    dve.wait_ge(S["qk_mm"], 2 * g + s + 1)
                    a, b_ = bank[2 + 2 * s], bank[3 + 2 * s]
                    ba, bb = bqk_s[:, 2 * s:2 * s + 1], bqk_s[:, 2 * s + 1:2 * s + 2]
                    link(V.scalar_tensor_tensor(tq[:, 0], a, ba, cos, ALU.add, ALU.mult))
                    link(V.scalar_tensor_tensor(tq[:, 1], b_, bb, sin, ALU.add, ALU.mult))
                    link(V.scalar_tensor_tensor(tq[:, 2], a, ba, sin, ALU.add, ALU.mult))
                    link(V.scalar_tensor_tensor(tq[:, 3], b_, bb, cos, ALU.add, ALU.mult))
                    V.tensor_tensor(rq[:, g % 2, 2 * s], tq[:, 0], tq[:, 1], ALU.subtract).then_inc(S["qk_used"], 1)
                    link(V.tensor_tensor(rq[:, g % 2, 2 * s + 1], tq[:, 2], tq[:, 3], ALU.add))
                    V.engine_nop().then_inc(S["r_done"], 1) if False else None
                V.memset(stats[:, 0, 0:1], 0.0).then_inc(S["r_done"], 1)

            def reduce_item(i, c_, q, kq, par, first_of_unit, units_before):
                dve.wait_ge(S["item"], v1(i, 4 * PU, c_ + 1))
                if first_of_unit and (units_before is not None):
                    dve.wait_ge(S["nm_done"], units_before)
                V.reduce_max(mxp[:, par, q, kq:kq + 1], bank[4 + c_ % 2], AX.X).then_inc(S["mxfree"], 1)

            def unit_max(i, c_, par, count):
                dve.wait_ge(S["mxfree"], v1(i, 4 * PU, c_ + 1))
                V.tensor_reduce(nm[:, par, :], mxp[:, par], AX.X, ALU.max, negate=True).then_inc(S["nm_done"], 1)

            for k in range(32):
                reduce_item(0, k, k // 4, k % 4, 0, False, None)
            unit_max(0, 31, 0, 0)
            dve.wait_ge(S["item"], 33)
            V.tensor_copy(nms[:, 0, :], bank[4].bitcast(bf16)[0:3 * QT, 0:P]).then_inc(S["mxfree"], 1)
            for k in range(32):
                reduce_item(0, 33 + k, k // 4, k % 4, 1, False, None)
            unit_max(0, 64, 1, 0)

            def att_body(i, last):
                for u in range(4):
                    base = PRO + PU * u
                    quiet = last and u >= 2
                    for k in range(32):
                        if k == 10 and not (last and u == 3):
                            c_ = base + (0 if quiet else 10)
                            dve.wait_ge(S["item"], v1(i, 4 * PU, c_ + 1))
                            par = (u + 1) % 2
                            src = bank[4 + c_ % 2].bitcast(bf16)[0:3 * QT, 0:P]
                            heads = (u + 1) // 2
                            dve.wait_ge(S[f"shift{par}"], v1(i, 32, 16 * heads)) \
                                if (heads or not isinstance(i, int)) else None
                            V.tensor_copy(nms[:, par, :], src).then_inc(S["mxfree"], 1)
                        if not quiet:
                            c_ = base + k + (k >= 10)
                            if k == 0:
                                dve.wait_ge(S["nm_done"], v1(i, 4, u + 1))
                            reduce_item(i, c_, k // 4, k % 4, u % 2, False, None)
                    if not quiet:
                        if u >= 1 or True:
                            dve.wait_ge(S["nmp_done"], v1(i, 4, u + 1))
                        unit_max(i, base + 32, u % 2, 0)

            with dve.Fori(0, NBODY - 1) as i:
                att_body(i, False)
            att_body(NBODY - 1, True)

            dve.wait_ge(S["l_in"], BH * 16)
            V.reciprocal(ls[:, 1, :], ls[:, 0, :]).then_inc(S["l_rec"], 1)
            dve.wait_ge(S["ctx_in"], B * KC * 8 * 16)
            for k in range(KC):
                dve.wait_ge(S["lb_in"], (k + 1) * B * 8 * 16)
                for b in range(B):
                    tok = slice(b * T, (b + 1) * T)
                    link(V.tensor_tensor(cxT[:, k, tok], cxT[:, k, tok], lT[:, tok], ALU.mult))
                    V.tensor_scalar(cxT[:, k, tok], cxT[:, k, tok], bv_s[:, k:k + 1], None, ALU.add) \
                        .then_inc(S["ctx_done"], 1)

            for t in range(TT):
                b = t // (TT // B)
                dve.wait_ge(S["wo_mm"], t + 1)
                link(V.tensor_tensor(t2[:, 0, :], bank[t % 2][:, 0:D], bob[:], ALU.add))
                link(V.tensor_tensor(t2[:, 1, :], t2[:, 0, :], bc[:, GA, b], ALU.mult))
                V.tensor_tensor(xs[:, t, :], xs[:, t, :], t2[:, 1, :], ALU.add).then_inc(S["x1_done"], 1)
                dve.wait_ge(S["x1_done"], t + 1)
                link(V.bn_stats(stats[:, t, :], xs[:, t, :]))
                link(V.bn_aggr(mv[:, t, :], stats[:, t, :]))
            norm_std(2)
            for t in range(TT):
                b = t // (TT // B)
                link(V.tensor_scalar(t2[:, 0, :], xs[:, t, :], mv[:, t, 0:1], rstd[:, t:t + 1],
                                     ALU.subtract, ALU.mult))
                link(V.tensor_tensor(t2[:, 1, :], t2[:, 0, :], bc[:, CB, b], ALU.mult))
                V.tensor_tensor(h2[:, t, :], t2[:, 1, :], bc[:, SB, b], ALU.add).then_inc(S["h2_done"], 1)

            dve.wait_ge(S["lg_mm"], TT)
            link(V.tensor_copy(lg[:], bank[4][:, 0:TT * NE].rearrange("p (t e) -> p t e", e=NE)))
            link(V.memset(onesm[:], 1.0))

            def over_e(a):
                return a.unsqueeze(2).broadcast_to([P, TT, NE])

            def over_t(a):
                return a.unsqueeze(1).broadcast_to([P, TT, NE])

            def pick(k, src):
                link(V.tensor_reduce(m12[:, k, :], src, AX.X, ALU.max))
                link(V.tensor_tensor(lw2[:], src, over_e(m12[:, k, :]), ALU.is_equal))
                link(V.tensor_tensor(lw2[:], lw2[:], over_t(iota_m8), ALU.mult))
                link(V.tensor_reduce(rk[:, 0, k, :], lw2[:], AX.X, ALU.min))
                link(V.tensor_tensor(oh[:, k], over_t(iota_m8), over_e(rk[:, 0, k, :]), ALU.is_equal))

            pick(0, lg[:])
            link(V.scalar_tensor_tensor(lw[:].rearrange("p t e -> p (t e)"), oh[:, 0].rearrange("p t e -> p (t e)"),
                                        -3.0e38, lg[:].rearrange("p t e -> p (t e)"), ALU.mult, ALU.add))
            pick(1, lw[:])
            V.tensor_tensor(sel[:], oh[:, 0], oh[:, 1], ALU.add).then_inc(S["oh_done"], 1)
            dve.wait_ge(S["oh_done"], 1)
            link(V.tensor_tensor(lw[:], lg[:], sel[:], ALU.mult))
            link(V.tensor_scalar(lw2[:], sel[:], -1.0, 1.0e9, ALU.add, ALU.mult))
            link(V.tensor_tensor(lw[:], lw[:], lw2[:], ALU.add))
            link(V.tensor_reduce(m12[:, 2, :], lw[:], AX.X, ALU.max))
            V.tensor_tensor(lw2[:], lw[:], over_e(m12[:, 2, :]), ALU.subtract).then_inc(S["ex_in"], 1)
            dve.wait_ge(S["ex_done"], 1)
            link(V.tensor_reduce(m12[:, 2, :], lw[:], AX.X, ALU.add))
            link(V.reciprocal(m12[:, 3, :], m12[:, 2, :]))
            for k in range(2):
                link(V.tensor_tensor(lw2[:], lw[:], oh[:, k], ALU.mult))
                link(V.tensor_reduce(rk[:, 1, k, :], lw2[:], AX.X, ALU.add))
                link(V.tensor_tensor(pw[:, k, :], rk[:, 1, k, :], m12[:, 3, :], ALU.mult))
            dve.wait_ge(S["cum_mm"], 2)
            tot = bank[6].rearrange("p (t e) -> p t e", e=NE)
            link(V.memset(pf[:, 0, 0:1, :], 0.0))
            link(V.tensor_copy(pf[:, 0, 1:64, :], tot[:, 0:63, :]))
            cur = 0
            for s in (1, 2, 4, 8, 16, 32):
                link(V.tensor_copy(pf[:, 1 - cur, 0:s, :], pf[:, cur, 0:s, :]))
                link(V.tensor_tensor(pf[:, 1 - cur, s:64, :], pf[:, cur, s:64, :], pf[:, cur, 0:64 - s, :], ALU.add))
                cur = 1 - cur
            link(V.tensor_tensor(pf[:, cur], pf[:, cur], bank[5].rearrange("p (t e) -> p t e", e=NE), ALU.add))
            for k in range(2):
                link(V.tensor_tensor(lw[:], pf[:, cur, 32 * k:32 * k + 32, :], oh[:, k], ALU.mult))
                link(V.tensor_reduce(rk[:, 1, k, :], lw[:], AX.X, ALU.add))
            link(V.tensor_scalar(rk[:, 2], rk[:, 1], float(CAP), None, ALU.is_lt))
            link(V.tensor_scalar(rk[:, 0], rk[:, 0], 8.0, float(CAP), ALU.add, ALU.mult))
            link(V.tensor_tensor(rk[:, 0], rk[:, 0], rk[:, 1], ALU.add))
            link(V.tensor_tensor(pw[:], pw[:], rk[:, 2], ALU.mult))
            link(V.tensor_tensor(rk[:, 3], rk[:, 0], rk[:, 2], ALU.mult))
            link(V.tensor_copy(idx[:, 1], rk[:, 3]))
            tid = trash_id.rearrange("p (k t) -> p k t", k=2)
            link(V.tensor_tensor(rk[:, 1], rk[:, 0], tid, ALU.subtract))
            link(V.tensor_tensor(rk[:, 1], rk[:, 1], rk[:, 2], ALU.mult))
            link(V.tensor_tensor(rk[:, 1], rk[:, 1], tid, ALU.add))
            V.tensor_copy(idx[:, 0], rk[:, 1]).then_inc(S["idx_done"], 1)

            def xt_out(i, n):
                dve.wait_ge(S["tx_mm"], v1(i, 2 * NB, n + 1))
                if not (isinstance(i, int) and i * 2 * NB + n < 2):
                    dve.wait_ge(S["fc_mm"], v1(i, 4 * NB, 2 * (n - 1)))
                V.tensor_copy(xT[:, n % 2], bank[6 + n % 2].rearrange("p (k s) -> p k s", k=KC)) \
                    .then_inc(S["xT_sb"], 1)

            def y_out(i, n):
                for t in range(2):
                    dve.wait_ge(S["pj_mm"], v1(i, 4 * NB, 2 * n + t + 1))
                    if t == 0 and not (isinstance(i, int) and i * 2 * NB + n < 2):
                        dve.wait_ge(S[f"y_out{n % 2}"], v1(i, 16 * NB, 16 * (n // 2)))
                    V.tensor_copy(yb[:, n % 2, t, :], bank[4 + t][:, 0:D]).then_inc(S["y_done"], 1)

            xt_out(0, 0)
            def moe_body(i, last):
                for n in range(2 * NB):
                    if not (last and n == 2 * NB - 1):
                        xt_out(i, n + 1)
                    y_out(i, n)

            moe_body(0, False)
            with dve.Fori(1, NE // 2 - 1) as i:
                moe_body(i, False)
            moe_body(NE // 2 - 1, True)

            for t in range(TT):
                b = t // (TT // B)
                dve.wait_ge(S[f"g_in{t % 4}"], 32 * (t // 4 + 1))
                g = ga_[:, t % 4]
                link(V.tensor_scalar(t3 := g[:, 0, :], g[:, 0, :], pw[:, 0, t:t + 1], None, ALU.mult))
                link(V.scalar_tensor_tensor(g[:, 1, :], g[:, 1, :], pw[:, 1, t:t + 1], g[:, 0, :], ALU.mult, ALU.add))
                link(V.tensor_tensor(g[:, 0, :], g[:, 1, :], bc[:, GB, b], ALU.mult))
                V.tensor_tensor(xs[:, t, :], xs[:, t, :], g[:, 0, :], ALU.add).then_inc(S["comb"], 1)

        @block.scalar
        def _(act):
            A = nc.scalar
            act.wait_ge(S["c_in"], 48)
            A.activation(sl[:, 0], cT[:], ACT.Exp, scale=-1.0).then_inc(S["sil_exp"], 1)
            act.wait_ge(S["std_in"], 1)
            A.activation(std[:], std[:], ACT.Sqrt).then_inc(S["std_out"], 1)

            for g in range(8 + 1):
                if g < 8:
                    b = g // 4
                    for k in range(KC):
                        act.wait_ge(S["xT_mm"], 2 * g + k + 1)
                        if g >= 2:
                            act.wait_ge(S["v_mm"], g - 1)
                        if g == 0:
                            act.wait_ge(S["mod_done"], 1)
                        A.activation(hT[:, g % 2, k, :], bank[k], ACT.Identity, scale=modc[:, 1, k, b:b + 1],
                                     bias=modc[:, 0, k, b:b + 1]).then_inc(S["hT_done"], 1)
                if g >= 1:
                    m = g - 1
                    act.wait_ge(S["v_mm"], m + 1)
                    b, k0 = m // 4, m % 4 * 4
                    if m == 0:
                        act.wait_ge(S["v_one"], 4)
                    for j in range(2):
                        src = bank[6 + j].rearrange("p (t h d) -> p t h d", t=2, h=H)
                        for t in range(2):
                            A.activation(vall[:, b * H:(b + 1) * H, k0 + 2 * j + t, 0:DH], src[:, t],
                                         ACT.Copy).then_inc(S["v_used"], 1)
                    act.wait_ge(S["r_done"], m + 1)
                    if m >= 2:
                        act.wait_ge(S[f"parts_out{m % 2}"], 12 * 16 * (m // 2))
                    if m == 0:
                        act.wait_ge(S["bc_mm"], 4)
                    A.activation(parts[:, m % 2, 0], rq[:, m % 2], ACT.Copy).then_inc(S["hi_done"], 1)
                    act.wait_ge(S["mid_in"], m + 1)
                    A.activation(parts[:, m % 2, 1], rq[:, m % 2], ACT.Copy).then_inc(S["mid_done"], 1)
                    act.wait_ge(S["lo_in"], m + 1)
                    A.activation(parts[:, m % 2, 2], rq[:, m % 2], ACT.Copy).then_inc(S["lo_done"], 1)

            def exp_step(i, c_):
                act.wait_ge(S["st_mm"], v1(i, 64, c_ + 1))
                if not (isinstance(i, int) and i == 0 and c_ < 4):
                    act.wait_ge(S["pv_mm"], v1(i, 64, c_ - 3))
                s = c_ % 2
                A.activation(pr[:, c_ % 4, :], ps[:, 2 * s:2 * s + 2, :].rearrange("p a n -> p (a n)"), ACT.Exp,
                             scale=0.25).then_inc(S["p_done"], 1)

            def att_body(i, last):
                for u in range(4):
                    for k in range(NKT):
                        if not (last and u == 3 and k >= NKT - 2):
                            exp_step(i, NKT * u + k + 2)
                    act.wait_ge(S["pv_mm"], v1(i, 64, NKT * (u + 1)))
                    if not (isinstance(i, int) and i == 0 and u < 2):
                        act.wait_ge(S[f"oout{u % 2}"], v1(i, 128, 64 * (u // 2)))
                    A.activation(osb[:, u % 2, :], bank[6 + u % 2][:, 0:256], ACT.Copy).then_inc(S["o_done"], 1)

            exp_step(0, 0)
            exp_step(0, 1)
            att_body(0, False)
            with act.Fori(1, NBODY - 1) as i:
                att_body(i, False)
            att_body(NBODY - 1, True)

            act.wait_ge(S["std_in"], 2)
            A.activation(std[:], std[:], ACT.Sqrt).then_inc(S["std_out"], 1)
            for t in range(TT):
                act.wait_ge(S["h2T_mm"], t + 1)
                if t >= 2:
                    act.wait_ge(S["lg_mm"], t - 1)
                A.activation(h2T[:, t % 2], bank[2 + t % 2][:, 0:D].rearrange("p (k n) -> p k n", k=KC), ACT.Copy) \
                    .then_inc(S["h2T_done"], 1)
            act.wait_ge(S["ex_in"], 1)
            A.activation(lw[:], lw2[:], ACT.Exp).then_inc(S["ex_done"], 1)

            def gelu(i, n):
                for hf in range(2):
                    act.wait_ge(S["fc_mm"], v1(i, 4 * NB, 2 * n + hf + 1))
                    if hf == 0 and not (isinstance(i, int) and i * 2 * NB + n < 2):
                        act.wait_ge(S["pj_mm"], v1(i, 4 * NB, 2 * (n - 1)))
                    A.activation(hd[:, n % 2, 4 * hf:4 * hf + 4, :].rearrange("p m s -> p (m s)"),
                                 ps[:, 2 * hf:2 * hf + 2, :].rearrange("p a n -> p (a n)"), ACT.Gelu) \
                        .then_inc(S["hd_done"], 1)

            for n in range(2 * NB):
                gelu(0, n)
            with act.Fori(1, NE // 2) as i:
                for n in range(2 * NB):
                    gelu(i, n)

        @block.gpsimd
        def _(pool):
            G = nc.gpsimd
            for g in range(8):
                pool.wait_ge(S["hi_done"], g + 1)
                G.tensor_tensor(rq[:, g % 2], rq[:, g % 2], parts[:, g % 2, 0], ALU.subtract).then_inc(S["mid_in"], 1)
                pool.wait_ge(S["mid_done"], g + 1)
                G.tensor_tensor(rq[:, g % 2], rq[:, g % 2], parts[:, g % 2, 1], ALU.subtract).then_inc(S["lo_in"], 1)

            def split_max(i, count, par):
                if not (isinstance(i, int) and i == 0 and count <= 2):
                    pool.wait_ge(S["mxfree"], turned(i, count - 3))
                pool.wait_ge(S["nm_done"], v1(i, 4, count))
                chn = lambda ins, k: (ins.then_inc(S["pch"], 1), pool.wait_ge(S["pch"], v1(i, 16, 4 * (count - 1) + k)))
                chn(G.tensor_tensor(nmp[:, par, 0], nm[:, par], nil[:], ALU.add), 1)
                chn(G.tensor_tensor(nmr[:, par, 0], nm[:, par], nmp[:, par, 0], ALU.subtract), 2)
                chn(G.tensor_tensor(nmp[:, par, 1], nmr[:, par, 0], nil[:], ALU.add), 3)
                chn(G.tensor_tensor(nmr[:, par, 1], nmr[:, par, 0], nmp[:, par, 1], ALU.subtract), 4)
                G.tensor_tensor(nmp[:, par, 2], nmr[:, par, 1], nil[:], ALU.add).then_inc(S["nmp_done"], 1)

            def stage_values(i, n, head):
                G.tensor_copy(vst[:, n, :, 0:DH + 1], vall[:, head]).then_inc(S["vst_done"], 1)

            pool.wait_ge(S["v_used"], 32)
            pool.wait_ge(S["v_one"], 4)
            stage_values(0, 0, 0)
            split_max(0, 1, 0)
            split_max(0, 2, 1)

            def att_body(i, last):
                for n in range(2):
                    if not (last and n == 1):
                        if not (isinstance(i, int) and i == 0 and n == 0):
                            pool.wait_ge(S["pv_mm"], v1(i, 64, 32 * n))
                        stage_values(i, 1 - n, i * 2 + (n + 1))
                    for half in range(2):
                        if not last:
                            split_max(i, 2 * n + half + 3, half)
                        elif n == 0:
                            split_max(i, 2 * n + half + 3, half)

            att_body(0, False)
            with pool.Fori(1, NBODY - 1) as i:
                att_body(i, False)
            att_body(NBODY - 1, True)

            pool.wait_ge(S["idx_done"], 1)
            pool.wait_ge(S["zero_out"], 16 * (TRASH // P * D // 328))
            for t in range(TT):
                for k in range(2):
                    pool.indirect_dma_start(out=xe, out_offset=bass.IndirectOffsetOnAxis(ap=idx[:, 0, k, t:t + 1], axis=0),
                                            in_=h2[:, t, :], in_offset=None).then_inc(S["slots_in"], 16)
            for par in range(2):
                pool.wait_ge(S[f"y_out{par}"], NE * NB // 2 * 16)
            for t in range(TT):
                if t >= 4:
                    pool.wait_ge(S["comb"], t - 3)
                for k in range(2):
                    pool.indirect_dma_start(out=ga_[:, t % 4, k, :], out_offset=None, in_=ye,
                                            in_offset=bass.IndirectOffsetOnAxis(ap=idx[:, 1, k, t:t + 1], axis=0)) \
                        .then_inc(S[f"g_in{t % 4}"], 16)

        @block.tensor
        def _(pe):
            M = nc.tensor.matmul
            pe.wait_ge(S["c_in"], 48)
            pe.wait_ge(S["sil_rep"], 1)
            for j, src in ((0, 0), (1, 1)):
                for f in range(KC):
                    o = bank[0][:, (j * KC + f) * B:(j * KC + f) * B + B]
                    for k in range(KC):
                        m = M(o, wm[:, k, src * D + f * P:src * D + f * P + P], sl[:, 0, k, :],
                              start=(k == 0), stop=(k == KC - 1))
            m.then_inc(S["modc_mm"], 1)
            for j, src in ((GA, 2), (GB, 5), (CB, 4), (SB, 3)):
                for b in range(B):
                    for k in range(KC):
                        m = M(bank[1 + j][:, D * b:D * b + D], rep[:, k, b, :], wm[:, k, src * D:src * D + D],
                              start=(k == 0), stop=(k == KC - 1))
                m.then_inc(S["bc_mm"], 1)
            pe.wait_ge(S["mod_done"], 1)
            pe.wait_ge(S["w_in"], 128)
            for g in range(8):
                pe.wait_ge(S["xn_done"], 4 * g + 4)
                for k in range(KC):
                    if g >= 1:
                        pe.wait_ge(S["hT_done"], 2 * (g - 1) + k + 1)
                    for t in range(4):
                        m = nc.tensor.transpose(bank[k][:, P * t:P * t + P], xn[:, g % 2, t, P * k:P * k + P], ident)
                    m.then_inc(S["xT_mm"], 1)
                pe.wait_ge(S["hT_done"], 2 * g + 2)
                for s in range(2):
                    if g >= 1:
                        pe.wait_ge(S["qk_used"], 2 * (g - 1) + s + 1)
                    for ab in range(2):
                        for k in range(KC):
                            m = M(bank[2 + 2 * s + ab], wqk_s[:, k, 2 * s + ab, :], hT[:, g % 2, k, :],
                                  start=(k == 0), stop=(k == KC - 1))
                    m.then_inc(S["qk_mm"], 1)
                if g >= 1:
                    pe.wait_ge(S["v_used"], 4 * g)
                for t in range(4):
                    for k in range(KC):
                        m = M(bank[6 + t // 2][:, D * (t % 2):D * (t % 2) + D], hT[:, g % 2, k, P * t:P * t + P],
                              wv_s[:, k, :], start=(k == 0), stop=(k == KC - 1))
                m.then_inc(S["v_mm"], 1)

            def score(i, par, item, q, kq, free):
                if free:
                    pe.wait_ge(S["mxfree"], v1(i, 4 * PU, item - 1))
                M(bank[4 + item % 2], qmx[:, par, P * q:P * q + P], kmx[:, par, 512 * kq:512 * kq + 512],
                  start=True, stop=True).then_inc(S["item"], 1)

            def turn(i, item, par, count):
                pe.wait_ge(S["nmp_done"], v1(i, 4, count))
                pe.wait_ge(S["mxfree"], v1(i, 4 * PU, item - 1))
                nc.tensor.transpose(bank[4 + item % 2].bitcast(bf16)[0:3 * QT, 0:P],
                                    nmp[:, par].rearrange("p c t -> p (c t)"), identb[:]).then_inc(S["item"], 1)

            def scoresT(i, c_):
                n, half, k = c_ // 32 % 2, c_ // NKT % 2, c_ % NKT
                if not (isinstance(i, int) and i == 0 and c_ < 2):
                    pe.wait_ge(S["p_done"], v1(i, 64, c_ - 1))
                s = c_ % 2
                for j in range(2):
                    q0 = UQ * half + 512 * j
                    m = M(bank[2 * s + j], kex[:, n, P * k:P * k + P], qex[:, n, q0:q0 + 512], start=True, stop=True)
                m.then_inc(S["st_mm"], 1)

            def unit_ready(i, c_):
                n, half = c_ // 32 % 2, c_ // NKT % 2
                if half == 0:
                    pe.wait_ge(S[f"exld{n}"], v1(i, 96, 96 * (c_ // 64 + 1)))
                pe.wait_ge(S[f"shift{half}"], v1(i, 32, 16 * (c_ // 32 + 1)))

            def weigh(i, c_):
                n, unit, k = c_ // 32 % 2, c_ // NKT % 2, c_ % NKT
                pe.wait_ge(S["p_done"], v1(i, 64, c_ + 1))
                if k == 0 and not (isinstance(i, int) and i == 0 and c_ < 32):
                    pe.wait_ge(S["o_done"], v1(i, 4, c_ // NKT - 1))
                if k == 0 and unit == 0:
                    pe.wait_ge(S["vst_done"], v1(i, 2, n + 1))
                for g in range(4):
                    m = M(bank[6 + unit][32 * g:32 * g + VW, 0:256], vst[:, n, k, :],
                          pr[:, c_ % 4, 256 * g:256 * g + 256], start=(k == 0), stop=(k == NKT - 1),
                          tile_position=(0, 32 * g))
                m.then_inc(S["pv_mm"], 1)

            pe.wait_ge(S["mxld0"], 96)
            pe.wait_ge(S["idb"], 1)
            pe.wait_ge(S["r_done"], 8)
            for k in range(32):
                score(0, 0, k, k // 4, k % 4, k >= 2)
            turn(0, 32, 0, 1)
            for k in range(32):
                score(0, 0, 33 + k, QT + k // 4, k % 4, True)
            unit_ready(0, 0)
            pe.wait_ge(S["v_one"], 4)
            pe.wait_ge(S["v_used"], 32)
            scoresT(0, 0)

            def att_body(i, last):
                for u in range(4):
                    n, half = u // 2, u % 2
                    quiet = last and u >= 2
                    base = PRO + PU * u
                    for k in range(NKT):
                        c_ = NKT * u + k
                        if not (last and c_ == 63):
                            if k == NKT - 1:
                                unit_ready(i, c_ + 1)
                            scoresT(i, c_ + 1)
                        if not quiet:
                            if k == 0 and half == 0:
                                pe.wait_ge(S[f"mxld{1 - n}"], v1(i, 96, 96 * (n + 1)))
                            for j in range(2):
                                m = 2 * k + j
                                score(i, 1 - n, base + m + (m >= 10), QT * half + m // 4, m % 4, True)
                        if k == 4 and not (last and u == 3):
                            turn(i, base + (0 if quiet else 10), (u + 1) % 2, u + 2)
                        weigh(i, c_)

            att_body(0, False)
            with pe.Fori(1, NBODY - 1) as i:
                att_body(i, False)
            att_body(NBODY - 1, True)

            pe.wait_ge(S["ctx_done"], B * KC)
            for t in range(TT):
                if t >= 2:
                    pe.wait_ge(S["x1_done"], t - 1)
                for k in range(KC):
                    m = M(bank[t % 2][:, 0:D], cxT[:, k, P * t:P * t + P], wo_s[:, k, :],
                          start=(k == 0), stop=(k == KC - 1))
                m.then_inc(S["wo_mm"], 1)
            for t in range(TT):
                pe.wait_ge(S["h2_done"], t + 1)
                if t >= 2:
                    pe.wait_ge(S["h2T_done"], t - 1)
                for k in range(KC):
                    m = nc.tensor.transpose(bank[2 + t % 2][:, P * k:P * k + P], h2[:, t, P * k:P * k + P], ident)
                m.then_inc(S["h2T_mm"], 1)
                pe.wait_ge(S["h2T_done"], t + 1)
                for k in range(KC):
                    m = M(bank[4][:, NE * t:NE * t + NE], h2T[:, t % 2, k, :], wg_s[:, k, :],
                          start=(k == 0), stop=(k == KC - 1))
                m.then_inc(S["lg_mm"], 1)
            pe.wait_ge(S["oh_done"], 1)
            ohf = oh[:].rearrange("p k t e -> p (k t e)")
            M(bank[5], tri, ohf, start=True, stop=True).then_inc(S["cum_mm"], 1)
            M(bank[6], onesm[:], ohf, start=True, stop=True).then_inc(S["cum_mm"], 1)

            def turn_rows(i, n):
                pe.wait_ge(S[f"xr_in{n % 2}"], v1(i, 16 * NB, 16 * (n // 2 + 1)))
                if not (isinstance(i, int) and i * 2 * NB + n < 2):
                    pe.wait_ge(S["xT_sb"], v1(i, 2 * NB, n - 1))
                for k in range(KC):
                    for t in range(2):
                        m = nc.tensor.transpose(bank[6 + n % 2][:, BLK * k + P * t:BLK * k + P * t + P],
                                                xr[:, n % 2, t, P * k:P * k + P], ident)
                m.then_inc(S["tx_mm"], 1)

            pe.wait_ge(S["idx_done"], 1)
            turn_rows(0, 0)

            def moe_body(i, last):
                for e in range(2):
                    for b in range(NB):
                        n = e * NB + b
                        if b == 0:
                            pe.wait_ge(S[f"w1_in{e}"], v1(i, 16, 16))
                            pe.wait_ge(S[f"w2_in{e}"], v1(i, 16, 16))
                        pe.wait_ge(S["xT_sb"], v1(i, 2 * NB, n + 1))
                        for hf in range(2):
                            if not (isinstance(i, int) and i == 0 and n == 0):
                                pe.wait_ge(S["hd_done"], v1(i, 4 * NB, 2 * (n - 1) + hf + 1))
                            for mm in range(4):
                                f = 4 * hf + mm
                                o = ps[:, 2 * hf + mm // 2, BLK * (mm % 2):BLK * (mm % 2) + BLK]
                                for k in range(KC):
                                    m = M(o, w1[:, e, k, P * f:P * f + P], xT[:, n % 2, k, :],
                                          start=(k == 0), stop=(k == KC - 1))
                            m.then_inc(S["fc_mm"], 1)
                        if not (last and n == 2 * NB - 1):
                            turn_rows(i, n + 1)
                        for t in range(2):
                            if not (isinstance(i, int) and i == 0 and n == 0):
                                pe.wait_ge(S["y_done"], v1(i, 4 * NB, 2 * (n - 1) + t + 1))
                            for f in range(HID // P):
                                if t == 0 and f % 4 == 0:
                                    pe.wait_ge(S["hd_done"], v1(i, 4 * NB, 2 * n + f // 4 + 1))
                                m = M(bank[4 + t][:, 0:D], hd[:, n % 2, f, P * t:P * t + P], w2[:, e, f, :],
                                      start=(f == 0), stop=(f == HID // P - 1))
                            m.then_inc(S["pj_mm"], 1)

            moe_body(0, False)
            with pe.Fori(1, NE // 2 - 1) as i:
                moe_body(i, False)
            moe_body(NE // 2 - 1, True)


_ORDER = ["x", "wqk", "bqk", "wv", "bv", "wo", "bo", "wg", "cfc", "cproj", "c", "wmod", "trig", "consts"]


def kernel(L0_attn_x, L0_attn_Wq, L0_attn_bq, L0_attn_Wk, L0_attn_bk, L0_attn_Wv, L0_attn_bv, L0_attn_Wo,
           L0_attn_bo, L0_ffn_w_g, L0_ffn_c_fc, L0_ffn_c_proj, L0_c, L0_wmod):
    import concourse.bacc as bacc
    from concourse.bass_utils import run_bass_kernel_spmd

    order = np.arange(D).reshape(H, 2, DH // 2).transpose(1, 0, 2).reshape(2, P)
    wq, wk = np.asarray(L0_attn_Wq)[:, order], np.asarray(L0_attn_Wk)[:, order]
    bq, bk = np.asarray(L0_attn_bq)[order], np.asarray(L0_attn_bk)[order]
    f = np.arange(DH // 2, dtype=np.float32)
    inv = (np.float32(1.0) / np.float32(10000.0) ** (f / np.float32(DH // 2))).astype(np.float32)
    ang = np.tile((np.arange(T, dtype=np.float32)[:, None] * inv[None]).T, (H, 1))
    consts = np.zeros((P, 336), np.float32)
    consts[:, 0:128] = np.eye(P)
    consts[:, 128:256] = np.triu(np.ones((P, P)), 1)
    consts[:, 256:264] = np.arange(NE) - 8
    consts[:, 264:272] = np.arange(NE)
    consts[:, 272:336] = (TRASH + np.arange(2)[None, :, None] * N + np.arange(TT)[None, None] * P
                          + np.arange(P)[:, None, None]).reshape(P, 2 * TT)
    arrays = {
        "x": np.asarray(L0_attn_x), "wqk": np.stack([wq[:, 0], wq[:, 1], wk[:, 0], wk[:, 1]], 1),
        "bqk": np.stack([bq[0], bq[1], bk[0], bk[1]], 1), "wv": np.asarray(L0_attn_Wv),
        "bv": np.asarray(L0_attn_bv).reshape(KC, P).T, "wo": np.asarray(L0_attn_Wo), "bo": np.asarray(L0_attn_bo),
        "wg": np.asarray(L0_ffn_w_g), "cfc": np.asarray(L0_ffn_c_fc), "cproj": np.asarray(L0_ffn_c_proj),
        "c": np.asarray(L0_c).T.reshape(KC, P, B).transpose(1, 0, 2), "wmod": np.asarray(L0_wmod),
        "trig": np.stack([np.cos(ang), np.sin(ang)], 1).astype(np.float32), "consts": consts,
    }
    arrays = {k: np.ascontiguousarray(v) for k, v in arrays.items()}
    nc = bacc.Bacc("TRN2", target_bir_lowering=False, num_devices=1)
    args = [nc.dram_tensor(k, arrays[k].shape, mybir.dt.from_np(arrays[k].dtype), kind="ExternalInput").ap()
            for k in _ORDER]
    out = nc.dram_tensor("out", (B, T, D), mybir.dt.float32, kind="ExternalOutput").ap()
    adaln_block(nc, *args, out)
    r = run_bass_kernel_spmd(nc, [arrays], core_ids=[0])
    return r.results[0]["out"]
```

```python
from contextlib import ExitStack

import numpy as np

import concourse.bass as bass
from concourse import mybir

B, T, D = 2, 2048, 256
N = B * T
H, DH = 16, 16
BH = B * H
NE, HID = 8, 1024
P = 128
TT = N // P
KC = D // P
CAP = int(2 * 1.25 * N / NE)
CAP += CAP % 2
SLOTS = NE * CAP
BLK = 256
NB = CAP // BLK
assert NB * BLK == CAP
TRASH = SLOTS + BLK
XROWS = TRASH + 2 * N
EPS = 1e-5

QT = 8
UQ = QT * P
NKT = T // P
VW = 32
KS = 6 * DH
PRO = 65
ROUTER_AT = 33000
PU = 33


def adaln_block(nc, x, wqk, bqk, wv, bv, wo, bo, wg, cfc, cproj, c, wmod, trig, consts, out):
    f32, bf16, i32, f32r = mybir.dt.float32, mybir.dt.bfloat16, mybir.dt.int32, mybir.dt.float32r
    ALU, ACT, AX = mybir.AluOpType, mybir.ActivationFunctionType, mybir.AxisListType

    qs = nc.dram_tensor("q_parts", [BH, 3 * DH, T], bf16, kind="Internal").ap()
    ks = nc.dram_tensor("k_parts", [BH, 3 * DH, T], bf16, kind="Internal").ap()
    os_ = nc.dram_tensor("o_heads", [2, BH, DH + 1, T], f32, kind="Internal").ap()
    linv = nc.dram_tensor("inv_sums", [BH, T], f32, kind="Internal").ap()
    xe = nc.dram_tensor("x_slots", [XROWS, D], f32, kind="Internal").ap()
    ye = nc.dram_tensor("y_slots", [SLOTS, D], f32, kind="Internal").ap()

    ctx = ExitStack()
    with ctx:
        def sb(name, shape, dt=f32, stack=ctx):
            return stack.enter_context(nc.sbuf_tensor(name, shape, dt))

        def sem(name):
            return ctx.enter_context(nc.semaphore(name))

        xs = sb("xs", [P, TT, D])
        cst = sb("cst", [P, 336])
        ident, tri = cst[:, 0:128], cst[:, 128:256]
        iota_m8, iota8 = cst[:, 256:264], cst[:, 264:272]
        trash_id = cst[:, 272:336]
        identb = sb("identb", [P, P], bf16)
        bc = sb("bc", [P, 4, B, D])
        GA, GB, CB, SB = range(4)
        bob = sb("bob", [P, D])
        wo_s = sb("wo_s", [P, KC, D])
        wg_s = sb("wg_s", [P, KC, NE])
        bv_s = sb("bv_s", [P, KC])
        stats = sb("stats", [P, TT, 6])
        mv = sb("mv", [P, TT, 2])
        std = sb("std", [P, TT])
        rstd = sb("rstd", [P, TT])
        lg = sb("lg", [P, TT, NE])
        pw = sb("pw", [P, 2, TT])
        idx = sb("idx", [P, 2, 2, TT], i32)

        att = ExitStack()
        vall = sb("vall", [P, BH, NKT, DH + 1], stack=att)
        stk = sb("stk", [P, 4, T], bf16, att)
        qmx, kmx = stk[0:KS, 0:2, :], stk[0:KS, 2:4, :]
        qex = sb("qex", [KS + 3, 2, T], bf16, att)
        kex = sb("kex", [KS + 3, 2, T], bf16, att)
        vst = sb("vst", [P, 2, NKT, VW], stack=att)
        pr = sb("pr", [P, 4, UQ], stack=att)
        osb = sb("osb", [P, 512], stack=att)
        zero = osb[:]
        mxp = sb("mxp", [P, 2, QT, 4], stack=att)
        nm = sb("nm", [P, 2, QT], stack=att)
        nmr = sb("nmr", [P, 2, 2, QT], stack=att)
        nil = sb("nil", [P, QT], stack=att)
        nmp = sb("nmp", [P, 2, 3, QT], bf16, att)
        nms = sb("nms", [3 * QT, 2, P], bf16, att)

        pre = ExitStack()
        wqk_s = sb("wqk_s", [P, KC, 4, P], stack=pre)
        bqk_s = sb("bqk_s", [P, 4], stack=pre)
        wv_s = sb("wv_s", [P, KC, D], stack=pre)
        trg = sb("trg", [P, 2, T], stack=pre)
        cT = sb("cT", [P, KC, B], stack=pre)
        sl = sb("sl", [P, 3, KC, B], stack=pre)
        modc = sb("modc", [P, 2, KC, B], stack=pre)
        hT = sb("hT", [P, 2, KC, 512], stack=pre)
        rq = sb("rq", [P, 2, 4, 512], stack=pre)
        gts = pr[:, 0, 0:2 * D].rearrange("p (a d) -> p a d", a=2)
        tq = pr[:, 0:2, :].rearrange("p a n -> p (a n)").rearrange("p (a n) -> p a n", a=4)
        xn = pr[:, 2:4, :].rearrange("p r (t d) -> p r t d", t=4)
        parts = sb("parts", [P, 2, 3, 4, 512], bf16, pre)
        rep = parts[:, 0, 0, :, :].rearrange("p s n -> p (s n)").bitcast(f32) \
            .rearrange("p (k b n) -> p k b n", k=KC, b=B)[:, :, :, 0:P]
        wm = stk[:].rearrange("p a n -> p (a n)").bitcast(f32)[:, 0:KC * 6 * D].rearrange("p (k n) -> p k n", k=KC)
        pre.close()

        epi = ExitStack()
        h2 = sb("h2", [P, TT, D], stack=epi)
        h2T = sb("h2T", [P, 2, KC, P], stack=epi)
        t2 = sb("t2", [P, 2, 2, D], stack=epi)
        ls = sb("ls", [P, 256], stack=epi)
        cxT = sb("cxT", [P, KC, T], stack=epi)
        lT = sb("lT", [P, KC, T], stack=epi)
        epi.close()
        att.close()

        moe = ExitStack()
        stg = sb("stg", [P, 2, HID * KC], stack=moe)
        w1p = [sb(f"w1{c_}", [P, 2, KC, HID], f32r, moe) for c_ in "hl"]
        w2p = [sb(f"w2{c_}", [P, 2, HID // P, D], f32r, moe) for c_ in "hl"]
        sb("clear", [P, 2048], stack=moe)
        xTp = [sb(f"xT{c_}", [P, 2, KC, BLK], f32r, moe) for c_ in "hl"]
        hd = sb("hd", [P, 2, 4, BLK], stack=moe)
        hdp = [sb(f"hd{c_}", [P, 2, HID // P, BLK], f32r, moe) for c_ in "hl"]
        xr = sb("xr", [P, 2, 2, D], stack=moe)
        yb = sb("yb", [P, 2, 2, D], stack=moe)
        ga_ = sb("gath", [P, 4, 2, D], stack=moe)
        moe.close()
        rt = ExitStack()
        sb("hold", [P, ROUTER_AT], stack=rt)
        oh = sb("oh", [P, 2, TT, NE], stack=rt)
        lw = sb("lw", [P, TT, NE], stack=rt)
        lw2 = sb("lw2", [P, TT, NE], stack=rt)
        sel = sb("sel", [P, TT, NE], stack=rt)
        m12 = sb("m12", [P, 4, TT], stack=rt)
        pf = sb("pf", [P, 2, 64, NE], stack=rt)
        rk = sb("rk", [P, 4, 2, TT], stack=rt)
        onesm = sb("onesm", [P, P], stack=rt)
        rt.close()

        ps = ctx.enter_context(nc.psum_tensor("ps", [P, 8, 512], f32))
        bank = [ps[:, b, :] for b in range(8)]

        names = """c_in w_in x_in0 x_in1 x_in2 x_in3 zero_set zero_out v_one
            sil_exp sil_rep modc_mm bc_mm mod_done dch pch ach std_in std_out xn_done xT_mm hT_done
            qk_mm qk_used v_mm v_used r_done hi_done mid_in mid_done lo_in lo_done parts_out0 parts_out1 idb
            mxld0 mxld1 exld0 exld1 item mxfree nm_done nmp_done shift0 shift1
            vst_done st_mm p_done pv_mm o_done oout0 oout1
            bo_mm bo_done l_in l_rec l_out lb_in cx_in cx_pool cx_dve wo_mm x1_done xn2_done h2_dve h2_pool
            h2T_mm h2T_done lg_mm lg_out
            ex_in ex_done oh_done cum_mm idx_done slots_in wt_in wt_hi wt_done xr_in0 xr_in1 tx_mm xT_hi xT_sb
            fc_mm hh_done ht_done hl_done pj_mm y_done y_out0 y_out1 g_in0 g_in1 g_in2 g_in3 comb out_done""".split()
        S = {n: sem(n) for n in names}

        block = ctx.enter_context(nc.Block())

        def turned(i, u):
            if isinstance(i, int) and 4 * i + u == 0:
                return 33
            quiet = isinstance(i, int) and 4 * i + u == 2 * BH - 1
            return v1(i, 4 * PU, PRO + PU * (u - 1) + (1 if quiet else 11))

        def v1(i, a, c_):
            return i * a + c_

        NBODY = BH // 2
        SPLIT = NBODY // B
        TB = TT // B

        @block.sync
        def _(sp):
            sp.dma_start(cT[:], c).then_inc(S["c_in"], 16)
            sp.dma_start(wm, wmod.rearrange("(k p) n -> p k n", p=P)).then_inc(S["c_in"], 16)
            sp.dma_start(cst[:], consts).then_inc(S["c_in"], 16)
            xv = x.rearrange("b (t p) d -> p (b t) d", p=P)
            for q in range(4):
                sp.dma_start(xs[:, 8 * q:8 * q + 8, :], xv[:, 8 * q:8 * q + 8, :]).then_inc(S[f"x_in{q}"], 16)
            sp.dma_start(wqk_s[:], wqk.rearrange("(k p) s n -> p k s n", p=P)).then_inc(S["w_in"], 16)
            sp.dma_start(bqk_s[:], bqk).then_inc(S["w_in"], 16)
            sp.dma_start(wv_s[:], wv.rearrange("(k p) n -> p k n", p=P)).then_inc(S["w_in"], 16)
            sp.dma_start(trg[:], trig).then_inc(S["w_in"], 16)
            sp.dma_start(wo_s[:], wo.rearrange("(k p) n -> p k n", p=P)).then_inc(S["w_in"], 16)
            sp.dma_start(wg_s[:], wg.rearrange("(k p) n -> p k n", p=P)).then_inc(S["w_in"], 16)
            sp.dma_start(bv_s[:], bv).then_inc(S["w_in"], 16)
            sp.dma_start(bob[:], bo.rearrange("(a n) -> a n", a=1).broadcast_to([P, D])).then_inc(S["w_in"], 16)

            sp.wait_ge(S["zero_set"], 1)
            zv = xe[0:TRASH, :].rearrange("(p r) d -> p (r d)", p=P)
            ZN = TRASH // P * D // 512
            for z in range(ZN):
                sp.dma_start(zv[:, 512 * z:512 * z + 512], zero).then_inc(S["zero_out"], 16)

            for g in range(8):
                b, t0 = g // 4, g % 4 * 512
                sp.wait_ge(S["lo_done"], g + 1)
                for s, scr in ((0, qs), (1, ks)):
                    for part in range(3):
                        row = (part if s == 0 else 2 - part) * DH
                        for ab in range(2):
                            dst = scr[b * H:(b + 1) * H, row + 8 * ab:row + 8 * ab + 8, t0:t0 + 512]
                            sp.dma_start(dst, parts[:, g % 2, part, 2 * s + ab, :]) \
                                .then_inc(S[f"parts_out{g % 2}"], 16)
            for par in range(2):
                sp.wait_ge(S[f"parts_out{par}"], 4 * 12 * 16)

            def load_stacks(qd, kd, par, head, sm):
                for dst, scr, q in ((qd, qs, True), (kd, ks, False)):
                    sp.dma_start(dst[0:48, par, :], scr[head, :, :]).then_inc(sm, 16)
                    src = scr[head, 0:32, :] if q else scr[head, 16:48, :]
                    sp.dma_start(dst[48:80, par, :], src).then_inc(sm, 16)
                    src = scr[head, 0:16, :] if q else scr[head, 32:48, :]
                    sp.dma_start(dst[80:96, par, :], src).then_inc(sm, 16)

            def shift(par, half, count):
                sp.wait_ge(S["mxfree"], count)
                dst = qex[KS:KS + 3, par, UQ * half:UQ * half + UQ].rearrange("r (t q) -> r t q", t=QT)
                sp.dma_start(dst, nms[:, half, :]).then_inc(S[f"shift{half}"], 16)

            load_stacks(qmx, kmx, 0, 0, S["mxld0"])
            load_stacks(qmx, kmx, 1, 1, S["mxld1"])
            load_stacks(qex, kex, 0, 0, S["exld0"])
            shift(0, 0, turned(0, 0))

            def body(i, last):
                for n in range(2):
                    head = i * 2 + n
                    final = last and n == 1
                    if not last:
                        sp.wait_ge(S["item"], v1(i, 4 * PU, PRO + 2 * PU * n))
                        load_stacks(qmx, kmx, n, i * 2 + (n + 2), S[f"mxld{n}"])
                    if not final:
                        if n or not isinstance(i, int):
                            sp.wait_ge(S["st_mm"], v1(i, 64, 32 * n))
                        load_stacks(qex, kex, 1 - n, i * 2 + (n + 1), S[f"exld{1 - n}"])
                    shift(n, 1, turned(i, 2 * n + 1))
                    for half in range(2):
                        sp.wait_ge(S["o_done"], v1(i, 4, 2 * n + half + 1))
                        for g in range(4):
                            q0 = UQ * half + 512 * (g % 2)
                            sp.dma_start(os_[g // 2, head, :, q0:q0 + 512],
                                         osb[32 * g:32 * g + DH + 1, :]).then_inc(S[f"oout{half}"], 16)
                        if half == 0 and not final:
                            shift(1 - n, 0, turned(i, 2 * n + 2))

            with sp.Fori(0, NBODY - 1) as i:
                body(i, False)
            body(NBODY - 1, True)

            sp.wait_ge(S["slots_in"], 2 * TT * 16)

            def load_rows_at(par, blk):
                sp.dma_start(xr[:, par], xe.rearrange("(g t p) d -> g p t d", p=P, t=2)[blk]) \
                    .then_inc(S[f"xr_in{par}"], 16)

            load_rows_at(0, 0)
            load_rows_at(1, 1)

            def moe_body(i, last):
                for e in range(2):
                    for b in range(NB):
                        n = e * NB + b
                        if not (last and n >= 2 * NB - 1):
                            sp.wait_ge(S["tx_mm"], v1(i, 2 * NB, n + 1))
                            load_rows_at(n % 2, i * (2 * NB) + (n + 2))
                        sp.wait_ge(S["y_done"], v1(i, 4 * NB, 2 * n + 2))
                        sp.dma_start(ye.rearrange("(g t p) d -> g p t d", p=P, t=2)[i * (2 * NB) + n],
                                     yb[:, n % 2]).then_inc(S[f"y_out{n % 2}"], 16)

            with sp.Fori(0, NE // 2 - 1) as i:
                moe_body(i, False)
            moe_body(NE // 2 - 1, True)

            ov = out.rearrange("b (t p) d -> p (b t) d", p=P)
            for q in range(4):
                sp.wait_ge(S["comb"], 8 * q + 8)
                sp.dma_start(ov[:, 8 * q:8 * q + 8, :], xs[:, 8 * q:8 * q + 8, :]).then_inc(S["out_done"], 16)
            sp.wait_ge(S["out_done"], 64)
            sp.wait_ge(S["zero_out"], 16 * ZN)

        @block.vector
        def _(dve):
            V = nc.vector
            chain = [0]

            def link(ins):
                chain[0] += 1
                ins.then_inc(S["dch"], 1)
                dve.wait_ge(S["dch"], chain[0])

            V.memset(zero, 0.0).then_inc(S["zero_set"], 1)
            V.memset(nil[:], 0.0).then_inc(S["v_one"], 1)
            V.memset(vst[:], 0.0).then_inc(S["v_one"], 1)
            V.memset(vall[:, :, :, DH:DH + 1], 1.0).then_inc(S["v_one"], 1)
            V.memset(onesb := kex[KS:KS + 3, :, :], 1.0).then_inc(S["v_one"], 1)
            dve.wait_ge(S["sil_exp"], 1)
            link(V.tensor_scalar(sl[:, 1], sl[:, 0], 1.0, None, ALU.add))
            link(V.reciprocal(sl[:, 2], sl[:, 1]))
            link(V.tensor_tensor(sl[:, 0], cT[:], sl[:, 2], ALU.mult))
            V.tensor_copy(rep, sl[:, 0].unsqueeze(3).broadcast_to([P, KC, B, P])).then_inc(S["sil_rep"], 1)
            dve.wait_ge(S["c_in"], 48)
            V.tensor_copy(identb[:], ident).then_inc(S["idb"], 1)
            dve.wait_ge(S["modc_mm"], 1)
            mc = bank[0][:, 0:8].rearrange("p (j k b) -> p j k b", j=2, k=KC)
            link(V.tensor_copy(modc[:, 0], mc[:, 0]))
            link(V.tensor_scalar(modc[:, 1], mc[:, 1], 1.0, None, ALU.add))
            for j in (GA, GB):
                dve.wait_ge(S["bc_mm"], j + 1)
                for b in range(B):
                    g = bank[1 + j][:, D * b:D * b + D]
                    link(V.tensor_scalar(gts[:, 0], g, 0.0, 2.0, ALU.is_ge, ALU.mult))
                    link(V.tensor_scalar(gts[:, 1], g, -1.0, 0.25, ALU.mult, ALU.max))
                    link(V.tensor_tensor(gts[:, 1], g, gts[:, 1], ALU.max))
                    link(V.scalar_tensor_tensor(bc[:, j, b], gts[:, 0], -1.0, gts[:, 1], ALU.add, ALU.mult))
            dve.wait_ge(S["bc_mm"], CB + 1)
            link(V.tensor_scalar(bc[:, CB], bank[1 + CB].rearrange("p (b n) -> p b n", b=B), 1.0, None, ALU.add))
            dve.wait_ge(S["bc_mm"], SB + 1)
            V.tensor_copy(bc[:, SB], bank[1 + SB].rearrange("p (b n) -> p b n", b=B)).then_inc(S["mod_done"], 1)
            dve.wait_ge(S["w_in"], 128)
            dve.wait_ge(S["bc_mm"], 4)
            V.tensor_copy(rep[:, :, 0, :], bv_s[:].unsqueeze(2).broadcast_to([P, KC, P])).then_inc(S["bo_done"], 1)
            dve.wait_ge(S["bo_mm"], 1)
            link(V.tensor_tensor(bob[:], bank[5][:, 0:D], bob[:], ALU.add))

            def norm_std(k, n0, n1):
                V.tensor_scalar(std[:, n0:n1], mv[:, n0:n1, 1], EPS, None, ALU.add).then_inc(S["std_in"], 1)
                dve.wait_ge(S["std_out"], k)
                link(V.reciprocal(rstd[:, n0:n1], std[:, n0:n1]))

            for t in range(TT):
                if t % 8 == 0:
                    dve.wait_ge(S[f"x_in{t // 8}"], 16)
                link(V.bn_stats(stats[:, t, :], xs[:, t, :]))
                link(V.bn_aggr(mv[:, t, :], stats[:, t, :]))
            norm_std(1, 0, TT)

            def normed(g):
                if g >= 2:
                    dve.wait_ge(S["xT_mm"], 2 * (g - 1))
                for t in range(4):
                    n = 4 * g + t
                    V.tensor_scalar(xn[:, g % 2, t, :], xs[:, n, :], mv[:, n, 0:1], rstd[:, n:n + 1],
                                    ALU.subtract, ALU.mult).then_inc(S["xn_done"], 1)

            normed(0)
            dve.wait_ge(S["w_in"], 128)
            for g in range(8):
                if g < 7:
                    normed(g + 1)
                pos = slice(g % 4 * 512, g % 4 * 512 + 512)
                cos, sin = trg[:, 0, pos], trg[:, 1, pos]
                if g >= 2:
                    dve.wait_ge(S["lo_in"], g - 1)
                    dve.wait_ge(S["lo_done"], g - 1)
                for s in range(2):
                    dve.wait_ge(S["qk_mm"], 2 * g + s + 1)
                    a, b_ = bank[2 + 2 * s], bank[3 + 2 * s]
                    ba, bb = bqk_s[:, 2 * s:2 * s + 1], bqk_s[:, 2 * s + 1:2 * s + 2]
                    link(V.scalar_tensor_tensor(tq[:, 0], a, ba, cos, ALU.add, ALU.mult))
                    link(V.scalar_tensor_tensor(tq[:, 1], b_, bb, sin, ALU.add, ALU.mult))
                    link(V.scalar_tensor_tensor(tq[:, 2], a, ba, sin, ALU.add, ALU.mult))
                    link(V.scalar_tensor_tensor(tq[:, 3], b_, bb, cos, ALU.add, ALU.mult))
                    V.tensor_tensor(rq[:, g % 2, 2 * s], tq[:, 0], tq[:, 1], ALU.subtract).then_inc(S["qk_used"], 1)
                    link(V.tensor_tensor(rq[:, g % 2, 2 * s + 1], tq[:, 2], tq[:, 3], ALU.add))
                    V.engine_nop().then_inc(S["r_done"], 1) if False else None
                V.memset(stats[:, 0, 0:1], 0.0).then_inc(S["r_done"], 1)

            def reduce_item(i, c_, q, kq, par, first_of_unit, units_before):
                dve.wait_ge(S["item"], v1(i, 4 * PU, c_ + 1))
                if first_of_unit and (units_before is not None):
                    dve.wait_ge(S["nm_done"], units_before)
                V.reduce_max(mxp[:, par, q, kq:kq + 1], bank[4 + c_ % 3], AX.X).then_inc(S["mxfree"], 1)

            def unit_max(i, c_, par, count):
                dve.wait_ge(S["mxfree"], v1(i, 4 * PU, c_ + 1))
                V.tensor_reduce(nm[:, par, :], mxp[:, par], AX.X, ALU.max, negate=True).then_inc(S["nm_done"], 1)

            for k in range(32):
                reduce_item(0, k, k // 4, k % 4, 0, False, None)
            unit_max(0, 31, 0, 0)
            dve.wait_ge(S["item"], 33)
            V.tensor_copy(nms[:, 0, :], bank[4 + 32 % 3].bitcast(bf16)[0:3 * QT, 0:P]).then_inc(S["mxfree"], 1)
            for k in range(32):
                reduce_item(0, 33 + k, k // 4, k % 4, 1, False, None)

            def att_body(i, last):
                for u in range(4):
                    base = PRO + PU * u
                    quiet = last and u >= 2
                    for k in range(32):
                        if k == 3 and not (last and u == 3):
                            if not (isinstance(i, int) and i == 0 and u == 0):
                                dve.wait_ge(S["nmp_done"], v1(i, 4, u))
                            unit_max(i, base - 1, (u + 1) % 2, 0)
                        if k == 10 and not (last and u == 3):
                            c_ = base + (0 if quiet else 10)
                            dve.wait_ge(S["item"], v1(i, 4 * PU, c_ + 1))
                            par = (u + 1) % 2
                            src = bank[4 + c_ % 3].bitcast(bf16)[0:3 * QT, 0:P]
                            heads = (u + 1) // 2
                            dve.wait_ge(S[f"shift{par}"], v1(i, 32, 16 * heads)) \
                                if (heads or not isinstance(i, int)) else None
                            V.tensor_copy(nms[:, par, :], src).then_inc(S["mxfree"], 1)
                        if not quiet:
                            c_ = base + k + (k >= 10)
                            if k == 0:
                                dve.wait_ge(S["nm_done"], v1(i, 4, u + 1))
                            reduce_item(i, c_, k // 4, k % 4, u % 2, False, None)
                        if u == 1 and k == 16 and isinstance(i, int) and i == SPLIT:
                            inv_sums(0)
            def inv_sums(b):
                dve.wait_ge(S["l_in"], 32 * (b + 1))
                V.reciprocal(ls[:], ls[:]).then_inc(S["l_rec"], 1)

            def batch_end(b):
                for t in range(TB * b, TB * b + TB):
                    dve.wait_ge(S["wo_mm"], t + 1)
                    y = t2[:, t % 2]
                    link(V.tensor_tensor(y[:, 0, :], bank[4 + t % 2][:, 0:D], bob[:], ALU.add))
                    link(V.tensor_tensor(y[:, 1, :], y[:, 0, :], bc[:, GA, b], ALU.mult))
                    V.tensor_tensor(xs[:, t, :], xs[:, t, :], y[:, 1, :], ALU.add).then_inc(S["x1_done"], 1)
                    dve.wait_ge(S["x1_done"], t + 1)
                    link(V.bn_stats(stats[:, t, :], xs[:, t, :]))
                    link(V.bn_aggr(mv[:, t, :], stats[:, t, :]))
                norm_std(2 + b, TB * b, TB * b + TB)
                for t in range(TB * b, TB * b + TB):
                    y = t2[:, t % 2]
                    if t % 2 and t > 1:
                        dve.wait_ge(S["h2_pool"], t // 2)
                    V.tensor_scalar(y[:, 0, :], xs[:, t, :], mv[:, t, 0:1], rstd[:, t:t + 1],
                                    ALU.subtract, ALU.mult).then_inc(S["xn2_done"], 1)
                    if t % 2 == 0:
                        dve.wait_ge(S["xn2_done"], t + 1)
                        link(V.tensor_tensor(y[:, 1, :], y[:, 0, :], bc[:, CB, b], ALU.mult))
                        V.tensor_tensor(h2[:, t, :], y[:, 1, :], bc[:, SB, b], ALU.add).then_inc(S["h2_dve"], 1)
                dve.wait_ge(S["lg_mm"], TB * b + TB)
                V.tensor_copy(lg[:, TB * b:TB * b + TB, :],
                              bank[6][:, 0:TB * NE].rearrange("p (t e) -> p t e", e=NE)).then_inc(S["lg_out"], 1)

            with dve.Fori(0, SPLIT) as i:
                att_body(i, False)
            att_body(SPLIT, False)
            batch_end(0)
            with dve.Fori(SPLIT + 1, NBODY - 1) as i:
                att_body(i, False)
            att_body(NBODY - 1, True)
            inv_sums(1)
            dve.wait_ge(S["lb_in"], 2 * 16 * KC * B)
            V.tensor_tensor(cxT[:, 0, :], cxT[:, 0, :], lT[:, 0, :], ALU.mult).then_inc(S["cx_dve"], 1)
            V.tensor_tensor(cxT[:, 1, 0:T // 2], cxT[:, 1, 0:T // 2], lT[:, 1, 0:T // 2], ALU.mult) \
                .then_inc(S["cx_dve"], 1)
            batch_end(1)

            dve.wait_ge(S["lg_out"], B)
            link(V.memset(onesm[:], 1.0))

            def over_e(a):
                return a.unsqueeze(2).broadcast_to([P, TT, NE])

            def over_t(a):
                return a.unsqueeze(1).broadcast_to([P, TT, NE])

            def pick(k, src):
                link(V.tensor_reduce(m12[:, k, :], src, AX.X, ALU.max))
                link(V.tensor_tensor(lw2[:], src, over_e(m12[:, k, :]), ALU.is_equal))
                link(V.tensor_tensor(lw2[:], lw2[:], over_t(iota_m8), ALU.mult))
                link(V.tensor_reduce(rk[:, 0, k, :], lw2[:], AX.X, ALU.min))
                link(V.tensor_tensor(oh[:, k], over_t(iota_m8), over_e(rk[:, 0, k, :]), ALU.is_equal))

            pick(0, lg[:])
            link(V.scalar_tensor_tensor(lw[:].rearrange("p t e -> p (t e)"), oh[:, 0].rearrange("p t e -> p (t e)"),
                                        -3.0e38, lg[:].rearrange("p t e -> p (t e)"), ALU.mult, ALU.add))
            pick(1, lw[:])
            V.tensor_tensor(sel[:], oh[:, 0], oh[:, 1], ALU.add).then_inc(S["oh_done"], 1)
            dve.wait_ge(S["oh_done"], 1)
            link(V.tensor_tensor(lw[:], lg[:], sel[:], ALU.mult))
            link(V.tensor_scalar(lw2[:], sel[:], -1.0, 1.0e9, ALU.add, ALU.mult))
            link(V.tensor_tensor(lw[:], lw[:], lw2[:], ALU.add))
            link(V.tensor_reduce(m12[:, 2, :], lw[:], AX.X, ALU.max))
            V.tensor_tensor(lw2[:], lw[:], over_e(m12[:, 2, :]), ALU.subtract).then_inc(S["ex_in"], 1)
            dve.wait_ge(S["ex_done"], 1)
            link(V.tensor_reduce(m12[:, 2, :], lw[:], AX.X, ALU.add))
            link(V.reciprocal(m12[:, 3, :], m12[:, 2, :]))
            for k in range(2):
                link(V.tensor_tensor(lw2[:], lw[:], oh[:, k], ALU.mult))
                link(V.tensor_reduce(rk[:, 1, k, :], lw2[:], AX.X, ALU.add))
                link(V.tensor_tensor(pw[:, k, :], rk[:, 1, k, :], m12[:, 3, :], ALU.mult))
            dve.wait_ge(S["cum_mm"], 2)
            tot = bank[6].rearrange("p (t e) -> p t e", e=NE)
            link(V.memset(pf[:, 0, 0:1, :], 0.0))
            link(V.tensor_copy(pf[:, 0, 1:64, :], tot[:, 0:63, :]))
            cur = 0
            for s in (1, 2, 4, 8, 16, 32):
                link(V.tensor_copy(pf[:, 1 - cur, 0:s, :], pf[:, cur, 0:s, :]))
                link(V.tensor_tensor(pf[:, 1 - cur, s:64, :], pf[:, cur, s:64, :], pf[:, cur, 0:64 - s, :], ALU.add))
                cur = 1 - cur
            link(V.tensor_tensor(pf[:, cur], pf[:, cur], bank[5].rearrange("p (t e) -> p t e", e=NE), ALU.add))
            for k in range(2):
                link(V.tensor_tensor(lw[:], pf[:, cur, 32 * k:32 * k + 32, :], oh[:, k], ALU.mult))
                link(V.tensor_reduce(rk[:, 1, k, :], lw[:], AX.X, ALU.add))
            link(V.tensor_scalar(rk[:, 2], rk[:, 1], float(CAP), None, ALU.is_lt))
            link(V.tensor_scalar(rk[:, 0], rk[:, 0], 8.0, float(CAP), ALU.add, ALU.mult))
            link(V.tensor_tensor(rk[:, 0], rk[:, 0], rk[:, 1], ALU.add))
            link(V.tensor_tensor(pw[:], pw[:], rk[:, 2], ALU.mult))
            link(V.tensor_tensor(rk[:, 3], rk[:, 0], rk[:, 2], ALU.mult))
            link(V.tensor_copy(idx[:, 1], rk[:, 3]))
            tid = trash_id.rearrange("p (k t) -> p k t", k=2)
            link(V.tensor_tensor(rk[:, 1], rk[:, 0], tid, ALU.subtract))
            link(V.tensor_tensor(rk[:, 1], rk[:, 1], rk[:, 2], ALU.mult))
            link(V.tensor_tensor(rk[:, 1], rk[:, 1], tid, ALU.add))
            V.tensor_copy(idx[:, 0], rk[:, 1]).then_inc(S["idx_done"], 1)

            def low_parts(i, n):
                for hf in range(2):
                    dve.wait_ge(S["ht_done"], v1(i, 4 * NB, 2 * n + hf + 1))
                    V.tensor_tensor(hdp[1][:, n % 2, 4 * hf:4 * hf + 4, :], hd[:, hf],
                                    hdp[0][:, n % 2, 4 * hf:4 * hf + 4, :].bitcast(f32), ALU.subtract) \
                        .then_inc(S["hl_done"], 1)

            def xt_out(i, n):
                dve.wait_ge(S["tx_mm"], v1(i, 2 * NB, n + 1))
                if not (isinstance(i, int) and i * 2 * NB + n < 2):
                    dve.wait_ge(S["fc_mm"], v1(i, 4 * NB, 2 * (n - 1)))
                src = bank[6 + n % 2].rearrange("p (k s) -> p k s", k=KC)
                V.tensor_copy(xTp[0][:, n % 2], src).then_inc(S["xT_hi"], 1)
                dve.wait_ge(S["xT_hi"], v1(i, 2 * NB, n + 1))
                V.tensor_tensor(xTp[1][:, n % 2], src, xTp[0][:, n % 2].bitcast(f32), ALU.subtract) \
                    .then_inc(S["xT_sb"], 1)

            def y_out(i, n):
                for t in range(2):
                    dve.wait_ge(S["pj_mm"], v1(i, 4 * NB, 2 * n + t + 1))
                    if t == 0 and not (isinstance(i, int) and i * 2 * NB + n < 2):
                        dve.wait_ge(S[f"y_out{n % 2}"], v1(i, 16 * NB, 16 * (n // 2)))
                    V.tensor_copy(yb[:, n % 2, t, :], bank[4 + t][:, 0:D]).then_inc(S["y_done"], 1)

            xt_out(0, 0)

            def moe_body(i, last):
                for n in range(2 * NB):
                    low_parts(i, n)
                    if not (last and n == 2 * NB - 1):
                        xt_out(i, n + 1)
                    y_out(i, n)

            moe_body(0, False)
            with dve.Fori(1, NE // 2 - 1) as i:
                moe_body(i, False)
            moe_body(NE // 2 - 1, True)

            for t in range(TT):
                b = t // (TT // B)
                dve.wait_ge(S[f"g_in{t % 4}"], 32 * (t // 4 + 1))
                g = ga_[:, t % 4]
                link(V.tensor_scalar(t3 := g[:, 0, :], g[:, 0, :], pw[:, 0, t:t + 1], None, ALU.mult))
                link(V.scalar_tensor_tensor(g[:, 1, :], g[:, 1, :], pw[:, 1, t:t + 1], g[:, 0, :], ALU.mult, ALU.add))
                link(V.tensor_tensor(g[:, 0, :], g[:, 1, :], bc[:, GB, b], ALU.mult))
                V.tensor_tensor(xs[:, t, :], xs[:, t, :], g[:, 0, :], ALU.add).then_inc(S["comb"], 1)

        @block.scalar
        def _(act):
            A = nc.scalar
            act.wait_ge(S["c_in"], 48)
            A.activation(sl[:, 0], cT[:], ACT.Exp, scale=-1.0).then_inc(S["sil_exp"], 1)
            act.wait_ge(S["std_in"], 1)
            A.activation(std[:], std[:], ACT.Sqrt).then_inc(S["std_out"], 1)

            for g in range(8 + 1):
                if g < 8:
                    b = g // 4
                    for k in range(KC):
                        act.wait_ge(S["xT_mm"], 2 * g + k + 1)
                        if g >= 2:
                            act.wait_ge(S["v_mm"], g - 1)
                        if g == 0:
                            act.wait_ge(S["mod_done"], 1)
                        A.activation(hT[:, g % 2, k, :], bank[k], ACT.Identity, scale=modc[:, 1, k, b:b + 1],
                                     bias=modc[:, 0, k, b:b + 1]).then_inc(S["hT_done"], 1)
                if g >= 1:
                    m = g - 1
                    act.wait_ge(S["v_mm"], m + 1)
                    b, k0 = m // 4, m % 4 * 4
                    if m == 0:
                        act.wait_ge(S["v_one"], 4)
                    for j in range(2):
                        src = bank[6 + j].rearrange("p (t h d) -> p t h d", t=2, h=H)
                        for t in range(2):
                            A.activation(vall[:, b * H:(b + 1) * H, k0 + 2 * j + t, 0:DH], src[:, t],
                                         ACT.Copy).then_inc(S["v_used"], 1)
                    act.wait_ge(S["r_done"], m + 1)
                    if m >= 2:
                        act.wait_ge(S[f"parts_out{m % 2}"], 12 * 16 * (m // 2))
                    if m == 0:
                        act.wait_ge(S["bc_mm"], 4)
                    A.activation(parts[:, m % 2, 0], rq[:, m % 2], ACT.Copy).then_inc(S["hi_done"], 1)
                    act.wait_ge(S["mid_in"], m + 1)
                    A.activation(parts[:, m % 2, 1], rq[:, m % 2], ACT.Copy).then_inc(S["mid_done"], 1)
                    act.wait_ge(S["lo_in"], m + 1)
                    A.activation(parts[:, m % 2, 2], rq[:, m % 2], ACT.Copy).then_inc(S["lo_done"], 1)

            def exp_step(i, c_):
                act.wait_ge(S["st_mm"], v1(i, 64, c_ + 1))
                if not (isinstance(i, int) and i == 0 and c_ < 4):
                    act.wait_ge(S["pv_mm"], v1(i, 32, c_ // 2 - 1))
                s = c_ % 2
                A.activation(pr[:, c_ % 4, :], ps[:, 2 * s:2 * s + 2, :].rearrange("p a n -> p (a n)"), ACT.Exp,
                             scale=0.25).then_inc(S["p_done"], 1)

            def att_body(i, last, split=False):
                for u in range(4):
                    for k in range(NKT):
                        if not ((last or split) and u == 3 and k >= NKT - 2):
                            exp_step(i, NKT * u + k + 2)
                    act.wait_ge(S["pv_mm"], v1(i, 32, NKT // 2 * (u + 1)))
                    if not (isinstance(i, int) and i == 0 and u == 0):
                        act.wait_ge(S[f"oout{(u + 1) % 2}"], v1(i, 128, 64 * ((u + 1) // 2)))
                    A.activation(osb[:], bank[7], ACT.Copy).then_inc(S["o_done"], 1)

            def batch_end(b):
                n0 = TB * b
                act.wait_ge(S["std_in"], 2 + b)
                A.activation(std[:, n0:n0 + TB], std[:, n0:n0 + TB], ACT.Sqrt).then_inc(S["std_out"], 1)
                for t in range(n0, n0 + TB):
                    act.wait_ge(S["h2T_mm"], t + 1)
                    if t >= 2:
                        act.wait_ge(S["lg_mm"], t - 1)
                    A.activation(h2T[:, t % 2], bank[4 + t % 2][:, 0:D].rearrange("p (k n) -> p k n", k=KC),
                                 ACT.Copy).then_inc(S["h2T_done"], 1)

            act.wait_ge(S["zero_out"], 16 * (TRASH // P * D // 512))
            exp_step(0, 0)
            exp_step(0, 1)
            att_body(0, False)
            with act.Fori(1, SPLIT) as i:
                att_body(i, False)
            att_body(SPLIT, False, split=True)
            batch_end(0)
            exp_step(SPLIT + 1, 0)
            exp_step(SPLIT + 1, 1)
            with act.Fori(SPLIT + 1, NBODY - 1) as i:
                att_body(i, False)
            att_body(NBODY - 1, True)
            batch_end(1)
            act.wait_ge(S["ex_in"], 1)
            A.activation(lw[:], lw2[:], ACT.Exp).then_inc(S["ex_done"], 1)

            def gelu(i, n):
                for hf in range(2):
                    act.wait_ge(S["fc_mm"], v1(i, 4 * NB, 2 * n + hf + 1))
                    if hf == 0 and not (isinstance(i, int) and i * 2 * NB + n < 2):
                        act.wait_ge(S["pj_mm"], v1(i, 4 * NB, 2 * (n - 1)))
                    src = ps[:, 2 * hf:2 * hf + 2, :].rearrange("p a n -> p (a n)")
                    A.activation(hdp[0][:, n % 2, 4 * hf:4 * hf + 4, :].rearrange("p m s -> p (m s)"), src,
                                 ACT.Gelu).then_inc(S["hh_done"], 1)
                    if not (isinstance(i, int) and i * 2 * NB + n < 1):
                        act.wait_ge(S["hl_done"], v1(i, 4 * NB, 2 * (n - 1) + hf + 1))
                    act.wait_ge(S["hh_done"], v1(i, 4 * NB, 2 * n + hf + 1))
                    A.activation(hd[:, hf].rearrange("p m s -> p (m s)"), src, ACT.Gelu).then_inc(S["ht_done"], 1)

            for n in range(2 * NB):
                gelu(0, n)
            with act.Fori(1, NE // 2) as i:
                for n in range(2 * NB):
                    gelu(i, n)

        @block.gpsimd
        def _(pool):
            G = nc.gpsimd
            for g in range(8):
                pool.wait_ge(S["hi_done"], g + 1)
                G.tensor_tensor(rq[:, g % 2], rq[:, g % 2], parts[:, g % 2, 0], ALU.subtract).then_inc(S["mid_in"], 1)
                pool.wait_ge(S["mid_done"], g + 1)
                G.tensor_tensor(rq[:, g % 2], rq[:, g % 2], parts[:, g % 2, 1], ALU.subtract).then_inc(S["lo_in"], 1)

            def split_max(i, count, par):
                if not (isinstance(i, int) and i == 0 and count <= 2):
                    pool.wait_ge(S["mxfree"], turned(i, count - 3))
                pool.wait_ge(S["nm_done"], v1(i, 4, count))
                chn = lambda ins, k: (ins.then_inc(S["pch"], 1), pool.wait_ge(S["pch"], v1(i, 16, 4 * (count - 1) + k)))
                chn(G.tensor_tensor(nmp[:, par, 0], nm[:, par], nil[:], ALU.add), 1)
                chn(G.tensor_tensor(nmr[:, par, 0], nm[:, par], nmp[:, par, 0], ALU.subtract), 2)
                chn(G.tensor_tensor(nmp[:, par, 1], nmr[:, par, 0], nil[:], ALU.add), 3)
                chn(G.tensor_tensor(nmr[:, par, 1], nmr[:, par, 0], nmp[:, par, 1], ALU.subtract), 4)
                G.tensor_tensor(nmp[:, par, 2], nmr[:, par, 1], nil[:], ALU.add).then_inc(S["nmp_done"], 1)

            def stage_values(i, n, head):
                G.tensor_copy(vst[:, n, :, 0:DH + 1], vall[:, head]).then_inc(S["vst_done"], 1)

            pool.wait_ge(S["v_used"], 32)
            pool.wait_ge(S["v_one"], 4)
            stage_values(0, 0, 0)
            split_max(0, 1, 0)
            split_max(0, 2, 1)

            def att_body(i, last):
                for n in range(2):
                    if not (last and n == 1):
                        if not (isinstance(i, int) and i == 0 and n == 0):
                            pool.wait_ge(S["pv_mm"], v1(i, 32, 16 * n))
                        stage_values(i, 1 - n, i * 2 + (n + 1))
                    for half in range(2):
                        if (not last or n == 0) and not (isinstance(i, int) and i == SPLIT and n + half == 2):
                            split_max(i, 2 * n + half + 3, half)
                        if isinstance(i, int) and i == SPLIT:
                            if n == 0 and half == 0:
                                load_sums(0)
                            elif n == 0:
                                load_outputs(0)
                            else:
                                normalise(0, n - 1 + half, range(4))

            def load_sums(b):
                for half in range(2):
                    pool.wait_ge(S[f"oout{half}"], (b + 1) * H * 4 * 16)
                for half in range(2):
                    if half:
                        pool.wait_ge(S["l_in"], 32 * b + 16)
                    pool.dma_start(ls[:], os_[half, b * H:(b + 1) * H, DH, :],
                                   accum_op=ALU.add if half else ALU.bypass).then_inc(S["l_in"], 16)

            def load_outputs(b):
                pool.wait_ge(S["l_rec"], b + 1)
                pool.dma_start(linv[b * H:(b + 1) * H, :], ls[:]).then_inc(S["l_out"], 16)
                pool.wait_ge(S["l_out"], 16 * (b + 1))
                if b:
                    pool.wait_ge(S["wo_mm"], TB * b)
                for k in range(KC):
                    h0 = b * H + 8 * k
                    pool.dma_start(cxT[:, k, :], os_[0, h0:h0 + 8, 0:DH, :]).then_inc(S["cx_in"], 16)
                pool.wait_ge(S["cx_in"], 16 * KC * (b + 1))
                for k in range(KC):
                    h0 = b * H + 8 * k
                    pool.dma_start(cxT[:, k, :], os_[1, h0:h0 + 8, 0:DH, :], accum_op=ALU.add).then_inc(S["lb_in"], 16)
                    pool.dma_start(lT[:, k, :], linv[h0:h0 + 8, :].unsqueeze(1).broadcast_to([8, DH, T])) \
                        .then_inc(S["lb_in"], 16)

            def normalise(b, k, quarters):
                pool.wait_ge(S["lb_in"], 2 * 16 * KC * (b + 1))
                for q in quarters:
                    part = slice(512 * q, 512 * q + 512)
                    G.tensor_tensor(cxT[:, k, part], cxT[:, k, part], lT[:, k, part], ALU.mult) \
                        .then_inc(S["cx_pool"], 1)

            def batch_end(b):
                for t in range(TB * b + 1, TB * b + TB, 2):
                    pool.wait_ge(S["xn2_done"], t + 1)
                    y = t2[:, 1]
                    G.tensor_tensor(y[:, 1, :], y[:, 0, :], bc[:, CB, b], ALU.mult).then_inc(S["ach"], 1)
                    pool.wait_ge(S["ach"], t // 2 + 1)
                    G.tensor_tensor(h2[:, t, :], y[:, 1, :], bc[:, SB, b], ALU.add).then_inc(S["h2_pool"], 1)

            w1v = cfc.rearrange("e (k p) n -> e p k n", p=P)
            w2v = cproj.rearrange("e (k p) n -> e p k n", p=P)

            def load_weights(e):
                if e:
                    pool.wait_ge(S["wt_done"], 2 * e)
                pool.dma_start(stg[:, 0, :].rearrange("p (k n) -> p k n", k=KC), w1v[e]).then_inc(S["wt_in"], 16)
                pool.dma_start(stg[:, 1, :].rearrange("p (k n) -> p k n", n=D), w2v[e]).then_inc(S["wt_in"], 16)

            def split_weights(e):
                pool.wait_ge(S["wt_in"], 32 * (e + 1))
                if e >= 2:
                    pool.wait_ge(S["pj_mm"], 2 * NB * (e - 1))
                for j, w in enumerate((w1p, w2p)):
                    hi, lo = (w[c_][:, e % 2].rearrange("p k n -> p (k n)") for c_ in range(2))
                    G.tensor_copy(hi, stg[:, j, :]).then_inc(S["wt_hi"], 1)
                    pool.wait_ge(S["wt_hi"], 2 * e + j + 1)
                    G.tensor_tensor(lo, stg[:, j, :], hi.bitcast(f32), ALU.subtract).then_inc(S["wt_done"], 1)

            att_body(0, False)
            with pool.Fori(1, SPLIT) as i:
                att_body(i, False)
            att_body(SPLIT, False)
            batch_end(0)
            split_max(SPLIT, 6, 1)
            with pool.Fori(SPLIT + 1, NBODY - 1) as i:
                att_body(i, False)
            att_body(NBODY - 1, True)
            load_sums(1)
            load_outputs(1)
            normalise(1, 1, range(2, 4))
            pool.wait_ge(S["o_done"], 2 * BH)
            pool.wait_ge(S["lb_in"], 2 * 16 * KC * B)
            load_weights(0)
            batch_end(1)
            split_weights(0)
            load_weights(1)
            split_weights(1)

            pool.wait_ge(S["idx_done"], 1)
            pool.wait_ge(S["zero_out"], 16 * (TRASH // P * D // 512))
            for t in range(TT):
                for k in range(2):
                    pool.indirect_dma_start(out=xe, out_offset=bass.IndirectOffsetOnAxis(ap=idx[:, 0, k, t:t + 1], axis=0),
                                            in_=h2[:, t, :], in_offset=None).then_inc(S["slots_in"], 16)
            for e in range(2, NE):
                load_weights(e)
                split_weights(e)
            for par in range(2):
                pool.wait_ge(S[f"y_out{par}"], NE * NB // 2 * 16)
            for t in range(TT):
                if t >= 4:
                    pool.wait_ge(S["comb"], t - 3)
                for k in range(2):
                    pool.indirect_dma_start(out=ga_[:, t % 4, k, :], out_offset=None, in_=ye,
                                            in_offset=bass.IndirectOffsetOnAxis(ap=idx[:, 1, k, t:t + 1], axis=0)) \
                        .then_inc(S[f"g_in{t % 4}"], 16)

        @block.tensor
        def _(pe):
            M = nc.tensor.matmul
            pe.wait_ge(S["c_in"], 48)
            pe.wait_ge(S["sil_rep"], 1)
            for j, src in ((0, 0), (1, 1)):
                for f in range(KC):
                    o = bank[0][:, (j * KC + f) * B:(j * KC + f) * B + B]
                    for k in range(KC):
                        m = M(o, wm[:, k, src * D + f * P:src * D + f * P + P], sl[:, 0, k, :],
                              start=(k == 0), stop=(k == KC - 1))
            m.then_inc(S["modc_mm"], 1)
            for j, src in ((GA, 2), (GB, 5), (CB, 4), (SB, 3)):
                for b in range(B):
                    for k in range(KC):
                        m = M(bank[1 + j][:, D * b:D * b + D], rep[:, k, b, :], wm[:, k, src * D:src * D + D],
                              start=(k == 0), stop=(k == KC - 1))
                m.then_inc(S["bc_mm"], 1)
            pe.wait_ge(S["bo_done"], 1)
            for k in range(KC):
                m = M(bank[5][:, 0:D], rep[:, k, 0, :], wo_s[:, k, :], start=(k == 0), stop=(k == KC - 1))
            m.then_inc(S["bo_mm"], 1)
            pe.wait_ge(S["mod_done"], 1)
            pe.wait_ge(S["w_in"], 128)
            for g in range(8):
                pe.wait_ge(S["xn_done"], 4 * g + 4)
                for k in range(KC):
                    if g >= 1:
                        pe.wait_ge(S["hT_done"], 2 * (g - 1) + k + 1)
                    for t in range(4):
                        m = nc.tensor.transpose(bank[k][:, P * t:P * t + P], xn[:, g % 2, t, P * k:P * k + P], ident)
                    m.then_inc(S["xT_mm"], 1)
                pe.wait_ge(S["hT_done"], 2 * g + 2)
                for s in range(2):
                    if g >= 1:
                        pe.wait_ge(S["qk_used"], 2 * (g - 1) + s + 1)
                    for ab in range(2):
                        for k in range(KC):
                            m = M(bank[2 + 2 * s + ab], wqk_s[:, k, 2 * s + ab, :], hT[:, g % 2, k, :],
                                  start=(k == 0), stop=(k == KC - 1))
                    m.then_inc(S["qk_mm"], 1)
                if g >= 1:
                    pe.wait_ge(S["v_used"], 4 * g)
                for t in range(4):
                    for k in range(KC):
                        m = M(bank[6 + t // 2][:, D * (t % 2):D * (t % 2) + D], hT[:, g % 2, k, P * t:P * t + P],
                              wv_s[:, k, :], start=(k == 0), stop=(k == KC - 1))
                m.then_inc(S["v_mm"], 1)

            def score(i, par, item, q, kq, free):
                if free:
                    pe.wait_ge(S["mxfree"], v1(i, 4 * PU, item - 2))
                M(bank[4 + item % 3], qmx[:, par, P * q:P * q + P], kmx[:, par, 512 * kq:512 * kq + 512],
                  start=True, stop=True).then_inc(S["item"], 1)

            def turn(i, item, par, count):
                pe.wait_ge(S["nmp_done"], v1(i, 4, count))
                pe.wait_ge(S["mxfree"], v1(i, 4 * PU, item - 2))
                nc.tensor.transpose(bank[4 + item % 3].bitcast(bf16)[0:3 * QT, 0:P],
                                    nmp[:, par].rearrange("p c t -> p (c t)"), identb[:]).then_inc(S["item"], 1)

            def scoresT(i, c_):
                n, half, k = c_ // 32 % 2, c_ // NKT % 2, c_ % NKT
                if not (isinstance(i, int) and i == 0 and c_ < 2):
                    pe.wait_ge(S["p_done"], v1(i, 64, c_ - 1))
                s = c_ % 2
                for j in range(2):
                    q0 = UQ * half + 512 * j
                    m = M(bank[2 * s + j], kex[:, n, P * k:P * k + P], qex[:, n, q0:q0 + 512], start=True, stop=True)
                m.then_inc(S["st_mm"], 1)

            def unit_ready(i, c_):
                n, half = c_ // 32 % 2, c_ // NKT % 2
                if half == 0:
                    pe.wait_ge(S[f"exld{n}"], v1(i, 96, 96 * (c_ // 64 + 1)))
                pe.wait_ge(S[f"shift{half}"], v1(i, 32, 16 * (c_ // 32 + 1)))

            def weigh(i, c_):
                n, unit, k = c_ // 32 % 2, c_ // NKT, c_ % NKT
                pe.wait_ge(S["p_done"], v1(i, 64, c_ + 2))
                if k == 0 and not (isinstance(i, int) and i == 0 and unit == 0):
                    pe.wait_ge(S["o_done"], v1(i, 4, unit))
                if k == 0 and unit % 2 == 0:
                    pe.wait_ge(S["vst_done"], v1(i, 2, n + 1))
                for g in range(4):
                    odd, q0 = g // 2, 512 * (g % 2)
                    m = M(bank[7][32 * g:32 * g + VW, :], vst[:, n, k + odd, :], pr[:, (c_ + odd) % 4, q0:q0 + 512],
                          start=(k == 0), stop=(k == NKT - 2), tile_position=(0, 32 * g))
                m.then_inc(S["pv_mm"], 1)

            pe.wait_ge(S["mxld0"], 96)
            pe.wait_ge(S["idb"], 1)
            pe.wait_ge(S["r_done"], 8)
            for k in range(32):
                score(0, 0, k, k // 4, k % 4, k >= 3)
            turn(0, 32, 0, 1)
            for k in range(32):
                score(0, 0, 33 + k, QT + k // 4, k % 4, True)
            unit_ready(0, 0)
            pe.wait_ge(S["v_one"], 4)
            pe.wait_ge(S["v_used"], 32)
            scoresT(0, 0)
            scoresT(0, 1)

            def att_body(i, last):
                for u in range(4):
                    n, half = u // 2, u % 2
                    quiet = last and u >= 2
                    base = PRO + PU * u
                    for k in range(0, NKT, 2):
                        c_ = NKT * u + k

                        def maxima(m):
                            if not quiet:
                                score(i, 1 - n, base + m + (m >= 10), QT * half + m // 4, m % 4, True)

                        if not quiet and k == 0 and half == 0:
                            pe.wait_ge(S[f"mxld{1 - n}"], v1(i, 96, 96 * (n + 1)))
                        more = not (last and c_ == 62)
                        if more:
                            if k == NKT - 2:
                                unit_ready(i, c_ + 2)
                            scoresT(i, c_ + 2)
                        maxima(2 * k)
                        maxima(2 * k + 1)
                        if k == 4 and not (last and u == 3):
                            turn(i, base + (0 if quiet else 10), (u + 1) % 2, u + 2)
                        if more:
                            scoresT(i, c_ + 3)
                        maxima(2 * k + 2)
                        weigh(i, c_)
                        maxima(2 * k + 3)

            def logits(t):
                pe.wait_ge(S["h2T_done"], t + 1)
                for k in range(KC):
                    m = M(bank[6][:, NE * (t % TB):NE * (t % TB) + NE], h2T[:, t % 2, k, :], wg_s[:, k, :],
                          start=(k == 0), stop=(k == KC - 1))
                m.then_inc(S["lg_mm"], 1)

            def batch_end(b):
                n0 = TB * b
                items = PRO + PU * 4 * (SPLIT + 1) if b == 0 else PRO + PU * (2 * BH - 2) + 1
                pe.wait_ge(S["mxfree"], items)
                pe.wait_ge(S["cx_pool"], 8 + 2 * b)
                if b:
                    pe.wait_ge(S["cx_dve"], 2)
                for t in range(n0, n0 + TB):
                    if t >= n0 + 2:
                        pe.wait_ge(S["x1_done"], t - 1)
                    for k in range(KC):
                        m = M(bank[4 + t % 2][:, 0:D], cxT[:, k, P * (t - n0):P * (t - n0) + P], wo_s[:, k, :],
                              start=(k == 0), stop=(k == KC - 1))
                    m.then_inc(S["wo_mm"], 1)
                for t in range(n0, n0 + TB):
                    pe.wait_ge(S["h2_pool" if t % 2 else "h2_dve"], t // 2 + 1)
                    pe.wait_ge(*((S["h2T_done"], t - 1) if t >= n0 + 2 else (S["x1_done"], n0 + TB)))
                    for k in range(KC):
                        m = nc.tensor.transpose(bank[4 + t % 2][:, P * k:P * k + P], h2[:, t, P * k:P * k + P],
                                                ident)
                    m.then_inc(S["h2T_mm"], 1)
                    if t > n0:
                        logits(t - 1)
                logits(n0 + TB - 1)
                pe.wait_ge(S["lg_out"], b + 1)

            att_body(0, False)
            with pe.Fori(1, SPLIT) as i:
                att_body(i, False)
            att_body(SPLIT, False)
            batch_end(0)
            with pe.Fori(SPLIT + 1, NBODY - 1) as i:
                att_body(i, False)
            att_body(NBODY - 1, True)
            batch_end(1)
            pe.wait_ge(S["oh_done"], 1)
            ohf = oh[:].rearrange("p k t e -> p (k t e)")
            M(bank[5], tri, ohf, start=True, stop=True).then_inc(S["cum_mm"], 1)
            M(bank[6], onesm[:], ohf, start=True, stop=True).then_inc(S["cum_mm"], 1)

            def turn_rows(i, n):
                pe.wait_ge(S[f"xr_in{n % 2}"], v1(i, 16 * NB, 16 * (n // 2 + 1)))
                if not (isinstance(i, int) and i * 2 * NB + n < 2):
                    pe.wait_ge(S["xT_sb"], v1(i, 2 * NB, n - 1))
                for k in range(KC):
                    for t in range(2):
                        m = nc.tensor.transpose(bank[6 + n % 2][:, BLK * k + P * t:BLK * k + P * t + P],
                                                xr[:, n % 2, t, P * k:P * k + P], ident)
                m.then_inc(S["tx_mm"], 1)

            pe.wait_ge(S["idx_done"], 1)
            turn_rows(0, 0)

            PAIRS = ((0, 0), (0, 1), (1, 0))

            def moe_body(i, last):
                for e in range(2):
                    for b in range(NB):
                        n = e * NB + b
                        if b == 0:
                            pe.wait_ge(S["wt_done"], v1(i, 4, 2 * e + 2))
                        pe.wait_ge(S["xT_sb"], v1(i, 2 * NB, n + 1))
                        for hf in range(2):
                            if not (isinstance(i, int) and i == 0 and n == 0):
                                pe.wait_ge(S["ht_done"], v1(i, 4 * NB, 2 * (n - 1) + hf + 1))
                            for mm in range(4):
                                f = 4 * hf + mm
                                o = ps[:, 2 * hf + mm // 2, BLK * (mm % 2):BLK * (mm % 2) + BLK]
                                for k in range(KC):
                                    for q, (wp, xp) in enumerate(PAIRS):
                                        m = M(o, w1p[wp][:, e, k, P * f:P * f + P], xTp[xp][:, n % 2, k, :],
                                              start=(k + q == 0), stop=(k == KC - 1 and q == 2))
                            m.then_inc(S["fc_mm"], 1)
                        if not (last and n == 2 * NB - 1):
                            turn_rows(i, n + 1)
                        for hf in range(2):
                            for t in range(2):
                                if hf == 0 and not (isinstance(i, int) and i == 0 and n == 0):
                                    pe.wait_ge(S["y_done"], v1(i, 4 * NB, 2 * (n - 1) + t + 1))
                                if t == 0:
                                    pe.wait_ge(S["hl_done"], v1(i, 4 * NB, 2 * n + hf + 1))
                                for f in range(4 * hf, 4 * hf + 4):
                                    for q, (hp, wp) in enumerate(PAIRS):
                                        m = M(bank[4 + t][:, 0:D], hdp[hp][:, n % 2, f, P * t:P * t + P],
                                              w2p[wp][:, e, f, :], start=(f + q == 0),
                                              stop=(f == HID // P - 1 and q == 2))
                                if hf == 1:
                                    m.then_inc(S["pj_mm"], 1)

            moe_body(0, False)
            with pe.Fori(1, NE // 2 - 1) as i:
                moe_body(i, False)
            moe_body(NE // 2 - 1, True)


_ORDER = ["x", "wqk", "bqk", "wv", "bv", "wo", "bo", "wg", "cfc", "cproj", "c", "wmod", "trig", "consts"]


def kernel(L0_attn_x, L0_attn_Wq, L0_attn_bq, L0_attn_Wk, L0_attn_bk, L0_attn_Wv, L0_attn_bv, L0_attn_Wo,
           L0_attn_bo, L0_ffn_w_g, L0_ffn_c_fc, L0_ffn_c_proj, L0_c, L0_wmod):
    import concourse.bacc as bacc
    from concourse.bass_utils import run_bass_kernel_spmd

    order = np.arange(D).reshape(H, 2, DH // 2).transpose(1, 0, 2).reshape(2, P)
    wq, wk = np.asarray(L0_attn_Wq)[:, order], np.asarray(L0_attn_Wk)[:, order]
    bq, bk = np.asarray(L0_attn_bq)[order], np.asarray(L0_attn_bk)[order]
    f = np.arange(DH // 2, dtype=np.float32)
    inv = (np.float32(1.0) / np.float32(10000.0) ** (f / np.float32(DH // 2))).astype(np.float32)
    ang = np.tile((np.arange(T, dtype=np.float32)[:, None] * inv[None]).T, (H, 1))
    consts = np.zeros((P, 336), np.float32)
    consts[:, 0:128] = np.eye(P)
    consts[:, 128:256] = np.triu(np.ones((P, P)), 1)
    consts[:, 256:264] = np.arange(NE) - 8
    consts[:, 264:272] = np.arange(NE)
    consts[:, 272:336] = (TRASH + np.arange(2)[None, :, None] * N + np.arange(TT)[None, None] * P
                          + np.arange(P)[:, None, None]).reshape(P, 2 * TT)
    arrays = {
        "x": np.asarray(L0_attn_x), "wqk": np.stack([wq[:, 0], wq[:, 1], wk[:, 0], wk[:, 1]], 1),
        "bqk": np.stack([bq[0], bq[1], bk[0], bk[1]], 1), "wv": np.asarray(L0_attn_Wv),
        "bv": np.asarray(L0_attn_bv).reshape(KC, P).T, "wo": np.asarray(L0_attn_Wo), "bo": np.asarray(L0_attn_bo),
        "wg": np.asarray(L0_ffn_w_g), "cfc": np.asarray(L0_ffn_c_fc), "cproj": np.asarray(L0_ffn_c_proj),
        "c": np.asarray(L0_c).T.reshape(KC, P, B).transpose(1, 0, 2), "wmod": np.asarray(L0_wmod),
        "trig": np.stack([np.cos(ang), np.sin(ang)], 1).astype(np.float32), "consts": consts,
    }
    arrays = {k: np.ascontiguousarray(v) for k, v in arrays.items()}
    nc = bacc.Bacc("TRN2", target_bir_lowering=False, num_devices=1)
    args = [nc.dram_tensor(k, arrays[k].shape, mybir.dt.from_np(arrays[k].dtype), kind="ExternalInput").ap()
            for k in _ORDER]
    out = nc.dram_tensor("out", (B, T, D), mybir.dt.float32, kind="ExternalOutput").ap()
    adaln_block(nc, *args, out)
    r = run_bass_kernel_spmd(nc, [arrays], core_ids=[0])
    return r.results[0]["out"]
```

```python
from contextlib import ExitStack

import numpy as np

import concourse.bass as bass
from concourse import mybir

B, T, D = 2, 2048, 256
N = B * T
H, DH = 16, 16
BH = B * H
NE, HID = 8, 1024
P = 128
TT = N // P
KC = D // P
CAP = int(2 * 1.25 * N / NE)
CAP += CAP % 2
SLOTS = NE * CAP
BLK = 256
NB = CAP // BLK
assert NB * BLK == CAP
PAIRS_AT = SLOTS + BLK
EMPTY_AT = PAIRS_AT + 2 * N
XROWS = EMPTY_AT + SLOTS
RW = D + 1
EPS = 1e-5

QT = 8
UQ = QT * P
NKT = T // P
VW = 32
KS = 6 * DH
PRO = 65
PU = 33


def adaln_block(nc, x, wqk, bqk, wv, bv, wo, bo, wg, cfc, cproj, c, wmod, trig, consts, out):
    f32, bf16, i32, f32r = mybir.dt.float32, mybir.dt.bfloat16, mybir.dt.int32, mybir.dt.float32r
    ALU, ACT, AX = mybir.AluOpType, mybir.ActivationFunctionType, mybir.AxisListType

    qs = nc.dram_tensor("q_parts", [BH, 3 * DH, T], bf16, kind="Internal").ap()
    ks = nc.dram_tensor("k_parts", [BH, 3 * DH, T], bf16, kind="Internal").ap()
    os_ = nc.dram_tensor("o_heads", [2, BH, DH + 1, T], f32, kind="Internal").ap()
    linv = nc.dram_tensor("inv_sums", [BH, T], f32, kind="Internal").ap()
    xe = nc.dram_tensor("rows", [XROWS, RW], f32, kind="Internal").ap()

    ctx = ExitStack()
    with ctx:
        def sb(name, shape, dt=f32, stack=ctx):
            return stack.enter_context(nc.sbuf_tensor(name, shape, dt))

        def sem(name):
            return ctx.enter_context(nc.semaphore(name))

        xs = sb("xs", [P, TT, D])
        cst = sb("cst", [P, 330])
        ident, tri = cst[:, 0:128], cst[:, 128:256]
        iota_m8 = cst[:, 256:264]
        pair_row = cst[:, 264:328].rearrange("p (k t) -> p k t", k=2)
        slot_row = cst[:, 328:330]
        identb = sb("identb", [P, P], bf16)
        bc = sb("bc", [P, 4, B, D])
        GA, GB, CB, SB = range(4)
        bob = sb("bob", [P, D])
        wo_s = sb("wo_s", [P, KC, D])
        wg_s = sb("wg_s", [P, KC, NE])
        bv_s = sb("bv_s", [P, KC])
        modc = sb("modc", [P, 4, KC, B])
        stats = sb("stats", [P, TT, 6])
        mv = sb("mv", [P, TT, 2])
        std = sb("std", [P, TT])
        rstd = sb("rstd", [P, TT])
        lg = sb("lg", [P, TT, NE])
        pw = sb("pw", [P, 2, TT])
        idx = sb("idx", [P, 2, TT], i32)

        att = ExitStack()
        vall = sb("vall", [P, BH, NKT, DH + 1], stack=att)
        stk = sb("stk", [P, 4, T], bf16, att)
        qmx, kmx = stk[0:KS, 0:2, :], stk[0:KS, 2:4, :]
        qex = sb("qex", [KS + 3, 2, T], bf16, att)
        kex = sb("kex", [KS + 3, 2, T], bf16, att)
        vst = sb("vst", [P, 2, NKT, VW], stack=att)
        pr = sb("pr", [P, 4, UQ], stack=att)
        osb = sb("osb", [P, 2 * RW], stack=att)
        zero = osb[:]
        mxp = sb("mxp", [P, 2, QT, 4], stack=att)
        nm = sb("nm", [P, 2, QT], stack=att)
        nmr = sb("nmr", [P, 2, 2, QT], stack=att)
        nil = sb("nil", [P, QT], stack=att)
        nmp = sb("nmp", [P, 2, 3, QT], bf16, att)
        nms = sb("nms", [3 * QT, 2, P], bf16, att)

        pre = ExitStack()
        wqk_s = sb("wqk_s", [P, KC, 4, P], stack=pre)
        bqk_s = sb("bqk_s", [P, 4], stack=pre)
        wv_s = sb("wv_s", [P, KC, D], stack=pre)
        trg = sb("trg", [P, 2, T], stack=pre)
        cT = sb("cT", [P, KC, B], stack=pre)
        sl = sb("sl", [P, 3, KC, B], stack=pre)
        hT = sb("hT", [P, 2, KC, 512], stack=pre)
        rq = sb("rq", [P, 2, 4, 512], stack=pre)
        gts = pr[:, 0, 0:2 * D].rearrange("p (a d) -> p a d", a=2)
        tq = pr[:, 0:2, :].rearrange("p a n -> p (a n)").rearrange("p (a n) -> p a n", a=4)
        xn = pr[:, 2:4, :].rearrange("p r (t d) -> p r t d", t=4)
        parts = sb("parts", [P, 2, 3, 4, 512], bf16, pre)
        rep = parts[:, 0, 0, :, :].rearrange("p s n -> p (s n)").bitcast(f32) \
            .rearrange("p (k b n) -> p k b n", k=KC, b=B)[:, :, :, 0:P]
        wm = stk[:].rearrange("p a n -> p (a n)").bitcast(f32)[:, 0:KC * 6 * D].rearrange("p (k n) -> p k n", k=KC)
        pre.close()

        epi = ExitStack()
        h2 = sb("h2", [P, TT, RW], stack=epi)
        h2T = sb("h2T", [P, 2, KC, P], stack=epi)
        wog = sb("wog", [P, KC, D], stack=epi)
        gbo = sb("gbo", [P, D], stack=epi)
        ls = sb("ls", [P, 256], stack=epi)
        cxT = sb("cxT", [P, KC, T], stack=epi)
        lT = sb("lT", [P, KC, T], stack=epi)
        epi.close()
        att.close()

        moe = ExitStack()
        stg = sb("stg", [P, 2, HID * KC], stack=moe)
        w1p = [sb(f"w1{c_}", [P, 2, KC, HID], f32r, moe) for c_ in "hl"]
        w2p = [sb(f"w2{c_}", [P, 2, HID // P, D], f32r, moe) for c_ in "hl"]
        sb("clear", [P, 2048], stack=moe)
        xTp = [sb(f"xT{c_}", [P, 2, KC, BLK], f32r, moe) for c_ in "hl"]
        hd = sb("hd", [P, 2, 4, BLK], stack=moe)
        hdp = [sb(f"hd{c_}", [P, 2, HID // P, BLK], f32r, moe) for c_ in "hl"]
        xr = sb("xr", [P, 2, 2, RW], stack=moe)
        yb = sb("yb", [P, 2, 2, RW], stack=moe)
        er = sb("er", [P, 2, 2], stack=moe)
        tgt = sb("tgt", [P, 2, 2], i32, moe)
        moe.close()
        fin = ExitStack()
        yp = sb("yp", [P, TT // 4, 2, 4, D], stack=fin)
        fin.close()
        rt = ExitStack()
        sb("hold", [P, BH * NKT * (DH + 1)], stack=rt)
        oh = sb("oh", [P, B, 2, TT // B, NE], stack=rt)
        lw = sb("lw", [P, B, TT // B, NE], stack=rt)
        lw2 = sb("lw2", [P, B, TT // B, NE], stack=rt)
        sel = sb("sel", [P, B, TT // B, NE], stack=rt)
        m12 = sb("m12", [P, 2, B, TT // B], stack=rt)
        rk = sb("rk", [P, 6, 2, TT // B], stack=rt)
        lim = sb("lim", [P, TT // B], stack=rt)
        pf = sb("pf", [P, 2, 2, TT // B + 1, NE], stack=rt)
        base = sb("base", [P, 2, NE], stack=rt)
        first0 = sb("first0", [P, NE], stack=rt)
        onesm = sb("onesm", [P, P], stack=rt)
        rt.close()

        ps = ctx.enter_context(nc.psum_tensor("ps", [P, 8, 512], f32))
        bank = [ps[:, b, :] for b in range(8)]

        names = """c_in wmod_in w_in x_in0 x_in1 x_in2 x_in3 zero_set zero_out v_one sil_exp sil_rep modc_mm
            modc_set bc_mm dve_step pool_step h2_step std_in std_out xn_done xT_mm hT_done qk_mm
            qk_used v_mm v_used r_done hi_done mid_in mid_done lo_in lo_done parts_out0 parts_out1 idb
            mxld0 mxld1 exld0 exld1 item mxfree nm_set nm_split shift0 shift1 vst_done st_mm p_set
            pv_mm o_done oout0 oout1 bo_mm bo_done wo_in sums_in sums_inv inv_out added_in even_in
            cx_pool cx_dve wog_set xb_set h2_set wo_mm x1_set xn2_done h2T_mm h2T_act h2T_dve lg_mm
            lg_out ex_in ex_done oh_done cum_mm idx_done slots_in wt_in wt_hi wt_done xr_in0 xr_in1
            tx_mm xT_hi xT_sb fc_mm hh_done ht_done hl_done pj_mm y_done y_out0 y_out1 g_in0 g_in1
            g_in2 g_in3 g_in4 g_in5 g_in6 g_in7 er_set tgt_done idcol w0_done yw_done comb out_done""".split()
        S = {n: sem(n) for n in names}

        block = ctx.enter_context(nc.Block())

        def turned(i, u):
            if isinstance(i, int) and 4 * i + u == 0:
                return 33
            quiet = isinstance(i, int) and 4 * i + u == 2 * BH - 1
            return at(i, 4 * PU, PRO + PU * (u - 1) + (1 if quiet else 11))

        def first(i, n=0):
            return isinstance(i, int) and i == 0 and n == 0

        def at(i, per, count):
            return i * per + count

        NBODY = BH // 2
        SPLIT = NBODY // B
        TB = TT // B
        ZN, ZP = PAIRS_AT // P // 2, N // B // P // 2
        GOES = ((0, H), (H, 2 * H - 2), (2 * H - 2, 2 * H))

        def chunks(go):
            h0, h1 = GOES[go]
            return [(c % KC, max(h0, 8 * c), min(h1, 8 * c + 8)) for c in range(h0 // 8, (h1 + 7) // 8)]

        FETCHED = [sum(len(chunks(j)) for j in range(go + 1)) for go in range(3)]

        @block.sync
        def _(sp):
            sp.dma_start(cT[:], c).then_inc(S["c_in"], 16)
            sp.dma_start(wm, wmod.rearrange("(k p) n -> p k n", p=P)).then_inc(S["wmod_in"], 16)
            sp.dma_start(cst[:], consts).then_inc(S["wmod_in"], 16)
            sp.dma_start(wo_s[:], wo.rearrange("(k p) n -> p k n", p=P)).then_inc(S["wo_in"], 16)
            sp.dma_start(bv_s[:], bv).then_inc(S["wo_in"], 16)
            sp.dma_start(bob[:], bo.rearrange("(a n) -> a n", a=1).broadcast_to([P, D])).then_inc(S["wo_in"], 16)
            xv = x.rearrange("b (t p) d -> p (b t) d", p=P)

            def load_x(q):
                sp.dma_start(xs[:, 8 * q:8 * q + 8, :], xv[:, 8 * q:8 * q + 8, :]).then_inc(S[f"x_in{q}"], 16)

            load_x(0)
            sp.dma_start(wqk_s[:], wqk.rearrange("(k p) s n -> p k s n", p=P)).then_inc(S["w_in"], 16)
            sp.dma_start(bqk_s[:], bqk).then_inc(S["w_in"], 16)
            sp.dma_start(wv_s[:], wv.rearrange("(k p) n -> p k n", p=P)).then_inc(S["w_in"], 16)
            sp.dma_start(trg[:], trig).then_inc(S["w_in"], 16)
            sp.dma_start(wg_s[:], wg.rearrange("(k p) n -> p k n", p=P)).then_inc(S["w_in"], 16)
            for q in range(1, 4):
                load_x(q)

            def load_stacks(qd, kd, par, head, sm):
                for dst, scr, q in ((qd, qs, True), (kd, ks, False)):
                    sp.dma_start(dst[0:48, par, :], scr[head, :, :]).then_inc(sm, 16)
                    src = scr[head, 0:32, :] if q else scr[head, 16:48, :]
                    sp.dma_start(dst[48:80, par, :], src).then_inc(sm, 16)
                    src = scr[head, 0:16, :] if q else scr[head, 32:48, :]
                    sp.dma_start(dst[80:96, par, :], src).then_inc(sm, 16)

            def shift(par, half, count):
                sp.wait_ge(S["mxfree"], count)
                dst = qex[KS:KS + 3, par, UQ * half:UQ * half + UQ].rearrange("r (t q) -> r t q", t=QT)
                sp.dma_start(dst, nms[:, half, :]).then_inc(S[f"shift{half}"], 16)

            zv = xe[0:PAIRS_AT, :].rearrange("(p r s) d -> p r (s d)", p=P, s=2)
            zp = xe[PAIRS_AT + N:PAIRS_AT + N + N // B, :].rearrange("(p r s) d -> p r (s d)", p=P, s=2)
            for g in range(8):
                b, t0 = g // 4, g % 4 * 512
                for s, scr in ((0, qs), (1, ks)):
                    sp.wait_ge(S["lo_done"], 2 * g + s + 1)
                    for part in range(3):
                        row = (part if s == 0 else 2 - part) * DH
                        for ab in range(2):
                            dst = scr[b * H:(b + 1) * H, row + 8 * ab:row + 8 * ab + 8, t0:t0 + 512]
                            sp.dma_start(dst, parts[:, g % 2, part, 2 * s + ab, :]) \
                                .then_inc(S[f"parts_out{g % 2}"], 16)
                if g == 0:
                    sp.wait_ge(S["zero_set"], 1)
                for dst, n in ((zv, ZN), (zp, ZP)):
                    z0, z1 = n * g // 8, n * (g + 1) // 8
                    sp.dma_start(dst[:, z0:z1, :], zero.unsqueeze(1).broadcast_to([P, z1 - z0, 2 * RW])) \
                        .then_inc(S["zero_out"], 16)
                if g == 3:
                    for par in range(2):
                        sp.wait_ge(S[f"parts_out{par}"], 2 * 12 * 16)
                    load_stacks(qmx, kmx, 0, 0, S["mxld0"])

            load_stacks(qex, kex, 0, 0, S["exld0"])
            load_stacks(qmx, kmx, 1, 1, S["mxld1"])
            shift(0, 0, turned(0, 0))
            for par in range(2):
                sp.wait_ge(S[f"parts_out{par}"], 4 * 12 * 16)

            def body(i, last):
                for n in range(2):
                    head = i * 2 + n
                    final = last and n == 1
                    if not last:
                        sp.wait_ge(S["item"], at(i, 4 * PU, PRO + 2 * PU * n))
                        load_stacks(qmx, kmx, n, i * 2 + (n + 2), S[f"mxld{n}"])
                    if not final:
                        if not first(i, n):
                            sp.wait_ge(S["st_mm"], at(i, 64, 32 * n))
                        load_stacks(qex, kex, 1 - n, i * 2 + (n + 1), S[f"exld{1 - n}"])
                    shift(n, 1, turned(i, 2 * n + 1))
                    for half in range(2):
                        sp.wait_ge(S["o_done"], at(i, 4, 2 * n + half + 1))
                        for g in range(4):
                            q0 = UQ * half + 512 * (g % 2)
                            sp.dma_start(os_[g // 2, head, :, q0:q0 + 512],
                                         osb[32 * g:32 * g + DH + 1, 0:512]).then_inc(S[f"oout{half}"], 16)
                        if half == 0 and not final:
                            shift(1 - n, 0, turned(i, 2 * n + 2))

            body(0, False)
            with sp.Fori(1, NBODY - 1) as i:
                body(i, False)
            body(NBODY - 1, True)

            w1v = cfc.rearrange("e (k p) n -> e p k n", p=P)
            w2v = cproj.rearrange("e (k p) n -> e p k n", p=P)

            def load_weights(e):
                sp.dma_start(stg[:, 0, :].rearrange("p (k n) -> p k n", k=KC), w1v[e]).then_inc(S["wt_in"], 16)
                sp.dma_start(stg[:, 1, :].rearrange("p (k n) -> p k n", n=D), w2v[e]).then_inc(S["wt_in"], 16)

            sp.wait_ge(S["cx_dve"], 1)
            load_weights(0)
            sp.wait_ge(S["wt_done"], 2)
            load_weights(1)
            sp.wait_ge(S["slots_in"], 2 * TT * 16)

            def load_rows(par, blk):
                sp.dma_start(xr[:, par], xe.rearrange("(g t p) d -> g p t d", p=P, t=2)[blk]) \
                    .then_inc(S[f"xr_in{par}"], 16)

            load_rows(0, 0)
            load_rows(1, 1)

            def moe_body(i, last):
                for n in range(2 * NB):
                    if not (last and n >= 2 * NB - 2):
                        sp.wait_ge(S["tx_mm"], at(i, 2 * NB, n + 1))
                        sp.wait_ge(S["tgt_done"], at(i, 2 * NB, n + 1))
                        load_rows(n % 2, i * (2 * NB) + (n + 2))
                    if n == 2 and not last:
                        sp.wait_ge(S["wt_done"], at(i, 4, 4))
                        load_weights(i * 2 + 2)
                    if n == NB + 2 and not last:
                        sp.wait_ge(S["wt_done"], at(i, 4, 6))
                        load_weights(i * 2 + 3)

            with sp.Fori(0, NE // 2 - 1) as i:
                moe_body(i, False)
            moe_body(NE // 2 - 1, True)

            sp.wait_ge(S["y_done"], 2 * NE * NB)
            for par in range(2):
                sp.wait_ge(S[f"y_out{par}"], NE * NB * 16)
            yv = xe[PAIRS_AT:EMPTY_AT, :].rearrange("(k t p) d -> k p t d", k=2, p=P)
            for q in range(TT // 4):
                for k in range(2):
                    sp.dma_start(yp[:, q, k], yv[k][:, 4 * q:4 * q + 4, 0:D]).then_inc(S[f"g_in{q}"], 16)
            ov = out.rearrange("b (t p) d -> p (b t) d", p=P)
            for q in range(TT // 4):
                sp.wait_ge(S["comb"], q + 1)
                sp.dma_start(ov[:, 4 * q:4 * q + 4, :], xs[:, 4 * q:4 * q + 4, :]).then_inc(S["out_done"], 16)
            sp.wait_ge(S["out_done"], 16 * (TT // 4))
            sp.wait_ge(S["zero_out"], 2 * 8 * 16)

        @block.vector
        def _(dve):
            V = nc.vector
            chain = [0]

            def link(ins):
                chain[0] += 1
                ins.then_inc(S["dve_step"], 1)
                dve.wait_ge(S["dve_step"], chain[0])

            def stats_of(n0, n1):
                for t in range(n0, n1):
                    last = V.bn_stats(stats[:, t, :], xs[:, t, :])
                link(last)
                for t in range(n0, n1):
                    last = V.bn_aggr(mv[:, t, :], stats[:, t, :])
                link(last)

            def std_start(n0, n1):
                V.tensor_scalar(std[:, n0:n1], mv[:, n0:n1, 1], EPS, None, ALU.add).then_inc(S["std_in"], 1)

            def std_end(k, n0, n1):
                dve.wait_ge(S["std_out"], k)
                link(V.reciprocal(rstd[:, n0:n1], std[:, n0:n1]))

            dve.wait_ge(S["sil_exp"], 1)
            link(V.tensor_scalar(sl[:, 1], sl[:, 0], 1.0, None, ALU.add))
            link(V.reciprocal(sl[:, 2], sl[:, 1]))
            link(V.tensor_tensor(sl[:, 0], cT[:], sl[:, 2], ALU.mult))
            V.tensor_copy(rep, sl[:, 0].unsqueeze(3).broadcast_to([P, KC, B, P])).then_inc(S["sil_rep"], 1)
            dve.wait_ge(S["wmod_in"], 32)
            V.tensor_copy(identb[:], ident).then_inc(S["idb"], 1)
            dve.wait_ge(S["x_in0"], 16)
            stats_of(0, 8)
            std_start(0, 8)
            std_end(1, 0, 8)
            dve.wait_ge(S["modc_mm"], 1)
            mc = bank[0][:, 0:16].rearrange("p (j k b) -> p j k b", j=4, k=KC)
            V.tensor_copy(modc[:, 0:4:2], mc[:, 0:4:2])
            V.tensor_scalar(modc[:, 1:4:2], mc[:, 1:4:2], 1.0, None, ALU.add).then_inc(S["modc_set"], 1)

            def normed(g):
                if g >= 2:
                    dve.wait_ge(S["xT_mm"], 2 * (g - 1))
                for t in range(4):
                    n = 4 * g + t
                    V.tensor_scalar(xn[:, g % 2, t, :], xs[:, n, :], mv[:, n, 0:1], rstd[:, n:n + 1],
                                    ALU.subtract, ALU.mult).then_inc(S["xn_done"], 1)

            normed(0)
            for j in (GA, GB):
                dve.wait_ge(S["bc_mm"], j + 1)
                for b in range(B):
                    g = bank[4 + j][:, D * b:D * b + D]
                    V.tensor_scalar(gts[:, 0], g, 0.0, 2.0, ALU.is_ge, ALU.mult)
                    link(V.tensor_scalar(gts[:, 1], g, -1.0, 0.25, ALU.mult, ALU.max))
                    link(V.tensor_tensor(gts[:, 1], g, gts[:, 1], ALU.max))
                    link(V.scalar_tensor_tensor(bc[:, j, b], gts[:, 0], -1.0, gts[:, 1], ALU.add, ALU.mult))
            dve.wait_ge(S["bc_mm"], CB + 1)
            V.tensor_scalar(bc[:, CB], bank[4 + CB].rearrange("p (b n) -> p b n", b=B), 1.0, None, ALU.add)
            dve.wait_ge(S["bc_mm"], SB + 1)
            V.tensor_copy(bc[:, SB], bank[4 + SB].rearrange("p (b n) -> p b n", b=B))
            dve.wait_ge(S["wo_in"], 48)
            V.tensor_copy(rep[:, :, 0, :], bv_s[:].unsqueeze(2).broadcast_to([P, KC, P])).then_inc(S["bo_done"], 1)
            dve.wait_ge(S["bo_mm"], 1)
            V.tensor_tensor(bob[:], bank[3][:, 0:D], bob[:], ALU.add).then_inc(S["bo_done"], 1)

            dve.wait_ge(S["w_in"], 80)
            for g in range(8):
                if g == 1:
                    std_end(2, 8, 16)
                if g == 3:
                    std_end(3, 16, TT)
                if g < 7:
                    normed(g + 1)
                if g == 0:
                    dve.wait_ge(S["x_in1"], 16)
                    stats_of(8, 16)
                    std_start(8, 16)
                if g == 1:
                    dve.wait_ge(S["x_in2"], 16)
                    dve.wait_ge(S["x_in3"], 16)
                    stats_of(16, TT)
                    std_start(16, TT)
                pos = slice(g % 4 * 512, g % 4 * 512 + 512)
                cos, sin = trg[:, 0, pos], trg[:, 1, pos]
                for s in range(2):
                    dve.wait_ge(S["qk_mm"], 2 * g + s + 1)
                    if g >= 2:
                        dve.wait_ge(S["lo_done"], 2 * (g - 2) + s + 1)
                    a, b_ = bank[2 + 2 * s], bank[3 + 2 * s]
                    ba, bb = bqk_s[:, 2 * s:2 * s + 1], bqk_s[:, 2 * s + 1:2 * s + 2]
                    V.scalar_tensor_tensor(tq[:, 0], a, ba, cos, ALU.add, ALU.mult)
                    V.scalar_tensor_tensor(tq[:, 1], b_, bb, sin, ALU.add, ALU.mult)
                    V.scalar_tensor_tensor(tq[:, 2], a, ba, sin, ALU.add, ALU.mult)
                    V.scalar_tensor_tensor(tq[:, 3], b_, bb, cos, ALU.add, ALU.mult).then_inc(S["qk_used"], 1)
                    dve.wait_ge(S["qk_used"], 2 * g + s + 1)
                    V.tensor_tensor(rq[:, g % 2, 2 * s], tq[:, 0], tq[:, 1], ALU.subtract)
                    V.tensor_tensor(rq[:, g % 2, 2 * s + 1], tq[:, 2], tq[:, 3], ALU.add).then_inc(S["r_done"], 1)
                    dve.wait_ge(S["r_done"], 2 * g + s + 1)

            def reduce_item(i, c_, q, kq, par):
                dve.wait_ge(S["item"], at(i, 4 * PU, c_ + 1))
                V.reduce_max(mxp[:, par, q, kq:kq + 1], bank[4 + c_ % 3], AX.X).then_inc(S["mxfree"], 1)

            def unit_max(i, c_, par):
                dve.wait_ge(S["mxfree"], at(i, 4 * PU, c_ + 1))
                V.tensor_reduce(nm[:, par, :], mxp[:, par], AX.X, ALU.max, negate=True).then_inc(S["nm_set"], 1)

            for k in range(32):
                reduce_item(0, k, k // 4, k % 4, 0)
            unit_max(0, 31, 0)
            dve.wait_ge(S["item"], 33)
            V.tensor_copy(nms[:, 0, :], bank[4 + 32 % 3].bitcast(bf16)[0:3 * QT, 0:P]).then_inc(S["mxfree"], 1)
            for k in range(32):
                reduce_item(0, 33 + k, k // 4, k % 4, 1)

            def att_body(i, last):
                for u in range(4):
                    base = PRO + PU * u
                    quiet = last and u >= 2
                    for k in range(32):
                        if k == 3 and not (last and u == 3):
                            if not first(i, u):
                                dve.wait_ge(S["nm_split"], at(i, 4, u))
                            unit_max(i, base - 1, (u + 1) % 2)
                        if k == 10 and not (last and u == 3):
                            c_ = base + (0 if quiet else 10)
                            dve.wait_ge(S["item"], at(i, 4 * PU, c_ + 1))
                            par = (u + 1) % 2
                            src = bank[4 + c_ % 3].bitcast(bf16)[0:3 * QT, 0:P]
                            heads = (u + 1) // 2
                            if not first(i, heads):
                                dve.wait_ge(S[f"shift{par}"], at(i, 32, 16 * heads))
                            V.tensor_copy(nms[:, par, :], src).then_inc(S["mxfree"], 1)
                        if not quiet:
                            c_ = base + k + (k >= 10)
                            if k == 0:
                                dve.wait_ge(S["nm_set"], at(i, 4, u + 1))
                            reduce_item(i, c_, k // 4, k % 4, u % 2)
                        if u == 1 and k == 16 and isinstance(i, int) and i == SPLIT:
                            inv_sums(0)
                        if u == 1 and k == 16 and last:
                            inv_sums(1)

            def inv_sums(go):
                rows = slice(0, 8 * (GOES[go][1] - GOES[go][0]))
                dve.wait_ge(S["sums_in"], 32 * (go + 1))
                V.reciprocal(ls[rows, :], ls[rows, :]).then_inc(S["sums_inv"], 1)

            def batch_end(b):
                n0, n1 = TB * b, TB * b + TB
                dve.wait_ge(S["xb_set"], b + 1)
                for t in range(n0, n1 + 1):
                    if t < n1:
                        dve.wait_ge(S["wo_mm"], t + 1)
                        V.tensor_tensor(xs[:, t, :], bank[4 + t % 2][:, 0:D], xs[:, t, :], ALU.add) \
                            .then_inc(S["x1_set"], 1)
                    if t > n0:
                        dve.wait_ge(S["x1_set"], t)
                        last = V.bn_stats(stats[:, t - 1, :], xs[:, t - 1, :])
                link(last)
                for t in range(n0, n1):
                    last = V.bn_aggr(mv[:, t, :], stats[:, t, :])
                link(last)
                std_start(n0, n1)
                std_end(4 + b, n0, n1)
                for t in range(n0, n1 + 2):
                    if t < n1:
                        V.tensor_scalar(h2[:, t, 0:D], xs[:, t, :], mv[:, t, 0:1], rstd[:, t:t + 1],
                                        ALU.subtract, ALU.mult).then_inc(S["xn2_done"], 1)
                    u = t - 2
                    if t >= n0 + 2 and u % 2:
                        dve.wait_ge(S["h2T_mm"], u + 1)
                        if u >= 2:
                            dve.wait_ge(S["lg_mm"], u - 1)
                        for k in range(KC):
                            m = V.tensor_scalar(h2T[:, 1, k, :], bank[5][:, P * k:P * k + P],
                                                modc[:, 3, k, b:b + 1], modc[:, 2, k, b:b + 1], ALU.mult, ALU.add)
                        m.then_inc(S["h2T_dve"], 1)
                dve.wait_ge(S["lg_mm"], TB * b + TB)
                V.tensor_copy(lg[:, TB * b:TB * b + TB, :],
                              bank[6][:, 0:TB * NE].rearrange("p (t e) -> p t e", e=NE)).then_inc(S["lg_out"], 1)

            att_body(0, False)
            with dve.Fori(1, SPLIT) as i:
                att_body(i, False)
            att_body(SPLIT, False)
            batch_end(0)
            with dve.Fori(SPLIT + 1, NBODY - 1) as i:
                att_body(i, False)
            att_body(NBODY - 1, True)
            V.memset(onesm[:], 1.0)
            V.memset(base[:], 0.0)

            def over_e(a):
                shape = list(a.shape) + [NE]
                return a.unsqueeze(len(a.shape)).broadcast_to(shape)

            def over_t(a):
                return a.unsqueeze(1).broadcast_to([P, TB, NE])

            def pick(b, k, src):
                link(V.tensor_reduce(m12[:, 0, b], src, AX.X, ALU.max))
                link(V.tensor_tensor(lw2[:, b], src, over_e(m12[:, 0, b]), ALU.is_equal))
                link(V.tensor_tensor(lw2[:, b], lw2[:, b], over_t(iota_m8), ALU.mult))
                link(V.tensor_reduce(rk[:, 0, k, :], lw2[:, b], AX.X, ALU.min))
                return V.tensor_tensor(oh[:, b, k], over_t(iota_m8), over_e(rk[:, 0, k, :]), ALU.is_equal)

            def flat(a):
                return a.rearrange("p t e -> p (t e)")

            def place(b):
                logit = lg[:, TB * b:TB * b + TB, :]
                link(pick(b, 0, logit))
                link(V.scalar_tensor_tensor(flat(lw[:, b]), flat(oh[:, b, 0]), -3.0e38, flat(logit),
                                            ALU.mult, ALU.add))
                pick(b, 1, lw[:, b]).then_inc(S["oh_done"], 1)
                link(V.tensor_copy(pf[:, 0, :, 0, :], base[:]))
                dve.wait_ge(S["cum_mm"], b + 1)
                cum, tot = (bank[5][:, 256 * j:256 * j + 256].rearrange("p (k t e) -> p k t e", k=2, e=NE)
                            for j in range(2))
                link(V.tensor_copy(pf[:, 0, :, 1:TB + 1, :], tot))
                cur = 0
                for n in (1, 2, 4, 8, 16):
                    a_, b_ = pf[:, cur], pf[:, 1 - cur]
                    V.tensor_copy(b_[:, :, 0:n, :], a_[:, :, 0:n, :])
                    link(V.tensor_tensor(b_[:, :, n:, :], a_[:, :, n:, :], a_[:, :, 0:TB + 1 - n, :], ALU.add))
                    cur = 1 - cur
                V.tensor_copy(base[:], pf[:, cur, :, TB, :])
                link(V.tensor_tensor(pf[:, cur, :, 0:TB, :], pf[:, cur, :, 0:TB, :], cum, ALU.add))
                V.tensor_tensor(lw2[:, b], oh[:, b, 1], over_t(base[:, 0]), ALU.mult)
                link(V.tensor_tensor(pf[:, cur, :, 0:TB, :], pf[:, cur, :, 0:TB, :], oh[:, b], ALU.mult))
                V.tensor_reduce(rk[:, 2, 1, :], lw2[:, b], AX.X, ALU.add)
                link(V.tensor_reduce(rk[:, 1], pf[:, cur, :, 0:TB, :], AX.X, ALU.add))
                V.tensor_copy(rk[:, 2, 0, :], rk[:, 1, 0, :])
                V.tensor_scalar(rk[:, 3, 0, :], rk[:, 1, 0, :], 0.0, None, ALU.add)
                V.tensor_scalar(rk[:, 3, 1, :], rk[:, 1, 1, :], -1.0, float(CAP - 1), ALU.mult, ALU.add)
                V.tensor_scalar(rk[:, 0], rk[:, 0], 8.0, float(CAP), ALU.add, ALU.mult)
                link(V.tensor_tensor(rk[:, 2, 1, :], rk[:, 2, 1, :], rk[:, 1, 1, :], ALU.add))
                V.tensor_scalar(rk[:, 4], rk[:, 2], float(CAP), None, ALU.is_lt)
                link(V.tensor_tensor(rk[:, 0], rk[:, 0], rk[:, 3], ALU.add))
                tid = pair_row[:, :, TB * b:TB * b + TB]
                link(V.tensor_tensor(rk[:, 1], rk[:, 0], tid, ALU.subtract))
                link(V.tensor_tensor(rk[:, 1], rk[:, 1], rk[:, 4], ALU.mult))
                link(V.tensor_tensor(rk[:, 1], rk[:, 1], tid, ALU.add))
                V.tensor_copy(idx[:, :, TB * b:TB * b + TB], rk[:, 1]).then_inc(S["idx_done"], 1)
                if b == 0:
                    V.tensor_copy(lim[:], rk[:, 2, 1, :])
                link(V.tensor_copy(pw[:, :, TB * b:TB * b + TB], rk[:, 4]))

            place(0)
            inv_sums(2)
            dve.wait_ge(S["added_in"], 32 * FETCHED[2])
            c_, h0, _ = chunks(2)[0]
            rows = slice(DH * (h0 % 8), P)
            V.tensor_tensor(cxT[rows, c_, :], cxT[rows, c_, :], lT[rows, c_, :], ALU.mult).then_inc(S["cx_dve"], 1)
            batch_end(1)

            dve.wait_ge(S["lg_out"], B)
            V.tensor_copy(first0[:], base[:, 0])
            place(1)

            def weights():
                link(V.tensor_tensor(first0[:], base[:, 0], first0[:], ALU.subtract))
                link(V.tensor_tensor(lw2[:, 0], oh[:, 0, 1], over_t(first0[:]), ALU.mult))
                link(V.tensor_reduce(rk[:, 5, 0, :], lw2[:, 0], AX.X, ALU.add))
                link(V.tensor_tensor(lim[:], lim[:], rk[:, 5, 0, :], ALU.add))
                link(V.tensor_scalar(pw[:, 1, 0:TB], lim[:], float(CAP), None, ALU.is_lt))
                def tiles(a):
                    return a.rearrange("p b t e -> p (b t) e")

                link(V.tensor_tensor(sel[:], oh[:, :, 0], oh[:, :, 1], ALU.add))
                link(V.tensor_tensor(tiles(lw[:]), lg[:], tiles(sel[:]), ALU.mult))
                link(V.tensor_scalar(lw2[:], sel[:], -1.0, 1.0e9, ALU.add, ALU.mult))
                link(V.tensor_tensor(lw[:], lw[:], lw2[:], ALU.add))
                link(V.tensor_reduce(m12[:, 0], lw[:], AX.X, ALU.max))
                V.tensor_tensor(lw2[:], lw[:], over_e(m12[:, 0]), ALU.subtract).then_inc(S["ex_in"], 1)
                dve.wait_ge(S["ex_done"], 1)
                link(V.tensor_reduce(m12[:, 0], lw[:], AX.X, ALU.add))
                link(V.reciprocal(m12[:, 1], m12[:, 0]))
                one = m12[:, 1].rearrange("p b t -> p (b t)")
                for k in range(2):
                    link(V.tensor_tensor(lw2[:], lw[:], oh[:, :, k], ALU.mult))
                    link(V.tensor_reduce(m12[:, 0], lw2[:], AX.X, ALU.add))
                    link(V.tensor_tensor(pw[:, k, :], m12[:, 0].rearrange("p b t -> p (b t)"), pw[:, k, :], ALU.mult))
                    link(V.tensor_tensor(pw[:, k, :], one, pw[:, k, :], ALU.mult))

            weights()
            def low_weights(i, e):
                for j, w in enumerate((w1p, w2p)):
                    hi, lo = (w[c_][:, e % 2].rearrange("p k n -> p (k n)") for c_ in range(2))
                    dve.wait_ge(S["wt_hi"], at(i, 4, 2 * e + j + 1))
                    V.tensor_tensor(lo, stg[:, j, :], hi.bitcast(f32), ALU.subtract).then_inc(S["wt_done"], 1)

            low_weights(0, 0)
            low_weights(0, 1)
            V.memset(yb[:, :, :, D:RW], 0.0)

            def low_parts(i, n):
                for hf in range(2):
                    dve.wait_ge(S["ht_done"], at(i, 4 * NB, 2 * n + hf + 1))
                    V.tensor_tensor(hdp[1][:, n % 2, 4 * hf:4 * hf + 4, :], hd[:, hf],
                                    hdp[0][:, n % 2, 4 * hf:4 * hf + 4, :].bitcast(f32), ALU.subtract) \
                        .then_inc(S["hl_done"], 1)

            def targets(i, n):
                dve.wait_ge(S[f"xr_in{n % 2}"], at(i, 16 * NB, 16 * (n // 2 + 1)))
                if not first(i, n // 2):
                    dve.wait_ge(S[f"y_out{n % 2}"], at(i, 32 * NB, 32 * (n // 2)))
                row = xr[:, n % 2, :, D]
                V.scalar_tensor_tensor(er[:, 0], row, 0.0, slot_row, ALU.is_equal, ALU.mult).then_inc(S["er_set"], 1)
                dve.wait_ge(S["er_set"], at(i, 4 * NB, 2 * n + 1))
                V.tensor_scalar(slot_row, slot_row, float(BLK), None, ALU.add)
                V.tensor_tensor(er[:, 1], er[:, 0], row, ALU.add).then_inc(S["er_set"], 1)
                dve.wait_ge(S["er_set"], at(i, 4 * NB, 2 * n + 2))
                V.tensor_copy(tgt[:, n % 2], er[:, 1]).then_inc(S["tgt_done"], 1)

            def xt_out(i, n):
                targets(i, n)
                dve.wait_ge(S["tx_mm"], at(i, 2 * NB, n + 1))
                if not first(i, n // 2):
                    dve.wait_ge(S["fc_mm"], at(i, 4 * NB, 2 * (n - 1)))
                src = bank[6 + n % 2].rearrange("p (k s) -> p k s", k=KC)
                V.tensor_copy(xTp[0][:, n % 2], src).then_inc(S["xT_hi"], 1)
                dve.wait_ge(S["xT_hi"], at(i, 2 * NB, n + 1))
                V.tensor_tensor(xTp[1][:, n % 2], src, xTp[0][:, n % 2].bitcast(f32), ALU.subtract) \
                    .then_inc(S["xT_sb"], 1)

            def y_out(i, n):
                for t in range(2):
                    dve.wait_ge(S["pj_mm"], at(i, 4 * NB, 2 * n + t + 1))
                    V.tensor_copy(yb[:, n % 2, t, 0:D], bank[4 + t][:, 0:D]).then_inc(S["y_done"], 1)

            xt_out(0, 0)

            def moe_body(i, last):
                for n in range(2 * NB):
                    low_parts(i, n)
                    if not (last and n == 2 * NB - 1):
                        xt_out(i, n + 1)
                    y_out(i, n)
                    if n == 1 and not first(i):
                        low_weights(i, 1)
                    if n == NB + 1 and not last:
                        low_weights(i, 2)

            moe_body(0, False)
            with dve.Fori(1, NE // 2 - 1) as i:
                moe_body(i, False)
            moe_body(NE // 2 - 1, True)

            for q in range(TT // 4):
                dve.wait_ge(S[f"g_in{q}"], 32)
                dve.wait_ge(S["w0_done"], 4 * q + 4)
                for t in range(4):
                    y0, y1 = (yp[:, q, k, t, :] for k in range(2))
                    m = V.scalar_tensor_tensor(y1, y1, pw[:, 1, 4 * q + t:4 * q + t + 1], y0, ALU.mult, ALU.add)
                link(m)
                gb = bc[:, GB, q // (TB // 4)].unsqueeze(1).broadcast_to([P, 4, D])
                V.tensor_tensor(yp[:, q, 0], yp[:, q, 1], gb, ALU.mult).then_inc(S["yw_done"], 1)

        @block.scalar
        def _(act):
            A = nc.scalar
            act.wait_ge(S["c_in"], 16)
            A.activation(sl[:, 0], cT[:], ACT.Exp, scale=-1.0).then_inc(S["sil_exp"], 1)

            def root(q):
                part = (slice(0, 8), slice(8, 16), slice(16, TT))[q]
                act.wait_ge(S["std_in"], q + 1)
                A.activation(std[:, part], std[:, part], ACT.Sqrt).then_inc(S["std_out"], 1)

            root(0)

            def scale_h(g):
                for k in range(KC):
                    act.wait_ge(S["xT_mm"], 2 * g + k + 1)
                    if g >= 2:
                        act.wait_ge(S["v_mm"], g - 1)
                    if g == 0:
                        act.wait_ge(S["modc_set"], 1)
                    b = g // 4
                    A.activation(hT[:, g % 2, k, :], bank[k], ACT.Identity, scale=modc[:, 1, k, b:b + 1],
                                 bias=modc[:, 0, k, b:b + 1]).then_inc(S["hT_done"], 1)

            def values(m):
                act.wait_ge(S["v_mm"], m + 1)
                b, k0 = m // 4, m % 4 * 4
                if m == 0:
                    act.wait_ge(S["v_one"], 4)
                for j in range(2):
                    src = bank[6 + j].rearrange("p (t h d) -> p t h d", t=2, h=H)
                    for t in range(2):
                        A.activation(vall[:, b * H:(b + 1) * H, k0 + 2 * j + t, 0:DH], src[:, t],
                                     ACT.Copy).then_inc(S["v_used"], 1)

            def part(m, s, k, ready, done):
                act.wait_ge(S[ready], 2 * m + s + 1)
                A.activation(parts[:, m % 2, k, 2 * s:2 * s + 2], rq[:, m % 2, 2 * s:2 * s + 2],
                             ACT.Copy).then_inc(S[done], 1)

            def high(m, s):
                if m >= 2:
                    act.wait_ge(S[f"parts_out{m % 2}"], 12 * 16 * (m // 2))
                if m == 0:
                    act.wait_ge(S["bo_mm"], 1)
                part(m, s, 0, "r_done", "hi_done")

            def middle(m, s):
                part(m, s, 1, "mid_in", "mid_done")

            def low(m, s):
                part(m, s, 2, "lo_in", "lo_done")

            scale_h(0)
            root(1)
            for m in range(8):
                if m < 7:
                    scale_h(m + 1)
                high(m, 0)
                if m == 1:
                    root(2)
                if m > 0:
                    low(m - 1, 1)
                if m == 7:
                    values(m)
                middle(m, 0)
                high(m, 1)
                if m < 7:
                    values(m)
                low(m, 0)
                middle(m, 1)
            low(7, 1)

            def exp_step(i, c_):
                act.wait_ge(S["st_mm"], at(i, 64, c_ + 1))
                if not first(i, c_ // 4):
                    act.wait_ge(S["pv_mm"], at(i, 32, c_ // 2 - 1))
                s = c_ % 2
                A.activation(pr[:, c_ % 4, :], ps[:, 2 * s:2 * s + 2, :].rearrange("p a n -> p (a n)"), ACT.Exp,
                             scale=0.25).then_inc(S["p_set"], 1)

            def att_body(i, last, split=False):
                for u in range(4):
                    for k in range(NKT):
                        if not ((last or split) and u == 3 and k >= NKT - 2):
                            exp_step(i, NKT * u + k + 2)
                    act.wait_ge(S["pv_mm"], at(i, 32, NKT // 2 * (u + 1)))
                    if first(i, u):
                        act.wait_ge(S["zero_out"], 2 * 8 * 16)
                    else:
                        act.wait_ge(S[f"oout{(u + 1) % 2}"], at(i, 128, 64 * ((u + 1) // 2)))
                    A.activation(osb[:, 0:512], bank[7], ACT.Copy).then_inc(S["o_done"], 1)

            def batch_end(b):
                n0 = TB * b
                act.wait_ge(S["std_in"], 4 + b)
                A.activation(std[:, n0:n0 + TB], std[:, n0:n0 + TB], ACT.Sqrt).then_inc(S["std_out"], 1)
                for t in range(n0, n0 + TB, 2):
                    act.wait_ge(S["h2T_mm"], t + 1)
                    if t >= 2:
                        act.wait_ge(S["lg_mm"], t - 1)
                    for k in range(KC):
                        m = A.activation(h2T[:, 0, k, :], bank[4][:, P * k:P * k + P], ACT.Identity,
                                         scale=modc[:, 3, k, b:b + 1], bias=modc[:, 2, k, b:b + 1])
                    m.then_inc(S["h2T_act"], 1)

            exp_step(0, 0)
            exp_step(0, 1)
            att_body(0, False)
            with act.Fori(1, SPLIT) as i:
                att_body(i, False)
            att_body(SPLIT, False, split=True)
            batch_end(0)
            exp_step(SPLIT + 1, 0)
            exp_step(SPLIT + 1, 1)
            with act.Fori(SPLIT + 1, NBODY - 1) as i:
                att_body(i, False)
            att_body(NBODY - 1, True)
            batch_end(1)
            def high_parts(i, e):
                act.wait_ge(S["wt_in"], at(i, 64, 32 * (e + 1)))
                for j, w in enumerate((w1p, w2p)):
                    A.activation(w[0][:, e % 2].rearrange("p k n -> p (k n)"), stg[:, j, :], ACT.Copy) \
                        .then_inc(S["wt_hi"], 1)

            high_parts(0, 0)
            act.wait_ge(S["ex_in"], 1)
            A.activation(lw[:], lw2[:], ACT.Exp).then_inc(S["ex_done"], 1)
            high_parts(0, 1)

            def gelu(i, n):
                for hf in range(2):
                    act.wait_ge(S["fc_mm"], at(i, 4 * NB, 2 * n + hf + 1))
                    if hf == 0 and not first(i, n // 2):
                        act.wait_ge(S["pj_mm"], at(i, 4 * NB, 2 * (n - 1)))
                    src = ps[:, 2 * hf:2 * hf + 2, :].rearrange("p a n -> p (a n)")
                    A.activation(hdp[0][:, n % 2, 4 * hf:4 * hf + 4, :].rearrange("p m s -> p (m s)"), src,
                                 ACT.Gelu).then_inc(S["hh_done"], 1)
                    if not first(i, n):
                        act.wait_ge(S["hl_done"], at(i, 4 * NB, 2 * (n - 1) + hf + 1))
                    act.wait_ge(S["hh_done"], at(i, 4 * NB, 2 * n + hf + 1))
                    A.activation(hd[:, hf].rearrange("p m s -> p (m s)"), src, ACT.Gelu).then_inc(S["ht_done"], 1)

            def moe_body(i, last):
                for n in range(2 * NB):
                    gelu(i, n)
                    if n == 0 and not first(i):
                        high_parts(i, 1)
                    if n == NB and not last:
                        high_parts(i, 2)

            moe_body(0, False)
            with act.Fori(1, NE // 2 - 1) as i:
                moe_body(i, False)
            moe_body(NE // 2 - 1, True)
            for t in range(TT):
                if t % 4 == 0:
                    act.wait_ge(S[f"g_in{t // 4}"], 32)
                y = yp[:, t // 4, 0, t % 4, :]
                A.activation(y, y, ACT.Copy, scale=pw[:, 0, t:t + 1]).then_inc(S["w0_done"], 1)

        @block.gpsimd
        def _(pool):
            G = nc.gpsimd
            G.memset(zero, 0.0).then_inc(S["zero_set"], 1)
            G.memset(nil[:], 0.0).then_inc(S["v_one"], 1)
            G.memset(vst[:], 0.0).then_inc(S["v_one"], 1)
            G.memset(vall[:, :, :, DH:DH + 1], 1.0).then_inc(S["v_one"], 1)
            pool.wait_ge(S["v_one"], 3)
            G.memset(kex[KS:KS + 3, :, :], 1.0).then_inc(S["v_one"], 1)
            pool.wait_ge(S["v_one"], 4)
            for g in range(8):
                for left, k, done in (("mid_in", 0, "hi_done"), ("lo_in", 1, "mid_done")):
                    for s in range(2):
                        pool.wait_ge(S[done], 2 * g + s + 1)
                        q = rq[:, g % 2, 2 * s:2 * s + 2]
                        G.tensor_tensor(q, q, parts[:, g % 2, k, 2 * s:2 * s + 2], ALU.subtract).then_inc(S[left], 1)

            def split_max(i, count, par):
                if not first(i, (count - 1) // 2):
                    pool.wait_ge(S["mxfree"], turned(i, count - 3))
                pool.wait_ge(S["nm_set"], at(i, 4, count))

                def step(ins, k):
                    ins.then_inc(S["pool_step"], 1)
                    pool.wait_ge(S["pool_step"], at(i, 16, 4 * (count - 1) + k))

                step(G.tensor_tensor(nmp[:, par, 0], nm[:, par], nil[:], ALU.add), 1)
                step(G.tensor_tensor(nmr[:, par, 0], nm[:, par], nmp[:, par, 0], ALU.subtract), 2)
                step(G.tensor_tensor(nmp[:, par, 1], nmr[:, par, 0], nil[:], ALU.add), 3)
                step(G.tensor_tensor(nmr[:, par, 1], nmr[:, par, 0], nmp[:, par, 1], ALU.subtract), 4)
                G.tensor_tensor(nmp[:, par, 2], nmr[:, par, 1], nil[:], ALU.add).then_inc(S["nm_split"], 1)

            def stage_values(i, n, head):
                G.tensor_copy(vst[:, n, :, 0:DH + 1], vall[:, head]).then_inc(S["vst_done"], 1)

            pool.wait_ge(S["v_used"], 32)
            pool.wait_ge(S["v_one"], 4)
            stage_values(0, 0, 0)
            split_max(0, 1, 0)
            split_max(0, 2, 1)

            def att_body(i, last):
                for n in range(2):
                    if not (last and n == 1):
                        if not first(i, n):
                            pool.wait_ge(S["pv_mm"], at(i, 32, 16 * n))
                        stage_values(i, 1 - n, i * 2 + (n + 1))
                    for half in range(2):
                        if (not last or n == 0) and not (isinstance(i, int) and i == SPLIT and n + half == 2):
                            split_max(i, 2 * n + half + 3, half)
                        if isinstance(i, int) and i == SPLIT:
                            if n == 0 and half == 0:
                                load_sums(0)
                                scale_by_ga(0)
                            elif n == 0:
                                load_outputs(0)
                            else:
                                normalise(0, n - 1 + half)
                        if last:
                            if n == 0 and half == 0:
                                load_sums(1)
                                scale_by_ga(1)
                            elif n == 0:
                                load_outputs(1)
                            else:
                                normalise(1, n - 1 + half)

            def load_sums(go):
                h0, h1 = GOES[go]
                for half in range(2):
                    pool.wait_ge(S[f"oout{half}"], h1 * 4 * 16)
                sums = ls[0:8 * (h1 - h0), :]
                pool.dma_start(sums, os_[0, h0:h1, DH, :]).then_inc(S["sums_in"], 16)
                if go == 2:
                    outputs_in(go)
                pool.wait_ge(S["sums_in"], 32 * go + 16)
                pool.dma_start(sums, os_[1, h0:h1, DH, :], accum_op=ALU.add).then_inc(S["sums_in"], 16)
                if go == 2:
                    outputs_add(go)

            def rows_of(a, b):
                return slice(DH * (a % 8), DH * (a % 8) + DH * (b - a))

            def outputs_in(go):
                for k, a, b in chunks(go):
                    pool.dma_start(cxT[rows_of(a, b), k, :], os_[0, a:b, 0:DH, :]).then_inc(S["even_in"], 16)

            def outputs_add(go):
                pool.wait_ge(S["even_in"], 16 * FETCHED[go])
                for k, a, b in chunks(go):
                    pool.dma_start(cxT[rows_of(a, b), k, :], os_[1, a:b, 0:DH, :], accum_op=ALU.add) \
                        .then_inc(S["added_in"], 16)

            def scale_by_ga(b):
                pool.wait_ge(S["bo_done"], 2)
                if b:
                    pool.wait_ge(S["wo_mm"], TB)
                for k in range(KC):
                    G.tensor_tensor(wog[:, k, :], wo_s[:, k, :], bc[:, GA, b], ALU.mult).then_inc(S["wog_set"], 1)
                G.tensor_tensor(gbo[:], bob[:], bc[:, GA, b], ALU.mult).then_inc(S["wog_set"], 1)
                pool.wait_ge(S["wog_set"], 3 * b + 3)
                tiles = xs[:, TB * b:TB * b + TB, :]
                G.tensor_tensor(tiles, tiles, gbo[:].unsqueeze(1).broadcast_to([P, TB, D]), ALU.add) \
                    .then_inc(S["xb_set"], 1)

            def load_outputs(go):
                h0, h1 = GOES[go]
                pool.wait_ge(S["sums_inv"], go + 1)
                pool.dma_start(linv[h0:h1, :], ls[0:8 * (h1 - h0), :]).then_inc(S["inv_out"], 16)
                pool.wait_ge(S["inv_out"], 16 * (go + 1))
                if go < 2:
                    outputs_in(go)
                    outputs_add(go)
                for k, a, b in chunks(go):
                    pool.dma_start(lT[rows_of(a, b), k, :], linv[a:b, :].unsqueeze(1).broadcast_to([b - a, DH, T])) \
                        .then_inc(S["added_in"], 16)

            def normalise(go, j):
                k, a, b = chunks(go)[j]
                rows = slice(0, DH * (b - a))
                pool.wait_ge(S["added_in"], 32 * FETCHED[go])
                for q in range(4):
                    part = slice(512 * q, 512 * q + 512)
                    G.tensor_tensor(cxT[rows, k, part], cxT[rows, k, part], lT[rows, k, part], ALU.mult) \
                        .then_inc(S["cx_pool"], 1)

            def h_rows(b):
                for q in range(4):
                    n0 = TB * b + 4 * q
                    pool.wait_ge(S["h2T_mm"], n0 + 4)
                    tiles = h2[:, n0:n0 + 4, 0:D]
                    G.tensor_tensor(tiles, tiles, bc[:, CB, b].unsqueeze(1).broadcast_to([P, 4, D]), ALU.mult) \
                        .then_inc(S["h2_step"], 1)
                    pool.wait_ge(S["h2_step"], 4 * b + q + 1)
                    G.tensor_tensor(tiles, tiles, bc[:, SB, b].unsqueeze(1).broadcast_to([P, 4, D]), ALU.add) \
                        .then_inc(S["h2_set"], 1)

            def scatter(b):
                n0 = TB * b
                pool.wait_ge(S["idx_done"], b + 1)
                pool.wait_ge(S["h2_set"], 4 * b + 4)
                pool.wait_ge(S["zero_out"], 2 * 8 * 16)
                for k in range(2):
                    if b or k:
                        pool.wait_ge(S["slots_in"], 16 * (2 * n0 + TB * k))
                    G.tensor_copy(h2[:, n0:n0 + TB, D], pair_row[:, k, n0:n0 + TB]).then_inc(S["idcol"], 1)
                    pool.wait_ge(S["idcol"], 2 * b + k + 1)
                    for t in range(n0, n0 + TB):
                        pool.indirect_dma_start(out=xe, out_offset=bass.IndirectOffsetOnAxis(
                            ap=idx[:, k, t:t + 1], axis=0), in_=h2[:, t, :], in_offset=None) \
                            .then_inc(S["slots_in"], 16)

            att_body(0, False)
            with pool.Fori(1, SPLIT) as i:
                att_body(i, False)
            att_body(SPLIT, False)
            split_max(SPLIT, 6, 1)
            h_rows(0)
            with pool.Fori(SPLIT + 1, NBODY - 1) as i:
                att_body(i, False)
            att_body(NBODY - 1, True)
            load_sums(2)
            load_outputs(2)
            scatter(0)
            h_rows(1)
            scatter(1)

            for n in range(NE * NB):
                pool.wait_ge(S["tgt_done"], n + 1)
                for t in range(2):
                    pool.wait_ge(S["y_done"], 2 * n + t + 1)
                    pool.indirect_dma_start(out=xe, out_offset=bass.IndirectOffsetOnAxis(
                        ap=tgt[:, n % 2, t:t + 1], axis=0), in_=yb[:, n % 2, t, :], in_offset=None) \
                        .then_inc(S[f"y_out{n % 2}"], 16)
            for q in range(TT // 4):
                pool.wait_ge(S["yw_done"], q + 1)
                tiles = xs[:, 4 * q:4 * q + 4, :]
                G.tensor_tensor(tiles, tiles, yp[:, q, 0], ALU.add).then_inc(S["comb"], 1)

        @block.tensor
        def _(pe):
            M = nc.tensor.matmul
            pe.wait_ge(S["wmod_in"], 32)
            pe.wait_ge(S["sil_rep"], 1)
            for j, src in enumerate((0, 1, 3, 4)):
                for f in range(KC):
                    o = bank[0][:, (j * KC + f) * B:(j * KC + f) * B + B]
                    for k in range(KC):
                        m = M(o, wm[:, k, src * D + f * P:src * D + f * P + P], sl[:, 0, k, :],
                              start=(k == 0), stop=(k == KC - 1))
            m.then_inc(S["modc_mm"], 1)
            for j, src in ((GA, 2), (GB, 5), (CB, 4), (SB, 3)):
                for b in range(B):
                    for k in range(KC):
                        m = M(bank[4 + j][:, D * b:D * b + D], rep[:, k, b, :], wm[:, k, src * D:src * D + D],
                              start=(k == 0), stop=(k == KC - 1))
                m.then_inc(S["bc_mm"], 1)
            pe.wait_ge(S["bo_done"], 1)
            for k in range(KC):
                m = M(bank[3][:, 0:D], rep[:, k, 0, :], wo_s[:, k, :], start=(k == 0), stop=(k == KC - 1))
            m.then_inc(S["bo_mm"], 1)
            pe.wait_ge(S["modc_set"], 1)
            pe.wait_ge(S["w_in"], 80)
            def turn_x(g):
                pe.wait_ge(S["xn_done"], 4 * g + 4)
                for k in range(KC):
                    if g >= 1:
                        pe.wait_ge(S["hT_done"], 2 * (g - 1) + k + 1)
                    for t in range(4):
                        m = nc.tensor.transpose(bank[k][:, P * t:P * t + P], xn[:, g % 2, t, P * k:P * k + P], ident)
                    m.then_inc(S["xT_mm"], 1)

            turn_x(0)
            pe.wait_ge(S["bo_done"], 2)
            for g in range(8):
                pe.wait_ge(S["hT_done"], 2 * g + 2)
                for s in range(2):
                    if g >= 1:
                        pe.wait_ge(S["qk_used"], 2 * (g - 1) + s + 1)
                    for ab in range(2):
                        for k in range(KC):
                            m = M(bank[2 + 2 * s + ab], wqk_s[:, k, 2 * s + ab, :], hT[:, g % 2, k, :],
                                  start=(k == 0), stop=(k == KC - 1))
                    m.then_inc(S["qk_mm"], 1)
                if g < 7:
                    turn_x(g + 1)
                if g >= 1:
                    pe.wait_ge(S["v_used"], 4 * g)
                for t in range(4):
                    for k in range(KC):
                        m = M(bank[6 + t // 2][:, D * (t % 2):D * (t % 2) + D], hT[:, g % 2, k, P * t:P * t + P],
                              wv_s[:, k, :], start=(k == 0), stop=(k == KC - 1))
                m.then_inc(S["v_mm"], 1)

            def score(i, par, item, q, kq, free):
                if free:
                    pe.wait_ge(S["mxfree"], at(i, 4 * PU, item - 2))
                M(bank[4 + item % 3], qmx[:, par, P * q:P * q + P], kmx[:, par, 512 * kq:512 * kq + 512],
                  start=True, stop=True).then_inc(S["item"], 1)

            def turn(i, item, par, count):
                pe.wait_ge(S["nm_split"], at(i, 4, count))
                pe.wait_ge(S["mxfree"], at(i, 4 * PU, item - 2))
                nc.tensor.transpose(bank[4 + item % 3].bitcast(bf16)[0:3 * QT, 0:P],
                                    nmp[:, par].rearrange("p c t -> p (c t)"), identb[:]).then_inc(S["item"], 1)

            def scoresT(i, c_):
                n, half, k = c_ // 32 % 2, c_ // NKT % 2, c_ % NKT
                if not first(i, c_ // 2):
                    pe.wait_ge(S["p_set"], at(i, 64, c_ - 1))
                s = c_ % 2
                for j in range(2):
                    q0 = UQ * half + 512 * j
                    m = M(bank[2 * s + j], kex[:, n, P * k:P * k + P], qex[:, n, q0:q0 + 512], start=True, stop=True)
                m.then_inc(S["st_mm"], 1)

            def unit_ready(i, c_):
                n, half = c_ // 32 % 2, c_ // NKT % 2
                if half == 0:
                    pe.wait_ge(S[f"exld{n}"], at(i, 96, 96 * (c_ // 64 + 1)))
                pe.wait_ge(S[f"shift{half}"], at(i, 32, 16 * (c_ // 32 + 1)))

            def weigh(i, c_):
                n, unit, k = c_ // 32 % 2, c_ // NKT, c_ % NKT
                pe.wait_ge(S["p_set"], at(i, 64, c_ + 2))
                if k == 0 and not first(i, unit):
                    pe.wait_ge(S["o_done"], at(i, 4, unit))
                if k == 0 and unit % 2 == 0:
                    pe.wait_ge(S["vst_done"], at(i, 2, n + 1))
                for g in range(4):
                    odd, q0 = g // 2, 512 * (g % 2)
                    m = M(bank[7][32 * g:32 * g + VW, :], vst[:, n, k + odd, :], pr[:, (c_ + odd) % 4, q0:q0 + 512],
                          start=(k == 0), stop=(k == NKT - 2), tile_position=(0, 32 * g))
                m.then_inc(S["pv_mm"], 1)

            pe.wait_ge(S["mxld0"], 96)
            pe.wait_ge(S["idb"], 1)
            pe.wait_ge(S["r_done"], 16)
            pe.wait_ge(S["v_used"], 32)
            for k in range(32):
                score(0, 0, k, k // 4, k % 4, k >= 3)
            turn(0, 32, 0, 1)
            for k in range(32):
                score(0, 0, 33 + k, QT + k // 4, k % 4, True)
            unit_ready(0, 0)
            pe.wait_ge(S["v_one"], 4)
            scoresT(0, 0)
            scoresT(0, 1)

            def count_pairs(b):
                pe.wait_ge(S["oh_done"], b + 1)
                ohf = oh[:, b].rearrange("p k t e -> p (k t e)")
                M(bank[5][:, 0:256], tri, ohf, start=True, stop=True)
                M(bank[5][:, 256:512], onesm[:], ohf, start=True, stop=True).then_inc(S["cum_mm"], 1)

            def att_body(i, last):
                for u in range(4):
                    n, half = u // 2, u % 2
                    quiet = last and u >= 2
                    base = PRO + PU * u
                    for k in range(0, NKT, 2):
                        c_ = NKT * u + k

                        def maxima(m):
                            if not quiet:
                                score(i, 1 - n, base + m + (m >= 10), QT * half + m // 4, m % 4, True)

                        if not quiet and k == 0 and half == 0:
                            pe.wait_ge(S[f"mxld{1 - n}"], at(i, 96, 96 * (n + 1)))
                        more = not (last and c_ == 62)
                        if more:
                            if k == NKT - 2:
                                unit_ready(i, c_ + 2)
                            scoresT(i, c_ + 2)
                        maxima(2 * k)
                        maxima(2 * k + 1)
                        if last and u == 2 and k == 12:
                            count_pairs(0)
                        if k == 4 and not (last and u == 3):
                            turn(i, base + (0 if quiet else 10), (u + 1) % 2, u + 2)
                        if more:
                            scoresT(i, c_ + 3)
                        maxima(2 * k + 2)
                        weigh(i, c_)
                        maxima(2 * k + 3)

            def logits(t):
                pe.wait_ge(S["h2T_dve" if t % 2 else "h2T_act"], t // 2 + 1)
                for k in range(KC):
                    m = M(bank[6][:, NE * (t % TB):NE * (t % TB) + NE], h2T[:, t % 2, k, :], wg_s[:, k, :],
                          start=(k == 0), stop=(k == KC - 1))
                m.then_inc(S["lg_mm"], 1)

            def batch_end(b):
                n0 = TB * b
                items = PRO + PU * 4 * (SPLIT + 1) if b == 0 else PRO + PU * (2 * BH - 2) + 1
                pe.wait_ge(S["mxfree"], items)
                pe.wait_ge(S["cx_pool"], 8 * b + 8)
                if b:
                    pe.wait_ge(S["cx_dve"], 1)
                pe.wait_ge(S["xb_set"], b + 1)
                for t in range(n0, n0 + TB):
                    if t >= n0 + 2:
                        pe.wait_ge(S["x1_set"], t - 1)
                    for k in range(KC):
                        m = M(bank[4 + t % 2][:, 0:D], cxT[:, k, P * (t - n0):P * (t - n0) + P], wog[:, k, :],
                              start=(k == 0), stop=(k == KC - 1))
                    m.then_inc(S["wo_mm"], 1)
                for t in range(n0, n0 + TB):
                    pe.wait_ge(S["xn2_done"], t + 1)
                    if t >= n0 + 2:
                        pe.wait_ge(S["h2T_dve" if t % 2 else "h2T_act"], t // 2)
                    else:
                        pe.wait_ge(S["x1_set"], n0 + TB)
                    for k in range(KC):
                        m = nc.tensor.transpose(bank[4 + t % 2][:, P * k:P * k + P], h2[:, t, P * k:P * k + P],
                                                ident)
                    m.then_inc(S["h2T_mm"], 1)
                    if t > n0:
                        logits(t - 1)
                logits(n0 + TB - 1)
                pe.wait_ge(S["lg_out"], b + 1)

            att_body(0, False)
            with pe.Fori(1, SPLIT) as i:
                att_body(i, False)
            att_body(SPLIT, False)
            batch_end(0)
            with pe.Fori(SPLIT + 1, NBODY - 1) as i:
                att_body(i, False)
            att_body(NBODY - 1, True)
            batch_end(1)
            count_pairs(1)

            def turn_rows(i, n):
                pe.wait_ge(S[f"xr_in{n % 2}"], at(i, 16 * NB, 16 * (n // 2 + 1)))
                if not first(i, n // 2):
                    pe.wait_ge(S["xT_sb"], at(i, 2 * NB, n - 1))
                for k in range(KC):
                    for t in range(2):
                        m = nc.tensor.transpose(bank[6 + n % 2][:, BLK * k + P * t:BLK * k + P * t + P],
                                                xr[:, n % 2, t, P * k:P * k + P], ident)
                m.then_inc(S["tx_mm"], 1)

            pe.wait_ge(S["idx_done"], B)
            turn_rows(0, 0)

            PAIRS = ((0, 0), (0, 1), (1, 0))

            def moe_body(i, last):
                for e in range(2):
                    for b in range(NB):
                        n = e * NB + b
                        if b == 0:
                            pe.wait_ge(S["wt_done"], at(i, 4, 2 * e + 2))
                        pe.wait_ge(S["xT_sb"], at(i, 2 * NB, n + 1))
                        for hf in range(2):
                            if not first(i, n):
                                pe.wait_ge(S["ht_done"], at(i, 4 * NB, 2 * (n - 1) + hf + 1))
                            for mm in range(4):
                                f = 4 * hf + mm
                                o = ps[:, 2 * hf + mm // 2, BLK * (mm % 2):BLK * (mm % 2) + BLK]
                                for k in range(KC):
                                    for q, (wp, xp) in enumerate(PAIRS):
                                        m = M(o, w1p[wp][:, e, k, P * f:P * f + P], xTp[xp][:, n % 2, k, :],
                                              start=(k + q == 0), stop=(k == KC - 1 and q == 2))
                            m.then_inc(S["fc_mm"], 1)
                        if not (last and n == 2 * NB - 1):
                            turn_rows(i, n + 1)
                        for hf in range(2):
                            for t in range(2):
                                if hf == 0 and not first(i, n):
                                    pe.wait_ge(S["y_done"], at(i, 4 * NB, 2 * (n - 1) + t + 1))
                                if t == 0:
                                    pe.wait_ge(S["hl_done"], at(i, 4 * NB, 2 * n + hf + 1))
                                for f in range(4 * hf, 4 * hf + 4):
                                    for q, (hp, wp) in enumerate(PAIRS):
                                        m = M(bank[4 + t][:, 0:D], hdp[hp][:, n % 2, f, P * t:P * t + P],
                                              w2p[wp][:, e, f, :], start=(f + q == 0),
                                              stop=(f == HID // P - 1 and q == 2))
                                if hf == 1:
                                    m.then_inc(S["pj_mm"], 1)

            moe_body(0, False)
            with pe.Fori(1, NE // 2 - 1) as i:
                moe_body(i, False)
            moe_body(NE // 2 - 1, True)


_ORDER = ["x", "wqk", "bqk", "wv", "bv", "wo", "bo", "wg", "cfc", "cproj", "c", "wmod", "trig", "consts"]


def kernel(L0_attn_x, L0_attn_Wq, L0_attn_bq, L0_attn_Wk, L0_attn_bk, L0_attn_Wv, L0_attn_bv, L0_attn_Wo,
           L0_attn_bo, L0_ffn_w_g, L0_ffn_c_fc, L0_ffn_c_proj, L0_c, L0_wmod):
    import concourse.bacc as bacc
    from concourse.bass_utils import run_bass_kernel_spmd

    order = np.arange(D).reshape(H, 2, DH // 2).transpose(1, 0, 2).reshape(2, P)
    wq, wk = np.asarray(L0_attn_Wq)[:, order], np.asarray(L0_attn_Wk)[:, order]
    bq, bk = np.asarray(L0_attn_bq)[order], np.asarray(L0_attn_bk)[order]
    f = np.arange(DH // 2, dtype=np.float32)
    inv = (np.float32(1.0) / np.float32(10000.0) ** (f / np.float32(DH // 2))).astype(np.float32)
    ang = np.tile((np.arange(T, dtype=np.float32)[:, None] * inv[None]).T, (H, 1))
    consts = np.zeros((P, 330), np.float32)
    consts[:, 0:128] = np.eye(P)
    consts[:, 128:256] = np.triu(np.ones((P, P)), 1)
    consts[:, 256:264] = np.arange(NE) - 8
    consts[:, 264:328] = (PAIRS_AT + np.arange(2)[None, :, None] * N + np.arange(TT)[None, None] * P
                          + np.arange(P)[:, None, None]).reshape(P, 2 * TT)
    consts[:, 328:330] = EMPTY_AT + np.arange(2)[None] * P + np.arange(P)[:, None]
    arrays = {
        "x": np.asarray(L0_attn_x), "wqk": np.stack([wq[:, 0], wq[:, 1], wk[:, 0], wk[:, 1]], 1),
        "bqk": np.stack([bq[0], bq[1], bk[0], bk[1]], 1), "wv": np.asarray(L0_attn_Wv),
        "bv": np.asarray(L0_attn_bv).reshape(KC, P).T, "wo": np.asarray(L0_attn_Wo), "bo": np.asarray(L0_attn_bo),
        "wg": np.asarray(L0_ffn_w_g), "cfc": np.asarray(L0_ffn_c_fc), "cproj": np.asarray(L0_ffn_c_proj),
        "c": np.asarray(L0_c).T.reshape(KC, P, B).transpose(1, 0, 2), "wmod": np.asarray(L0_wmod),
        "trig": np.stack([np.cos(ang), np.sin(ang)], 1).astype(np.float32), "consts": consts,
    }
    arrays = {k: np.ascontiguousarray(v) for k, v in arrays.items()}
    nc = bacc.Bacc("TRN2", target_bir_lowering=False, num_devices=1)
    args = [nc.dram_tensor(k, arrays[k].shape, mybir.dt.from_np(arrays[k].dtype), kind="ExternalInput").ap()
            for k in _ORDER]
    out = nc.dram_tensor("out", (B, T, D), mybir.dt.float32, kind="ExternalOutput").ap()
    adaln_block(nc, *args, out)
    r = run_bass_kernel_spmd(nc, [arrays], core_ids=[0])
    return r.results[0]["out"]
```
